# Optimizing a Trainium2 kernel written in Bass

```python
import numpy as np
import jax
import jax.numpy as jnp

def _softmax(x, axis=-1):
    return jax.nn.softmax(x, axis=axis)

def _gelu(x):
    return jax.nn.gelu(x, approximate=True)

def _silu(x):
    return jax.nn.silu(x)

def _sigmoid(x):
    return jax.nn.sigmoid(x)

def _layernorm(x, axis=-1, eps=1e-05):
    m = jnp.mean(x, axis=axis, keepdims=True)
    v = jnp.var(x, axis=axis, keepdims=True)
    return (x - m) / jnp.sqrt(v + eps)

def _scatter_add(tgt, idx, src, axis=0):
    return tgt.at[idx].add(src)

def _segment_sum(src, seg, n):
    return jax.ops.segment_sum(src, seg, n)
kernel_name = 'mk_adj_ffn_d1_adj_r2_6f88b2'

def setup_inputs(seed: int=0):
    np.random.seed(seed)
    _w = jnp.asarray

    def _rec_inputs():
        import jax
        import jax.numpy as jnp
        _gk = jax.random.key(seed)
        x = -0.0003929 + 0.9999 * jax.random.normal(jax.random.fold_in(_gk, 1), (8, 1024, 128), jnp.float32)
        _a = jax.random.bernoulli(jax.random.fold_in(_gk, 2), 0.015625, (1024, 1024))
        _a = jnp.logical_or(_a, jnp.swapaxes(_a, -1, -2))
        _a = jnp.logical_or(_a, jnp.eye(1024, dtype=bool))
        _af = _a.astype(jnp.float32)
        _af = _af * jax.random.uniform(jax.random.fold_in(_gk, 3), (1024, 1024), jnp.float32, 0.05, 1)
        adj = _af
        return (x, adj)
    x, adj = _rec_inputs()

    def _L0_gnn_setup():
        import jax, jax.numpy as jnp
        import numpy as np
        EPS = 1e-05

        def _batchnorm(x, gamma, beta):
            mu = jnp.mean(x, axis=0)
            var = jnp.var(x, axis=0)
            return (x - mu) * jax.lax.rsqrt(var + EPS) * gamma + beta
        key = jax.random.key(seed)
        ks = jax.random.split(key, 4)
        b, n, d, h, o = (32, 1024, 128, 256, 128)
        features = jax.random.normal(ks[0], (b, n, d), dtype=jnp.float32)
        A = jax.random.uniform(ks[1], (n, n), dtype=jnp.float32)
        lim1 = float(np.sqrt(6.0 / (d + h)))
        W1 = jax.random.uniform(ks[2], (h, d), minval=-lim1, maxval=lim1, dtype=jnp.float32)
        b1 = jnp.zeros((h,), jnp.float32)
        lim2 = float(np.sqrt(6.0 / (h + o)))
        W2 = jax.random.uniform(ks[3], (o, h), minval=-lim2, maxval=lim2, dtype=jnp.float32)
        b2 = jnp.zeros((o,), jnp.float32)
        g1 = jnp.ones((h,), jnp.float32)
        be1 = jnp.zeros((h,), jnp.float32)
        g2 = jnp.ones((o,), jnp.float32)
        be2 = jnp.zeros((o,), jnp.float32)
        return {'features': features, 'A': A, 'W1': W1, 'b1': b1, 'g1': g1, 'be1': be1, 'W2': W2, 'b2': b2, 'g2': g2, 'be2': be2}
    _L0_gnn_all = _L0_gnn_setup()
    _L0_gnn_in = {k: v for k, v in _L0_gnn_all.items() if k in ('W1', 'b1', 'g1', 'be1', 'W2', 'b2', 'g2', 'be2')}
    del _L0_gnn_all

    def _L0_ffn_setup():
        import jax, jax.numpy as jnp
        import numpy as np
        B, S, D, F, E, K = (8, 1024, 128, 512, 8, 2)
        key = jax.random.key(seed)
        ks = jax.random.split(key, 10)
        s = 0.02
        return {'x': jax.random.normal(ks[0], (B, S, D), dtype=jnp.float32), 'Wr': jax.random.normal(ks[1], (D, E), dtype=jnp.float32) * s, 'W1s': jax.random.normal(ks[2], (D, F), dtype=jnp.float32) * s, 'b1s': jnp.zeros((F,), dtype=jnp.float32), 'W2s': jax.random.normal(ks[3], (F, D), dtype=jnp.float32) * s, 'b2s': jnp.zeros((D,), dtype=jnp.float32), 'W1p': jax.random.normal(ks[4], (E, D, F), dtype=jnp.float32) * s, 'b1p': jnp.zeros((E, F), dtype=jnp.float32), 'W2p': jax.random.normal(ks[5], (E, F, D), dtype=jnp.float32) * s, 'b2p': jnp.zeros((E, D), dtype=jnp.float32)}
    _L0_ffn_all = _L0_ffn_setup()
    _L0_ffn_in = {k: v for k, v in _L0_ffn_all.items() if k in ('Wr', 'W1s', 'b1s', 'W2s', 'b2s', 'W1p', 'b1p', 'W2p', 'b2p')}
    del _L0_ffn_all
    return {'x': x, 'adj': adj, 'L0_gnn_W1': _L0_gnn_in['W1'], 'L0_gnn_b1': _L0_gnn_in['b1'], 'L0_gnn_g1': _L0_gnn_in['g1'], 'L0_gnn_be1': _L0_gnn_in['be1'], 'L0_gnn_W2': _L0_gnn_in['W2'], 'L0_gnn_b2': _L0_gnn_in['b2'], 'L0_gnn_g2': _L0_gnn_in['g2'], 'L0_gnn_be2': _L0_gnn_in['be2'], 'L0_ffn_Wr': _L0_ffn_in['Wr'], 'L0_ffn_W1s': _L0_ffn_in['W1s'], 'L0_ffn_b1s': _L0_ffn_in['b1s'], 'L0_ffn_W2s': _L0_ffn_in['W2s'], 'L0_ffn_b2s': _L0_ffn_in['b2s'], 'L0_ffn_W1p': _L0_ffn_in['W1p'], 'L0_ffn_b1p': _L0_ffn_in['b1p'], 'L0_ffn_W2p': _L0_ffn_in['W2p'], 'L0_ffn_b2p': _L0_ffn_in['b2p']}

def reference(x, adj, L0_gnn_W1, L0_gnn_b1, L0_gnn_g1, L0_gnn_be1, L0_gnn_W2, L0_gnn_b2, L0_gnn_g2, L0_gnn_be2, L0_ffn_Wr, L0_ffn_W1s, L0_ffn_b1s, L0_ffn_W2s, L0_ffn_b2s, L0_ffn_W1p, L0_ffn_b1p, L0_ffn_W2p, L0_ffn_b2p):
    import jax
    import jax.numpy as jnp

    def _L0_gnn_ref(features, A, W1, b1, g1, be1, W2, b2, g2, be2):
        import jax, jax.numpy as jnp
        import numpy as np
        EPS = 1e-05

        def _batchnorm(x, gamma, beta):
            mu = jnp.mean(x, axis=0)
            var = jnp.var(x, axis=0)
            return (x - mu) * jax.lax.rsqrt(var + EPS) * gamma + beta
        b, n, d = features.shape
        A_norm = A + jnp.eye(n, dtype=A.dtype)
        deg = jnp.sum(A_norm, axis=0) + jnp.sum(A_norm, axis=1) - jnp.diagonal(A_norm)
        dinv = jax.lax.rsqrt(deg)
        A_hat = A_norm * dinv[:, None] * dinv[None, :]
        agg = jnp.einsum('nm,bmd->bnd', A_hat, features)
        x = agg.reshape(-1, d)
        h = jax.nn.relu(_batchnorm(x @ W1.T + b1, g1, be1))
        out = h @ W2.T + b2
        out = _batchnorm(out, g2, be2)
        return out.reshape(b, n, -1)

    def _L0_ffn_ref(x, Wr, W1s, b1s, W2s, b2s, W1p, b1p, W2p, b2p):
        import jax, jax.numpy as jnp
        import numpy as np
        B, S, D, F, E, K = (8, 1024, 128, 512, 8, 2)
        gelu = lambda t: jax.nn.gelu(t, approximate=False)
        shared = gelu(x @ W1s + b1s) @ W2s + b2s
        rw = jax.nn.softmax(x @ Wr, axis=-1)
        topw, topi = jax.lax.top_k(rw, K)
        topw = topw / jnp.sum(topw, axis=-1, keepdims=True)
        mask = jnp.sum(jax.nn.one_hot(topi, E, dtype=topw.dtype) * topw[..., None], axis=-2)
        h = gelu(jnp.einsum('bsd,edf->bsef', x, W1p) + b1p)
        priv = jnp.einsum('bsef,efd->bsed', h, W2p) + b2p
        routed = jnp.einsum('bsed,bse->bsd', priv, mask)
        return shared + routed
    x = x + _L0_gnn_ref(_layernorm(x, axis=-1), adj, L0_gnn_W1, L0_gnn_b1, L0_gnn_g1, L0_gnn_be1, L0_gnn_W2, L0_gnn_b2, L0_gnn_g2, L0_gnn_be2)
    x = x + _L0_ffn_ref(_layernorm(x, axis=-1), L0_ffn_Wr, L0_ffn_W1s, L0_ffn_b1s, L0_ffn_W2s, L0_ffn_b2s, L0_ffn_W1p, L0_ffn_b1p, L0_ffn_W2p, L0_ffn_b2p)
    return x

_drawn_inputs = setup_inputs


def setup_inputs(seed=0):
    import zlib

    import numpy as np

    out = dict(_drawn_inputs(seed))
    spreads = {'L0_gnn_b1': (0.0, 0.8),
     'L0_gnn_g1': (1.0, 0.2),
     'L0_gnn_be1': (0.0, 0.1),
     'L0_gnn_b2': (0.0, 0.8),
     'L0_gnn_g2': (1.0, 0.2),
     'L0_gnn_be2': (0.0, 0.1),
     'L0_ffn_b1s': (0.0, 0.488),
     'L0_ffn_b2s': (0.0, 0.1),
     'L0_ffn_b1p': (0.0, 0.663),
     'L0_ffn_b2p': (0.0, 0.1)}
    factors = {}
    for name, (base, spread) in spreads.items():
        noise = np.random.default_rng([zlib.crc32(name.encode()), seed]).standard_normal(out[name].shape)
        drawn = base * np.exp(spread * noise) if base else spread * noise
        out[name] = jnp.asarray(drawn.astype(out[name].dtype))
    for name, factor in factors.items():
        out[name] = (out[name] * factor).astype(out[name].dtype)
    return out
```

```python
import concourse.bass as bass
from concourse import mybir
from contextlib import ExitStack

P = 128
D = 128
NODES = 1024
BATCH = 8
TOK = BATCH * NODES
CH = NODES // P
BLK = TOK // P
H = 256
HG = H // P
F = 512
FC = F // P
E = 8
T = 512
NT = TOK // T
BT = T // P
HALVES = 2
HB = BLK // HALVES
HT = NT // HALVES
TR = 256
RB = TR // P
TILES = (2 * TOK // HALVES + E * (TR - 1)) // TR
NR = HALVES * TILES
ROW = D + 2
SKIP = 1 << 20
WSCALE = 256.0
EPS = 1e-5
BIG = 3.0e38

VEC = dict(b1=(0, HG), g1=(2, HG), be1=(4, HG), b2=(6, 1), g2=(7, 1), be2=(8, 1), b1s=(9, FC), b1p=(13, E * FC))
NVEC = 13 + E * FC


def build(nc, x, adj, W1, b1, g1, be1, W2, b2, g2, be2, Wr, W1s, b1s, W2s, b2s, W1p, b1p, W2p, b2p, out):
    f32, f16, i32 = mybir.dt.float32, mybir.dt.float16, mybir.dt.int32
    ALU = mybir.AluOpType
    ACT = mybir.ActivationFunctionType
    AX = mybir.AxisListType
    ds = bass.ds

    def wait_alone(engine, semaphore, value, tick):
        engine.wait_ge(semaphore, value)
        engine.sem_inc(tick, 1)

    ctx = ExitStack()
    with ctx:
        def sb(name, cols, dt=f32, parts=P):
            return ctx.enter_context(nc.sbuf_tensor(name, [parts, cols], dt))

        def sem(name):
            return ctx.enter_context(nc.semaphore(name))

        xres = sb("xres", BLK * D)
        region1 = sb("region1", 16384)
        region2 = sb("region2", 16384)
        misc = sb("misc", HB * ROW)
        wprep = sb("wprep", 4096)

        r1h = region1[:, :].bitcast(f16)
        at_hi, at_lo = r1h[:, 0:8192], r1h[:, 8192:16384]
        xn_hi, xn_lo = r1h[:, 16384:24576], r1h[:, 24576:32768]
        wall = r1h[:, 0:(E + 1) * 2048]
        pay0 = region1[:, 9216:9216 + HB * ROW]
        ybuf = [region1[:, 13440 + 512 * u:13952 + 512 * u] for u in range(2)]
        xt32 = [region1[:, 14464 + 512 * u:14976 + 512 * u] for u in range(2)]

        b2p_rep = region1[:, 13440:13440 + E * D]

        adjn = region2[:, 0:8192]
        hpre = region2
        out2 = region2[:, 0:8192]
        r2h = region2[:, 8192:16384].bitcast(f16)
        xt_hi, xt_lo = r2h[:, 0:8192], r2h[:, 8192:16384]
        h32 = region2[:, 0:FC * T]
        fh = region2[:, 2048:6144].bitcast(f16)
        h_hi = [fh[:, 4096 * u:4096 * u + 2048] for u in range(2)]
        h_lo = [fh[:, 4096 * u + 2048:4096 * u + 4096] for u in range(2)]
        xr = [region2[:, 6144 + 320 * u:6144 + 320 * u + RB * ROW] for u in range(2)]
        yr = [region2[:, 6784 + 256 * u:7040 + 256 * u] for u in range(2)]
        xrh = region2[:, 7296:7808].bitcast(f16)
        xr_hi = [xrh[:, 512 * u:512 * u + 256] for u in range(2)]
        xr_lo = [xrh[:, 512 * u + 256:512 * u + 512] for u in range(2)]
        rflag = [region2[:, 7808 + 8 * u:7808 + 8 * u + RB] for u in range(2)]
        rdest = [region2[:, 7824 + 8 * u:7824 + 8 * u + RB].bitcast(i32) for u in range(2)]

        xnf = misc[:, 0:1024]
        aggf = [misc[:, 1024 + 512 * u:1536 + 512 * u] for u in range(2)]
        mh = misc[:, 2048:3072].bitcast(f16)
        agg_hi = [mh[:, 1024 * u:1024 * u + 512] for u in range(2)]
        agg_lo = [mh[:, 1024 * u + 512:1024 * u + 1024] for u in range(2)]
        dinvrow = misc[:, 3072:4096]
        diagd = misc[:, 1024:2048]
        junk = misc[:, 0:1024]
        junkd = misc[:, 2048:2176]
        hr = [misc[:, 1024 * u:1024 * u + 1024] for u in range(2)]
        mc = misc[:, 2048:4096].bitcast(f16)
        hr_hi = [mc[:, 2048 * u:2048 * u + 1024] for u in range(2)]
        hr_lo = [mc[:, 2048 * u + 1024:2048 * u + 2048] for u in range(2)]
        pay1 = misc[:, 0:HB * ROW]
        pay = [pay0, pay1]
        GB = 8
        yload = [[misc[:, (2 * u + k) * 1024:(2 * u + k + 1) * 1024] for k in range(2)] for u in range(2)]

        wraw = [wprep[:, 1024 * u:1024 * u + 1024] for u in range(2)]
        wph = wprep[:, 2048:4096].bitcast(f16)
        wcut = [wph[:, 2048 * u:2048 * u + 2048] for u in range(2)]
        rt = [wprep[:, 256 * n:256 * n + 256] for n in range(16)]

        ident = sb("ident_sb", P)
        onesf = sb("onesf", P)
        ones16 = sb("ones16", P, f16)
        before16 = sb("before16", P, f16)
        gw1 = sb("gw1", HG * D)
        gw2 = sb("gw2", H)
        w1t_hi, w1t_lo = sb("w1t_hi", H, f16), sb("w1t_lo", H, f16)
        w2t_hi, w2t_lo = sb("w2t_hi", H, f16), sb("w2t_lo", H, f16)
        vrows = sb("vrows", P)
        vec = sb("vec", NVEC)
        wr_sb = sb("wr_sb", E)
        b2s_rep = sb("b2s_rep", D)
        st = sb("st", BLK * 6)
        st_bn = sb("st_bn", HG * NT * 6)
        msum, rstd = sb("msum", BLK), sb("rstd", BLK)
        mean = sb("mean", BLK)
        ids = sb("ids", BLK, i32)
        dest_all = sb("dest_all", NR * RB, i32)
        sdiff, sm2 = sb("sdiff", BLK), sb("sm2", BLK)
        mhalf = sb("mhalf", BLK)
        rsum, diag, dinv = sb("rsum", CH), sb("diag", CH), sb("dinv", CH)
        bnm = sb("bnm", 2 * HG)
        bna, bnc = sb("bna", 4), sb("bnc", 4)
        bnv = sb("bnv", 4)
        desc8, asc8 = sb("desc8", E), sb("asc8", E)
        tile_at = sb("tile_at", TILES)
        ones_hb = sb("ones_hb", HB)
        trash = sb("trash", RB * ROW)
        idx = [sb(f"idx{k}", BLK, i32) for k in range(2)]
        wgt = [sb(f"wgt{k}", BLK) for k in range(2)]
        tile_f = sb("tile_f", NR)
        tile_e = sb("tile_e", NR, i32)
        small = [sb(f"small{n}", E) for n in range(4)]
        small_i = sb("small_i", E, i32)

        bank = [ctx.enter_context(nc.psum_tensor(f"bank{n}", [P, 512], f32)) for n in range(8)]

        wsc = nc.dram_tensor("weights_cut", (E + 1, P, 2048), f16, kind="Internal").ap()
        xs = nc.dram_tensor("rows_by_expert", (NR * TR, ROW), f32, kind="Internal").ap()
        ys = nc.dram_tensor("rows_by_token", (2 * TOK, D), f32, kind="Internal").ap()

        small_loaded = sem("small_loaded")
        late_loaded, b2p_loaded = sem("late_loaded"), sem("b2p_loaded")
        adj_loaded = [sem(f"adj_loaded{c}") for c in range(CH)]
        x_loaded = [sem(f"x_loaded{b}") for b in range(BATCH)]
        pool_made = sem("pool_made")
        pool_pow = sem("pool_pow")
        act_tick, pool_tick = sem("act_tick"), sem("pool_tick")
        pow_in = sem("pow_in")
        dve = sem("dve")
        act_s = sem("act_s")
        w_raw = [sem(f"w_raw{u}") for u in range(2)]
        w_cut = sem("w_cut")
        w_chain = sem("w_chain")
        w_kept = [sem(f"w_kept{u}") for u in range(2)]
        wall_loaded = sem("wall_loaded")
        trash_stored = sem("trash_stored")
        prep_t = sem("prep_t")
        prep_hi = sem("prep_hi")
        prep_ready = sem("prep_ready")
        adj_eye = sem("adj_eye")
        at_t, at_hi_done, at_lo_done = sem("at_t"), sem("at_hi_done"), sem("at_lo_done")
        colsum_done = sem("colsum_done")
        rowsum_done = sem("rowsum_done")
        diagd_done = sem("diagd_done")
        dinv_in_psum = sem("dinv_in_psum")
        xn_f, xn_h, xn_l = sem("xn_f"), sem("xn_h"), sem("xn_l")
        agg_done, agg_f, agg_h, agg_l = sem("agg_done"), sem("agg_f"), sem("agg_h"), sem("agg_l")
        up1_done, up1_out = sem("up1_done"), sem("up1_out")
        bn_ready = sem("bn_ready")
        c_relu, c_hi, c_lo, c_mm, c_out, c_stat = (sem(n) for n in ("c_relu", "c_hi", "c_lo", "c_mm", "c_out", "c_stat"))
        y_done, y_t, x2_done = sem("y_done"), sem("y_t"), sem("x2_done")
        row_done, row_t, xt_f, xt_l, lg_done, lg_out = (
            sem(n) for n in ("row_done", "row_t", "xt_f", "xt_l", "lg_done", "lg_out"))
        exp_in, exp_done = sem("exp_in"), sem("exp_done")
        oh_ready, rank_done, route_ready = sem("oh_ready"), sem("rank_done"), sem("route_ready")
        dispatched = [sem(f"dispatched{s}") for s in range(HALVES)]
        stats_done, bias_in = sem("stats_done"), sem("bias_in")
        ids_read, hi_r, dest_made = sem("ids_read"), sem("hi_r"), sem("dest_made")
        up_done, gelu_done, lo_done, down_done, ffn_out = (
            sem(n) for n in ("up_done", "gelu_done", "lo_done", "down_done", "ffn_out"))
        xr_loaded = [sem(f"xr_loaded{u}") for u in range(2)]
        xr_t, xr_h, xr_l = sem("xr_t"), sem("xr_h"), sem("xr_l")
        returned = [sem(f"returned{u}") for u in range(2)]
        y_loaded = [sem(f"y_loaded{u}") for u in range(2)]
        y_used = sem("y_used")
        combined = sem("combined")
        stored = sem("stored")

        RING = 2

        block = ctx.enter_context(nc.Block())
        W1S, W1L, W2S, W2L = 0, 512, 1024, 1536
        NSH = NT * FC

        @block.sync
        def _(sp):
            def rows(v, n, at):
                sp.dma_start(vrows[at:at + n, :], v).then_inc(small_loaded, 16)
            rows(b1.rearrange("(g p) -> g p", p=P), HG, VEC["b1"][0])
            rows(g1.rearrange("(g p) -> g p", p=P), HG, VEC["g1"][0])
            rows(be1.rearrange("(g p) -> g p", p=P), HG, VEC["be1"][0])
            rows(b2.rearrange("(g p) -> g p", p=P), 1, VEC["b2"][0])
            rows(g2.rearrange("(g p) -> g p", p=P), 1, VEC["g2"][0])
            rows(be2.rearrange("(g p) -> g p", p=P), 1, VEC["be2"][0])
            rows(b1s.rearrange("(g p) -> g p", p=P), FC, VEC["b1s"][0])
            rows(b1p.rearrange("e (g p) -> (e g) p", p=P), E * FC, VEC["b1p"][0])
            sp.dma_start(gw1[:, :].rearrange("p (g d) -> p g d", g=HG),
                         W1.rearrange("(g p) d -> p g d", p=P)).then_inc(small_loaded, 16)
            sp.dma_start(gw2[:, :], W2).then_inc(small_loaded, 16)
            for c in range(CH):
                sp.dma_start(adjn[:, c * NODES:(c + 1) * NODES], adj[c * P:(c + 1) * P, :]).then_inc(adj_loaded[c], 16)
            for b in range(BATCH):
                sp.dma_start(xres[:, b * NODES:(b + 1) * NODES].rearrange("p (c d) -> p c d", c=CH),
                             x[b].rearrange("(c p) d -> p c d", p=P)).then_inc(x_loaded[b], 16)
            sp.dma_start(wr_sb[:, :], Wr).then_inc(late_loaded, 16)
            sp.dma_start(b2s_rep[:, :], b2s.rearrange("(o d) -> o d", o=1).broadcast_to((P, D))).then_inc(late_loaded, 16)

            def raw(u, w1, w2):
                sp.dma_start(wraw[u][:, 0:F], w1).then_inc(w_raw[u], 16)
                sp.dma_start(wraw[u][:, F:2 * F].rearrange("p (c d) -> p c d", c=FC), w2).then_inc(w_raw[u], 16)

            def keep(u, e):
                sp.dma_start(wsc[ds(e, 1), :, :].rearrange("o p n -> (o p) n"), wcut[u]).then_inc(w_kept[u], 16)

            raw(0, W1s, W2s.rearrange("(c p) d -> p c d", p=P))
            sp.wait_ge(w_cut, 1)
            keep(0, E)
            with sp.Fori(0, E // 2) as i:
                for u in range(2):
                    raw(u, W1p[ds(2 * i + u, 1), :, :].rearrange("o p f -> (o p) f"),
                        W2p[ds(2 * i + u, 1), :, :].rearrange("o (c p) d -> p (o c) d", p=P))
                for u in range(2):
                    sp.wait_ge(w_cut, 2 * i + u + 2)
                    keep(u, 2 * i + u)

            sp.wait_ge(pool_made, 9)
            with sp.Fori(0, NR) as k:
                sp.dma_start(xs[ds(k * TR, TR), :].rearrange("(j p) n -> p j n", p=P),
                             trash[:, :].rearrange("p (j n) -> p j n", j=RB)).then_inc(trash_stored, 16)

            sp.wait_ge(agg_done, NT)
            sp.wait_ge(w_kept[0], 16 * (1 + E // 2))
            sp.wait_ge(w_kept[1], 16 * (E // 2))
            sp.dma_start(wall.rearrange("p (e n) -> p e n", e=E + 1), wsc.rearrange("e p n -> p e n")).then_inc(wall_loaded, 16)

            def load_rows(u, g, use):
                sp.wait_ge(xr_t, use)
                sp.wait_ge(ids_read, use)
                sp.dma_start(xr[u].rearrange("p (j n) -> p j n", j=RB),
                             xs[ds(g * TR, TR), :].rearrange("(j p) n -> p j n", p=P)).then_inc(xr_loaded[u], 16)
            sp.wait_ge(x2_done, NT + RING)
            sp.dma_start(b2p_rep, b2p.rearrange("(o e) d -> o (e d)", o=1).broadcast_to((P, E * D))).then_inc(b2p_loaded, 16)
            sp.wait_ge(dispatched[0], 16 * 2 * HB)
            for g in range(2):
                sp.dma_start(xr[g].rearrange("p (j n) -> p j n", j=RB),
                             xs[g * TR:(g + 1) * TR, :].rearrange("(j p) n -> p j n", p=P)).then_inc(xr_loaded[g], 16)
            with sp.Fori(1, TILES // 2) as i:
                for u in range(2):
                    load_rows(u, 2 * i + u, 2 * i + u - 1)
            load_rows(0, TILES - 1, TILES - 2)
            sp.wait_ge(dispatched[1], 16 * 2 * HB)
            load_rows(1, TILES, TILES - 1)
            with sp.Fori((TILES + 1) // 2, NR // 2) as i:
                for u in range(2):
                    load_rows(u, 2 * i + u, 2 * i + u - 1)

            sp.wait_ge(returned[0], 16 * RB * NR // 2)
            sp.wait_ge(returned[1], 16 * RB * NR // 2)
            sp.wait_ge(route_ready, HALVES)

            def load_y(u, n):
                for k in range(2):
                    sp.dma_start(yload[u][k].rearrange("p (b d) -> p b d", b=GB),
                                 ys[ds(k * TOK + n * GB * P, GB * P), :].rearrange("(b p) d -> p b d", p=P)).then_inc(y_loaded[u], 16)

            def store(n):
                sp.dma_start(out[ds(n * GB * P, GB * P), :].rearrange("(b p) d -> p b d", p=P),
                             xres[:, ds(n * GB * D, GB * D)].rearrange("p (b d) -> p b d", b=GB)).then_inc(stored, 16)
            load_y(0, 0)
            load_y(1, 1)
            with sp.Fori(0, BLK // GB // 2 - 1) as i:
                for u in range(2):
                    sp.wait_ge(combined, 2 * i + u + 1)
                    load_y(u, 2 * i + u + 2)
                    store(2 * i + u)
            for n in range(BLK // GB - 2, BLK // GB):
                sp.wait_ge(combined, n + 1)
                store(n)
            sp.wait_ge(stored, 16 * (BLK // GB))
            sp.wait_ge(trash_stored, 16 * NR)

        @block.gpsimd
        def _(pool):
            pool.memset(ident[:, :], 0.0).then_inc(pool_made, 1)
            pool.memset(before16[:, :], 1.0).then_inc(pool_made, 1)
            pool.wait_ge(pool_made, 2)
            pool.affine_select(out=ident[:, :], in_=ident[:, :], compare_op=ALU.not_equal, fill=1.0,
                               base=0, pattern=[[-1, P]], channel_multiplier=1).then_inc(pool_made, 1)
            pool.affine_select(out=before16[:, :], in_=before16[:, :], compare_op=ALU.is_gt, fill=0.0,
                               base=0, pattern=[[1, P]], channel_multiplier=-1).then_inc(pool_made, 1)
            pool.memset(onesf[:, :], 1.0)
            pool.memset(ones16[:, :], 1.0)
            pool.memset(ones_hb[:, :], 1.0)
            pool.memset(mhalf[:, :], -0.5).then_inc(pool_made, 1)
            pool.iota(desc8[:, :], [[-1, E]], base=E, channel_multiplier=0, allow_small_or_imprecise_dtypes=True)
            pool.iota(asc8[:, :], [[1, E]], base=0, channel_multiplier=0, allow_small_or_imprecise_dtypes=True)
            pool.iota(tile_at[:, :], [[TR, TILES]], base=0, channel_multiplier=0,
                      allow_small_or_imprecise_dtypes=True).then_inc(pool_made, 1)
            pool.memset(trash[:, :], 0.0).then_inc(pool_made, 1)
            pool.wait_ge(pool_made, 7)
            tv = trash[:, :].rearrange("p (j n) -> p j n", j=RB)
            pool.iota(tv[:, :, D:D + 1].bitcast(i32), [[P, RB], [0, 1]], base=SKIP, channel_multiplier=1).then_inc(pool_made, 1)
            pool.memset(tv[:, :, D + 1:D + 2], -1.0).then_inc(pool_made, 1)

            def inverse_root(o, v, n, turn):
                pool.wait_ge(pow_in, turn)
                pool.tensor_tensor(o, v, mhalf[:, 0:n], ALU.pow).then_inc(pool_pow, 1)

            inverse_root(dinv[:, :], diag[:, :], CH, 1)
            for b in range(BATCH):
                inverse_root(rstd[:, b * CH:(b + 1) * CH], sm2[:, b * CH:(b + 1) * CH], CH, b + 2)

            pool.iota(ids[:, :], [[P, BLK]], base=0, channel_multiplier=1).then_inc(pool_made, 1)
            def cut(u, turn, kept):
                v = wraw[u].rearrange("p (w f) -> p w f", w=2)
                parts = wcut[u].rearrange("p (w s f) -> p w s f", w=2, s=2)
                wait_alone(pool, w_raw[u], 32 * turn, pool_tick)
                pool.tensor_scalar(v, v, WSCALE, None, ALU.mult).then_inc(w_chain, 1)
                if kept is not None:
                    pool.wait_ge(w_kept[u], kept)
                return v, parts

            def cut2(u, v, parts, c):
                wait_alone(pool, w_chain, c + 1, pool_tick)
                pool.tensor_copy(parts[:, :, 0, :], v).then_inc(w_chain, 1)
                pool.wait_ge(w_chain, c + 2)
                pool.tensor_tensor(parts[:, :, 1, :], v, parts[:, :, 0, :], ALU.subtract).then_inc(w_cut, 1)

            v, parts = cut(0, 1, None)
            cut2(0, v, parts, 0)
            v, parts = cut(0, 2, 16)
            cut2(0, v, parts, 2)
            v, parts = cut(1, 1, None)
            cut2(1, v, parts, 4)
            with pool.Fori(1, E // 2) as i:
                for u in range(2):
                    v, parts = cut(u, i + (2 if u == 0 else 1), 16 * i + (16 if u == 0 else 0))
                    cut2(u, v, parts, 4 * i + 2 * u + 2)

            inverse_root(bna[:, 0:HG], bnv[:, 0:HG], HG, BATCH + 2)
            with pool.Fori(0, NT // 2) as i:
                for u in range(2):
                    pool.wait_ge(c_relu, 2 * (2 * i + u) + 2)
                    wait_alone(pool, c_mm, 2 * i + u + 1, pool_tick)
                    pool.tensor_copy(hr_hi[u], hr[u]).then_inc(c_hi, 1)
            inverse_root(bna[:, HG:HG + 1], bnv[:, HG:HG + 1], 1, BATCH + 3)
            Q = BLK // 4
            for q in range(4):
                inverse_root(rstd[:, q * Q:(q + 1) * Q], sm2[:, q * Q:(q + 1) * Q], Q, BATCH + 4 + q)

            pool.wait_ge(trash_stored, 16 * NR)
            for s in range(HALVES):
                pool.wait_ge(route_ready, s + 1)
                for n in range(HB):
                    for k in range(2):
                        blk = s * HB + n
                        pool.indirect_dma_start(xs, bass.IndirectOffsetOnAxis(idx[k][:, blk:blk + 1], 0),
                                                pay[s][:, n * ROW:(n + 1) * ROW], None).then_inc(dispatched[s], 16)

            with pool.Fori(0, NR // 2) as i:
                for u in range(2):
                    wait_alone(pool, ffn_out, 2 * i + u + 1 + NT + RING, pool_tick)
                    for j in range(RB):
                        pool.indirect_dma_start(ys, bass.IndirectOffsetOnAxis(rdest[u][:, j:j + 1], 0),
                                                yr[u][:, j * D:(j + 1) * D], None,
                                                bounds_check=2 * TOK - 1, oob_is_err=False).then_inc(returned[u], 16)

        @block.scalar
        def _(act):
            act.sem_inc(c_out, RING)
            act.sem_inc(gelu_done, FC)
            act.wait_ge(prep_t, 1)
            nc.scalar.activation(vec[:, :], bank[7][:, 0:NVEC], ACT.Copy).then_inc(prep_hi, 1)
            nc.scalar.activation(w1t_hi[:, :], bank[6][:, 0:H], ACT.Copy, scale=WSCALE).then_inc(prep_hi, 1)
            nc.scalar.activation(w2t_hi[:, :], bank[6][:, H:2 * H], ACT.Copy, scale=WSCALE).then_inc(prep_hi, 1)

            atv = at_hi.rearrange("p (m n) -> p m n", m=CH)
            for c in range(CH):
                act.wait_ge(adj_eye, c + 1)
                if c:
                    act.wait_ge(rowsum_done, c)
                nc.scalar.activation(junk, adjn[:, c * NODES:(c + 1) * NODES], ACT.Copy,
                                     accum_out=rsum[:, c:c + 1]).then_inc(rowsum_done, 1)
                for h in range(2):
                    act.wait_ge(at_t, 2 * c + h + 1)
                    nc.scalar.activation(atv[:, 4 * h:4 * h + 4, c * P:(c + 1) * P],
                                         bank[2 * (c % 2) + h][:, :].rearrange("p (m n) -> p m n", m=4),
                                         ACT.Copy).then_inc(at_hi_done, 1)
            act.wait_ge(dinv_in_psum, 1)
            for h in range(2):
                nc.scalar.activation(dinvrow[:, h * T:(h + 1) * T], bank[5 + h][:, :], ACT.Copy).then_inc(act_s, 1)

            def xn_high(b):
                wait_alone(act, xn_f, b + 1, act_tick)
                nc.scalar.activation(xn_hi[:, ds(b * NODES, NODES)], xnf, ACT.Copy).then_inc(xn_h, 1)

            def agg_high(u, t):
                act.wait_ge(agg_f, t + 1)
                nc.scalar.activation(agg_hi[u], aggf[u], ACT.Copy).then_inc(agg_h, 1)

            def hidden_out(u, t):
                for g in range(HG):
                    wait_alone(act, up1_done, 2 * t + g + 1, act_tick)
                    nc.scalar.activation(hpre[:, ds(g * TOK + t * T, T)], bank[2 + 2 * u + g][:, :], ACT.Identity,
                                         bias=vec[:, g:g + 1], scale=1.0 / WSCALE).then_inc(up1_out, 1)

            xn_high(0)
            agg_high(0, 0)
            with act.Fori(0, BATCH - 1) as b:
                xn_high(b + 1)
                agg_high(1, 2 * b + 1)
                hidden_out(0, 2 * b)
                agg_high(0, 2 * b + 2)
                hidden_out(1, 2 * b + 1)
            agg_high(1, NT - 1)
            hidden_out(0, NT - 2)
            hidden_out(1, NT - 1)

            act.wait_ge(bn_ready, 1)

            def relu(u, t):
                wait_alone(act, c_lo, t + 1, act_tick)
                for g in range(HG):
                    nc.scalar.activation(hr[u][:, g * T:(g + 1) * T], hpre[:, ds(g * TOK + t * T, T)], ACT.Relu,
                                         bias=bnc[:, g:g + 1], scale=bna[:, g:g + 1]).then_inc(c_relu, 1)

            def second_out(u, t):
                wait_alone(act, c_mm, t + 1 + RING, act_tick)
                nc.scalar.activation(out2[:, ds(t * T, T)], bank[u][:, :], ACT.Identity,
                                     bias=vec[:, 6:7], scale=1.0 / WSCALE).then_inc(c_out, 1)
            relu(0, 0)
            with act.Fori(0, NT // 2 - 1) as i:
                relu(1, 2 * i + 1)
                second_out(0, 2 * i)
                relu(0, 2 * i + 2)
                second_out(1, 2 * i + 1)
            relu(1, NT - 1)
            second_out(0, NT - 2)
            second_out(1, NT - 1)

            act.wait_ge(bn_ready, 2)
            with act.Fori(0, NT // 4) as q:
                for k in range(4):
                    wait_alone(act, y_t, 4 * q + k + 1, act_tick)
                    nc.scalar.activation(ybuf[k % 2], out2[:, ds((4 * q + k) * T, T)], ACT.Identity,
                                         bias=bnc[:, HG:HG + 1], scale=bna[:, HG:HG + 1]).then_inc(y_done, 1)

            for s in range(HALVES):
                with act.Fori(0, HT // 2) as i:
                    for u in range(2):
                        t = s * HT + 2 * i + u
                        wait_alone(act, row_t, t + 1, act_tick)
                        nc.scalar.activation(xt_hi[:, ds(t * T, T)], bank[2 + u][:, :], ACT.Copy)
                        act.wait_ge(lg_done, t + 1)
                        nc.scalar.activation(xt32[u], bank[2 + u][:, :], ACT.Copy).then_inc(xt_f, 1)
                act.wait_ge(exp_in, s + 1)
                nc.scalar.activation(rt[3], rt[2], ACT.Exp).then_inc(exp_done, 1)

            def gelu_shared(u, t, c):
                act.wait_ge(up_done, FC * t + c + 1)
                act.wait_ge(lo_done, FC * t + c + 1)
                nc.scalar.activation(h32[:, c * T:(c + 1) * T], bank[c][:, :], ACT.Gelu,
                                     bias=vec[:, VEC["b1s"][0] + c:VEC["b1s"][0] + c + 1], scale=1.0 / WSCALE)
                nc.scalar.activation(h_hi[u][:, c * T:(c + 1) * T], bank[c][:, :], ACT.Gelu,
                                     bias=vec[:, VEC["b1s"][0] + c:VEC["b1s"][0] + c + 1],
                                     scale=1.0 / WSCALE).then_inc(gelu_done, 1)

            with act.Fori(0, NT // 2) as i:
                for u in range(2):
                    act.wait_ge(down_done, 2 * i + u + 1)
                    for c in range(FC):
                        gelu_shared(u, 2 * i + u, c)

            def row_high(u, g):
                act.wait_ge(xr_t, g + 1)
                nc.scalar.activation(xr_hi[u], bank[6 + u][:, 0:TR], ACT.Copy).then_inc(xr_h, 1)

            def gelu_routed(u, g):
                e = act.value_load(tile_e[0:1, ds(g, 1)], min_val=0, max_val=E - 1)
                for c in range(FC):
                    act.wait_ge(up_done, NSH + FC * g + c + 1)
                    wait_alone(act, lo_done, NSH + FC * g + c + 1, act_tick)
                    nc.scalar.activation(h32[:, c * TR:(c + 1) * TR], bank[c][:, 0:TR], ACT.Gelu,
                                         bias=vec[:, ds(e * FC + VEC["b1p"][0] + c, 1)],
                                         scale=1.0 / WSCALE).then_inc(gelu_done, 1)
            act.wait_ge(lo_done, NSH + FC)
            row_high(0, 0)
            row_high(1, 1)
            gelu_routed(0, 0)
            with act.Fori(0, NR // 2 - 1) as i:
                for u in range(2):
                    row_high(u, 2 * i + u + 2)
                    gelu_routed(1 - u, 2 * i + u + 1)
            gelu_routed(1, NR - 1)

        @block.vector
        def _(v):
            count = [0]

            def link(ins, base=None):
                count[0] += 1
                ins.then_inc(dve, 1)
                v.wait_ge(dve, count[0] if base is None else base + count[0])

            tt, ts, stt = nc.vector.tensor_tensor, nc.vector.tensor_scalar, nc.vector.scalar_tensor_tensor

            v.sem_inc(lo_done, FC)
            for ring in (c_lo, x2_done, xt_l, lg_out, ffn_out, xr_l):
                v.sem_inc(ring, RING)

            v.wait_ge(prep_hi, 3)
            stt(w1t_lo[:, :], bank[6][:, 0:H], WSCALE, w1t_hi[:, :], ALU.mult, ALU.subtract)
            stt(w2t_lo[:, :], bank[6][:, H:2 * H], WSCALE, w2t_hi[:, :], ALU.mult, ALU.subtract).then_inc(prep_ready, 1)

            def at_low(c):
                lov = at_lo.rearrange("p (m n) -> p m n", m=CH)
                hiv = at_hi.rearrange("p (m n) -> p m n", m=CH)
                for h in range(2):
                    v.wait_ge(at_hi_done, 2 * c + h + 1)
                    tt(lov[:, 4 * h:4 * h + 4, c * P:(c + 1) * P],
                       bank[2 * (c % 2) + h][:, :].rearrange("p (m n) -> p m n", m=4),
                       hiv[:, 4 * h:4 * h + 4, c * P:(c + 1) * P], ALU.subtract).then_inc(at_lo_done, 1)

            v.wait_ge(pool_made, 3)
            for c in range(CH):
                dblk = adjn[:, c * NODES + c * P:c * NODES + (c + 1) * P]
                v.wait_ge(adj_loaded[c], 16)
                tt(dblk, dblk, ident[:, :], ALU.add).then_inc(adj_eye, 1)
                v.wait_ge(adj_eye, c + 1)
                link(stt(junkd, dblk, 1.0, ident[:, :], ALU.mult, ALU.mult, accum_out=diag[:, c:c + 1]))
                if c:
                    at_low(c - 1)
            at_low(CH - 1)
            v.wait_ge(rowsum_done, CH)
            v.wait_ge(colsum_done, 1)
            link(tt(rsum[:, :], rsum[:, :], bank[4][:, 0:CH], ALU.add))
            tt(diag[:, :], rsum[:, :], diag[:, :], ALU.subtract).then_inc(pow_in, 1)

            def variance(b0, n, base=None):
                sv = st[:, :].rearrange("p (b s) -> p b s", s=6)[:, b0:b0 + n, :]
                w = slice(b0, b0 + n)
                tt(msum[:, w], sv[:, :, 1], sv[:, :, 4], ALU.add)
                tt(sm2[:, w], sv[:, :, 2], sv[:, :, 5], ALU.add)
                link(tt(sdiff[:, w], sv[:, :, 1], sv[:, :, 4], ALU.subtract), base)
                ts(mean[:, w], msum[:, w], 0.5, None, ALU.mult)
                link(stt(sdiff[:, w], sdiff[:, w], D / 4.0, sdiff[:, w], ALU.mult, ALU.mult), base)
                link(tt(sm2[:, w], sm2[:, w], sdiff[:, w], ALU.add), base)
                ts(sm2[:, w], sm2[:, w], 1.0 / D, EPS, ALU.mult, ALU.add).then_inc(pow_in, 1)

            for b in range(BATCH):
                v.wait_ge(x_loaded[b], 16)
                for j in range(CH):
                    n = b * CH + j
                    ins = nc.vector.bn_stats(st[:, 6 * n:6 * n + 6], xres[:, n * D:(n + 1) * D])
                link(ins)
                variance(b * CH, CH)
            v.wait_ge(pool_pow, BATCH + 1)
            for c in range(CH):
                ins = ts(diagd[:, c * P:(c + 1) * P], ident[:, :], dinv[:, c:c + 1], None, ALU.mult)
            ins.then_inc(diagd_done, 1)
            link(tt(rstd[:, :].rearrange("p (b c) -> p b c", c=CH), rstd[:, :].rearrange("p (b c) -> p b c", c=CH),
                    dinv[:, :].rearrange("p (o c) -> p o c", o=1).broadcast_to((P, BATCH, CH)), ALU.mult))

            def normalise(b):
                for j in range(CH):
                    n = b * CH + j
                    ins = ts(xnf[:, j * D:(j + 1) * D], xres[:, ds(n * D, D)], mean[:, ds(n, 1)], rstd[:, ds(n, 1)],
                             ALU.subtract, ALU.mult)
                ins.then_inc(xn_f, 1)
                v.wait_ge(xn_h, b + 1)
                tt(xn_lo[:, ds(b * NODES, NODES)], xnf, xn_hi[:, ds(b * NODES, NODES)], ALU.subtract).then_inc(xn_l, 1)

            def agg_low(u, t, wait_free):
                v.wait_ge(agg_done, t + 1)
                if wait_free:
                    v.wait_ge(up1_done, 2 * t - 2)
                tt(aggf[u], bank[u][:, :], dinvrow[:, u * T:(u + 1) * T], ALU.mult).then_inc(agg_f, 1)
                v.wait_ge(agg_h, t + 1)
                tt(agg_lo[u], aggf[u], agg_hi[u], ALU.subtract).then_inc(agg_l, 1)

            def hidden_stats(t):
                v.wait_ge(up1_out, 2 * t + 2)
                for g in range(HG):
                    ins = nc.vector.bn_stats(st_bn[:, ds((g * NT + t) * 6, 6)], hpre[:, ds(g * TOK + t * T, T)])
                return ins

            normalise(0)
            v.wait_ge(act_s, 2)
            agg_low(0, 0, False)
            normalise(1)
            agg_low(1, 1, False)
            hidden_stats(0)
            agg_low(0, 2, True)
            hidden_stats(1)
            with v.Fori(1, BATCH - 1) as b:
                normalise(b + 1)
                agg_low(1, 2 * b + 1, True)
                hidden_stats(2 * b)
                agg_low(0, 2 * b + 2, True)
                hidden_stats(2 * b + 1)
            agg_low(1, NT - 1, True)
            hidden_stats(NT - 2)
            link(hidden_stats(NT - 1))

            for g in range(HG):
                link(nc.vector.bn_aggr(bnm[:, 2 * g:2 * g + 2], st_bn[:, g * NT * 6:(g + 1) * NT * 6]))
            ts(bnv[:, 0:HG], bnm[:, 1:2 * HG:2], EPS, None, ALU.add).then_inc(pow_in, 1)
            v.wait_ge(pool_pow, BATCH + 2)
            link(tt(bna[:, 0:HG], bna[:, 0:HG], vec[:, 2:2 + HG], ALU.mult))
            link(tt(bnc[:, 0:HG], bnm[:, 0:2 * HG:2], bna[:, 0:HG], ALU.mult))
            tt(bnc[:, 0:HG], vec[:, 4:4 + HG], bnc[:, 0:HG], ALU.subtract).then_inc(bn_ready, 1)

            def c_low(u, t):
                v.wait_ge(c_hi, t + 1)
                tt(hr_lo[u], hr[u], hr_hi[u], ALU.subtract).then_inc(c_lo, 1)

            def c_stats(t):
                v.wait_ge(c_out, t + 1 + RING)
                return nc.vector.bn_stats(st_bn[:, ds(t * 6, 6)], out2[:, ds(t * T, T)])
            c_low(0, 0)
            with v.Fori(0, NT // 2 - 1) as i:
                c_low(1, 2 * i + 1)
                c_stats(2 * i)
                c_low(0, 2 * i + 2)
                c_stats(2 * i + 1)
            c_low(1, NT - 1)
            c_stats(NT - 2)
            link(c_stats(NT - 1))
            link(nc.vector.bn_aggr(bnm[:, 0:2], st_bn[:, 0:NT * 6]))
            ts(bnv[:, HG:HG + 1], bnm[:, 1:2], EPS, None, ALU.add).then_inc(pow_in, 1)
            v.wait_ge(pool_pow, BATCH + 3)
            link(tt(bna[:, HG:HG + 1], bna[:, HG:HG + 1], vec[:, 7:8], ALU.mult))
            link(tt(bnc[:, HG:HG + 1], bnm[:, 0:1], bna[:, HG:HG + 1], ALU.mult))
            tt(bnc[:, HG:HG + 1], vec[:, 8:9], bnc[:, HG:HG + 1], ALU.subtract).then_inc(bn_ready, 1)

            for q in range(4):
                with v.Fori(0, 2) as i:
                    for u in range(2):
                        t = 4 * q + 2 * i + u
                        v.wait_ge(y_t, t + 1 + RING)
                        tile = xres[:, ds(t * T, T)]
                        tt(tile, tile, bank[u][:, :], ALU.add).then_inc(x2_done, 1)
                        v.wait_ge(x2_done, t + 1 + RING)
                        for j in range(BT):
                            ins = nc.vector.bn_stats(st[:, ds((t * BT + j) * 6, 6)], xres[:, ds(t * T + j * D, D)])
                        ins.then_inc(stats_done, 1)
                v.wait_ge(stats_done, 4 * (q + 1))
                variance(q * BLK // 4, BLK // 4)

            def rows_out(s, t, tl):
                for j in range(BT):
                    n = t * BT + j
                    ins = ts(pay[s][:, ds((tl * BT + j) * ROW, D)], xres[:, ds(n * D, D)], mean[:, ds(n, 1)], rstd[:, ds(n, 1)],
                             ALU.subtract, ALU.mult)
                ins.then_inc(row_done, 1)

            def rows_low(u, t, tl):
                v.wait_ge(xt_f, t + 1)
                tt(xt_lo[:, ds(t * T, T)], bank[2 + u][:, :], xt_hi[:, ds(t * T, T)], ALU.subtract).then_inc(xt_l, 1)
                v.wait_ge(lg_done, t + 1 + RING)
                return nc.vector.tensor_copy(rt[0][:, ds(tl * BT * E, BT * E)], bank[4 + u][:, 0:BT * E]).then_inc(lg_out, 1)

            def eb(ap):
                return ap.rearrange("p (b o) -> p b o", o=1).broadcast_to((P, HB, E))

            def be(ap):
                return ap.rearrange("p (o e) -> p o e", o=1).broadcast_to((P, HB, E))

            def three(ap):
                return ap.rearrange("p (b e) -> p b e", e=E)

            reduce = nc.vector.tensor_reduce

            for s in range(HALVES):
                v.wait_ge(pool_pow, BATCH + 3 + 2 * (s + 1))
                if s == 0:
                    v.wait_ge(pool_made, 10)
                    v.wait_ge(w_kept[0], 16 * (1 + E // 2))
                    v.wait_ge(w_kept[1], 16 * (E // 2))
                rows_out(s, s * HT, 0)
                with v.Fori(0, HT // 2 - 1) as i:
                    for u in range(2):
                        rows_out(s, s * HT + 2 * i + u + 1, 2 * i + u + 1)
                        rows_low(u, s * HT + 2 * i + u, 2 * i + u)
                rows_out(s, s * HT + HT - 1, HT - 1)
                rows_low(0, s * HT + HT - 2, HT - 2)
                rows_low(1, s * HT + HT - 1, HT - 1)
                v.wait_ge(lg_out, s * HT + HT + RING)

                L, Z, X, EX = rt[0], rt[1], rt[2], rt[3]
                oh1, oh2 = rt[4], rt[5]
                sm = [rt[15][:, 32 * n:32 * n + HB] for n in range(8)]
                m1, f1, m2, f2, S, t1, t2, t3 = sm
                L3 = three(L)
                link(reduce(m1, L3, AX.X, ALU.max))
                tt(three(X), L3, eb(m1), ALU.subtract).then_inc(exp_in, 1)
                link(tt(three(Z), L3, eb(m1), ALU.is_equal))
                link(tt(three(Z), three(Z), be(desc8[:, :]), ALU.mult))
                link(reduce(f1, three(Z), AX.X, ALU.max))
                link(tt(three(oh1), three(Z), eb(f1), ALU.is_equal))
                link(stt(L, oh1, -BIG, L, ALU.mult, ALU.add))
                link(reduce(m2, L3, AX.X, ALU.max))
                link(tt(three(Z), L3, eb(m2), ALU.is_equal))
                link(tt(three(Z), three(Z), be(desc8[:, :]), ALU.mult))
                link(reduce(f2, three(Z), AX.X, ALU.max))
                link(tt(three(oh2), three(Z), eb(f2), ALU.is_equal))
                oh16 = rt[6].bitcast(f16)[:, 0:HB * E]
                tt(oh16, oh1, oh2, ALU.add).then_inc(oh_ready, 1)
                v.wait_ge(exp_done, s + 1)
                link(reduce(S, three(EX), AX.X, ALU.add))
                link(nc.vector.reciprocal(S, S))
                link(tt(three(EX), three(EX), eb(S), ALU.mult))
                tt(rt[8], EX, oh1, ALU.mult)
                link(tt(rt[9], EX, oh2, ALU.mult))
                reduce(t1, three(rt[8]), AX.X, ALU.add)
                link(reduce(t2, three(rt[9]), AX.X, ALU.add))
                link(tt(t3, t1, t2, ALU.add))
                link(nc.vector.reciprocal(t3, t3))
                tt(wgt[0][:, s * HB:(s + 1) * HB], t1, t3, ALU.mult)
                tt(wgt[1][:, s * HB:(s + 1) * HB], t2, t3, ALU.mult)
                pv = pay[s].rearrange("p (b n) -> p b n", n=ROW)
                ts(pv[:, :, D + 1], f2, -1.0, float(E), ALU.mult, ALU.add)
                nc.vector.tensor_copy(pv[:, :, D].bitcast(i32), ids[:, s * HB:(s + 1) * HB])
                v.wait_ge(rank_done, s + 1)
                rank, total = bank[6][:, 0:HB * E], bank[7][:, 0:HB * E]
                incl = rt[10]
                nc.vector.tensor_copy(rt[11].rearrange("p (e b) -> p b e", e=E), three(total))
                link(nc.vector.tensor_copy(rt[12], total))
                for e in range(E):
                    ins = nc.vector.tensor_tensor_scan(incl[:, e * HB:(e + 1) * HB], ones_hb[:, :], rt[11][:, e * HB:(e + 1) * HB],
                                                       0.0, ALU.mult, ALU.add)
                link(ins)
                inc3 = incl.rearrange("p (e b) -> p b e", e=E)
                padded, ends, base = small[0], small[1], small[2]
                sh = TR.bit_length() - 1
                link(ts(small_i[:, :], incl.rearrange("p (e b) -> p e b", e=E)[:, :, HB - 1], float(TR - 1), None, ALU.add))
                link(ts(small_i[:, :], small_i[:, :], sh, sh, ALU.logical_shift_right, ALU.logical_shift_left))
                link(nc.vector.tensor_copy(padded[:, :], small_i[:, :]))
                link(nc.vector.tensor_tensor_scan(ends[:, :], ones_hb[:, 0:E], padded[:, :], 0.0, ALU.mult, ALU.add))
                link(stt(base[:, :], ends[:, :], float(s * TILES * TR), padded[:, :], ALU.add, ALU.subtract))
                link(tt(three(rt[12]), inc3, three(rt[12]), ALU.subtract))
                link(tt(rt[12], rt[12], rank, ALU.add))
                link(tt(three(rt[12]), three(rt[12]), be(base[:, :]), ALU.add))
                tt(rt[8], rt[12], oh1, ALU.mult)
                link(tt(rt[9], rt[12], oh2, ALU.mult))
                reduce(t1, three(rt[8]), AX.X, ALU.add)
                link(reduce(t2, three(rt[9]), AX.X, ALU.add))
                nc.vector.tensor_copy(idx[0][:, s * HB:(s + 1) * HB], t1)
                nc.vector.tensor_copy(idx[1][:, s * HB:(s + 1) * HB], t2)
                cmp = wprep[:, 256 * 13:256 * 13 + TILES * E].rearrange("p (k e) -> p k e", e=E)
                link(tt(cmp, tile_at[:, :].rearrange("p (k o) -> p k o", o=1).broadcast_to((P, TILES, E)),
                        ends[:, :].rearrange("p (o e) -> p o e", o=1).broadcast_to((P, TILES, E)), ALU.is_ge))
                tf = tile_f[:, s * TILES:(s + 1) * TILES]
                link(reduce(tf, cmp, AX.X, ALU.add))
                link(ts(tf, tf, float(E - 1), None, ALU.min))
                nc.vector.tensor_copy(tile_e[:, s * TILES:(s + 1) * TILES], tf).then_inc(route_ready, 1)

            def shared_low(u, t, c):
                v.wait_ge(gelu_done, FC * (t + 1) + c + 1)
                tt(h_lo[u][:, c * T:(c + 1) * T], h32[:, c * T:(c + 1) * T], h_hi[u][:, c * T:(c + 1) * T],
                   ALU.subtract).then_inc(lo_done, 1)

            def shared_out(u, t):
                tile = xres[:, ds(t * T, T)]
                tv = tile.rearrange("p (j d) -> p j d", j=BT)
                tt(tv, tv, b2s_rep[:, :].rearrange("p (o d) -> p o d", o=1).broadcast_to((P, BT, D)), ALU.add).then_inc(bias_in, 1)
                v.wait_ge(bias_in, t + 1)
                v.wait_ge(down_done, t + 1 + RING)
                stt(tile, bank[4 + u][:, :], 1.0 / WSCALE, tile, ALU.mult, ALU.add).then_inc(ffn_out, 1)

            v.wait_ge(late_loaded, 32)
            for c in range(FC):
                shared_low(0, 0, c)
            with v.Fori(0, NT // 2 - 1) as i:
                for u in range(2):
                    for c in range(FC):
                        shared_low(1 - u, 2 * i + u + 1, c)
                    shared_out(u, 2 * i + u)
            for c in range(FC):
                shared_low(1, NT - 1, c)
            shared_out(0, NT - 2)
            shared_out(1, NT - 1)

            def row_low(u, g, turn):
                v.wait_ge(xr_loaded[u], 16 * turn)
                xv = xr[u].rearrange("p (j n) -> p j n", j=RB)
                ts(rflag[u], xv[:, :, D + 1], tile_f[:, ds(g, 1)], float(TOK), ALU.is_equal, ALU.mult).then_inc(dest_made, 1)
                v.wait_ge(xr_h, g + 1)
                tt(xr_lo[u], bank[6 + u][:, 0:TR], xr_hi[u], ALU.subtract).then_inc(xr_l, 1)
                v.wait_ge(dest_made, g + 1)
                tt(dest_all[:, ds(g * RB, RB)], rflag[u], xv[:, :, D].bitcast(i32), ALU.add).then_inc(ids_read, 1)

            def routed_cut(u, g):
                for c in range(0, FC, 2):
                    w = slice(c * TR, (c + 2) * TR)
                    v.wait_ge(gelu_done, NSH + FC * (g + 1) + c + 2)
                    v.wait_ge(down_done, NT + g + 1)
                    nc.vector.tensor_copy(h_hi[u][:, w], h32[:, w]).then_inc(hi_r, 1)
                    v.wait_ge(hi_r, 2 * g + c // 2 + 1)
                    tt(h_lo[u][:, w], h32[:, w], h_hi[u][:, w], ALU.subtract).then_inc(lo_done, 2)

            def routed_out(u, g, free):
                e = v.value_load(tile_e[0:1, ds(g, 1)], min_val=0, max_val=E - 1)
                if free is not None:
                    v.wait_ge(returned[u], free)
                nc.vector.tensor_copy(rdest[u], dest_all[:, ds(g * RB, RB)])
                v.wait_ge(down_done, NT + g + 1 + RING)
                yv = yr[u].rearrange("p (j d) -> p j d", j=RB)
                stt(yv, bank[4 + u][:, 0:TR].rearrange("p (j d) -> p j d", j=RB), 1.0 / WSCALE,
                    b2p_rep[:, ds(e * D, D)].rearrange("p (o d) -> p o d", o=1).broadcast_to((P, RB, D)),
                    ALU.mult, ALU.add).then_inc(ffn_out, 1)

            v.wait_ge(route_ready, HALVES)
            v.wait_ge(b2p_loaded, 16)
            row_low(0, 0, 1)
            row_low(1, 1, 1)
            routed_cut(0, 0)
            for g in range(2):
                row_low(g, g + 2, 2)
                routed_cut(1 - g, g + 1)
                routed_out(g, g, None)
            with v.Fori(1, NR // 2 - 1) as i:
                for u in range(2):
                    g = 2 * i + u
                    row_low(u, g + 2, i + 2)
                    routed_cut(1 - u, g + 1)
                    routed_out(u, g, 16 * RB * i)
            routed_cut(1, NR - 1)
            routed_out(0, NR - 2, 16 * RB * (NR // 2 - 1))
            routed_out(1, NR - 1, 16 * RB * (NR // 2 - 1))

            def combine(u, n, turn):
                v.wait_ge(y_loaded[u], 32 * turn)
                for k, done in enumerate((y_used, combined)):
                    for j in range(GB):
                        blk = n * GB + j
                        acc = xres[:, ds(blk * D, D)]
                        ins = stt(acc, yload[u][k][:, j * D:(j + 1) * D], wgt[k][:, ds(blk, 1)], acc, ALU.mult, ALU.add)
                    ins.then_inc(done, 1)
                    if k == 0:
                        v.wait_ge(y_used, n + 1)

            with v.Fori(0, BLK // GB // 2) as i:
                for u in range(2):
                    combine(u, 2 * i + u, i + 1)

        @block.tensor
        def _(pe):
            mm, transpose = nc.tensor.matmul, nc.tensor.transpose
            for ring in (c_mm, y_t, lg_done, down_done):
                pe.sem_inc(ring, RING)

            def three_pass(o, l, r, start, stop, last_inc=None):
                (lh, ll), (rh, rl) = l, r
                mm(o, lh, rh, start=start, stop=False)
                mm(o, lh, rl, start=False, stop=False)
                return mm(o, ll, rh, start=False, stop=stop)

            pe.wait_ge(small_loaded, 16 * 10)
            pe.wait_ge(pool_made, 5)
            transpose(bank[7][:, 0:NVEC], vrows[0:NVEC, :], ident[0:NVEC, 0:NVEC])
            for g in range(HG):
                transpose(bank[6][:, g * P:(g + 1) * P], gw1[:, g * D:(g + 1) * D], ident[:, :])
                ins = transpose(bank[6][:, H + g * P:H + (g + 1) * P], gw2[:, g * P:(g + 1) * P], ident[:, :])
            ins.then_inc(prep_t, 1)

            for c in range(CH):
                pe.wait_ge(adj_eye, c + 1)
                if c >= 2:
                    pe.wait_ge(at_lo_done, 2 * c - 2)
                for h in range(2):
                    for m in range(4):
                        k = 4 * h + m
                        ins = transpose(bank[2 * (c % 2) + h][:, m * P:(m + 1) * P],
                                        adjn[:, c * NODES + k * P:c * NODES + (k + 1) * P], ident[:, :])
                    ins.then_inc(at_t, 1)
                for k in range(CH):
                    ins = mm(bank[4][:, k:k + 1], adjn[:, c * NODES + k * P:c * NODES + (k + 1) * P], onesf[:, 0:1],
                             start=(c == 0 and k == 0), stop=(c == CH - 1), skip_group_check=True)
            ins.then_inc(colsum_done, 1)
            pe.wait_ge(diagd_done, 1)
            pe.wait_ge(prep_ready, 1)
            for h in range(2):
                ins = mm(bank[5 + h][:, :], onesf[:, :], diagd[:, h * T:(h + 1) * T], start=True, stop=True)
            ins.then_inc(dinv_in_psum, 1)

            def aggregate(u, b, t, free):
                pe.wait_ge(xn_l, b + 1)
                if free is not None:
                    pe.wait_ge(agg_f, free)
                for m in range(CH):
                    l = (xn_hi[:, ds((b * CH + m) * D, D)], xn_lo[:, ds((b * CH + m) * D, D)])
                    w = slice(m * NODES + u * T, m * NODES + (u + 1) * T)
                    ins = three_pass(bank[u][:, :], l, (at_hi[:, w], at_lo[:, w]), m == 0, m == CH - 1)
                ins.then_inc(agg_done, 1)

            def first_product(u, t, free):
                pe.wait_ge(agg_l, t + 1)
                if free is not None:
                    pe.wait_ge(up1_out, free)
                for g in range(HG):
                    w = slice(g * P, (g + 1) * P)
                    three_pass(bank[2 + 2 * u + g][:, :], (w1t_hi[:, w], w1t_lo[:, w]), (agg_hi[u], agg_lo[u]),
                               True, True).then_inc(up1_done, 1)
            pe.wait_ge(at_lo_done, 2 * CH)
            pe.wait_ge(act_s, 2)
            aggregate(0, 0, 0, None)
            aggregate(1, 0, 1, None)
            first_product(0, 0, None)
            aggregate(0, 1, 2, 1)
            first_product(1, 1, None)
            with pe.Fori(1, BATCH - 1) as b:
                aggregate(1, b, 2 * b + 1, 2 * b)
                first_product(0, 2 * b, 4 * b - 2)
                aggregate(0, b + 1, 2 * b + 2, 2 * b + 1)
                first_product(1, 2 * b + 1, 4 * b)
            aggregate(1, BATCH - 1, NT - 1, NT - 2)
            first_product(0, NT - 2, 2 * NT - 6)
            first_product(1, NT - 1, 2 * NT - 4)

            with pe.Fori(0, NT // 2) as i:
                for u in range(2):
                    t = 2 * i + u
                    pe.wait_ge(c_lo, t + 1 + RING)
                    pe.wait_ge(c_out, t + 1)
                    for g in range(HG):
                        w = slice(g * P, (g + 1) * P)
                        r = (hr_hi[u][:, g * T:(g + 1) * T], hr_lo[u][:, g * T:(g + 1) * T])
                        ins = three_pass(bank[u][:, :], (w2t_hi[:, w], w2t_lo[:, w]), r, g == 0, g == HG - 1)
                    ins.then_inc(c_mm, 1)

            with pe.Fori(0, NT // 2) as i:
                for u in range(2):
                    t = 2 * i + u
                    pe.wait_ge(y_done, t + 1)
                    pe.wait_ge(x2_done, t + 1)
                    for j in range(BT):
                        ins = transpose(bank[u][:, j * P:(j + 1) * P], ybuf[u][:, j * P:(j + 1) * P], ident[:, :])
                    ins.then_inc(y_t, 1)

            pe.wait_ge(late_loaded, 32)

            def rows_t(s, u, t, tl):
                pe.wait_ge(row_done, t + 1)
                pe.wait_ge(xt_l, t + 1)
                for j in range(BT):
                    ins = transpose(bank[2 + u][:, j * P:(j + 1) * P], pay[s][:, (tl * BT + j) * ROW:(tl * BT + j) * ROW + D], ident[:, :])
                ins.then_inc(row_t, 1)

            def logits(u, t):
                pe.wait_ge(xt_f, t + 1)
                pe.wait_ge(lg_out, t + 1)
                for j in range(BT):
                    ins = mm(bank[4 + u][:, j * E:(j + 1) * E], xt32[u][:, j * P:(j + 1) * P], wr_sb[:, :], start=True, stop=True)
                ins.then_inc(lg_done, 1)
            for s in range(HALVES):
                rows_t(s, 0, s * HT, 0)
                for n in range(HT):
                    if n + 1 < HT:
                        rows_t(s, (n + 1) % 2, s * HT + n + 1, n + 1)
                    logits(n % 2, s * HT + n)
                pe.wait_ge(oh_ready, s + 1)
                oh16 = rt[6].bitcast(f16)[:, 0:HB * E]
                mm(bank[6][:, 0:HB * E], before16[:, :], oh16, start=True, stop=True)
                mm(bank[7][:, 0:HB * E], ones16[:, :], oh16, start=True, stop=True).then_inc(rank_done, 1)

            pe.wait_ge(wall_loaded, 16)
            SW = E * 2048

            def shared_up(t):
                for c in range(FC):
                    pe.wait_ge(gelu_done, FC * t + c + 1)
                    a, b_ = SW + W1S + c * P, SW + W1L + c * P
                    three_pass(bank[c][:, :], (wall[:, a:a + P], wall[:, b_:b_ + P]),
                               (xt_hi[:, ds(t * T, T)], xt_lo[:, ds(t * T, T)]), True, True).then_inc(up_done, 1)

            def shared_down(u, t):
                pe.wait_ge(lo_done, FC * (t + 2))
                pe.wait_ge(ffn_out, t + 1)
                for j in range(BT):
                    for c in range(FC):
                        l = tuple(h[:, c * T + j * P:c * T + (j + 1) * P] for h in (h_hi[u], h_lo[u]))
                        a, b_ = SW + W2S + c * D, SW + W2L + c * D
                        ins = three_pass(bank[4 + u][:, j * D:(j + 1) * D], l, (wall[:, a:a + D], wall[:, b_:b_ + D]),
                                         c == 0, c == FC - 1)
                ins.then_inc(down_done, 1)

            pe.wait_ge(x2_done, NT + RING)
            pe.wait_ge(xt_l, NT + RING)
            pe.wait_ge(lg_out, NT + RING)
            shared_up(0)
            with pe.Fori(0, NT // 2 - 1) as i:
                for u in range(2):
                    shared_up(2 * i + u + 1)
                    shared_down(u, 2 * i + u)
            shared_up(NT - 1)
            shared_down(0, NT - 2)
            shared_down(1, NT - 1)

            def routed_t(u, g, turn):
                pe.wait_ge(xr_loaded[u], 16 * turn)
                pe.wait_ge(xr_l, g + 1)
                for j in range(RB):
                    ins = transpose(bank[6 + u][:, j * P:(j + 1) * P], xr[u][:, j * ROW:j * ROW + D], ident[:, :])
                ins.then_inc(xr_t, 1)

            def routed_up(u, g):
                e = pe.value_load(tile_e[0:1, ds(g, 1)], min_val=0, max_val=E - 1)
                pe.wait_ge(xr_l, g + 1 + RING)
                for c in range(FC):
                    pe.wait_ge(gelu_done, NSH + FC * g + c + 1)
                    l = (wall[:, ds(e * 2048 + W1S + c * P, P)], wall[:, ds(e * 2048 + W1L + c * P, P)])
                    three_pass(bank[c][:, 0:TR], l, (xr_hi[u], xr_lo[u]), True, True).then_inc(up_done, 1)

            def routed_down(u, g):
                e = pe.value_load(tile_e[0:1, ds(g, 1)], min_val=0, max_val=E - 1)
                pe.wait_ge(lo_done, NSH + FC * (g + 2))
                pe.wait_ge(ffn_out, NT + g + 1)
                for j in range(RB):
                    for c in range(FC):
                        l = tuple(h[:, c * TR + j * P:c * TR + (j + 1) * P] for h in (h_hi[u], h_lo[u]))
                        r = (wall[:, ds(e * 2048 + W2S + c * D, D)], wall[:, ds(e * 2048 + W2L + c * D, D)])
                        ins = three_pass(bank[4 + u][:, j * D:(j + 1) * D], l, r, c == 0, c == FC - 1)
                ins.then_inc(down_done, 1)

            routed_t(0, 0, 1)
            routed_t(1, 1, 1)
            routed_up(0, 0)
            with pe.Fori(0, NR // 2 - 1) as i:
                for u in range(2):
                    g = 2 * i + u
                    routed_t(u, g + 2, i + 2)
                    routed_up(1 - u, g + 1)
                    routed_down(u, g)
            routed_up(1, NR - 1)
            routed_down(0, NR - 2)
            routed_down(1, NR - 1)


INS = ["x", "adj"] + [f"L0_gnn_{n}" for n in ("W1", "b1", "g1", "be1", "W2", "b2", "g2", "be2")] + \
      [f"L0_ffn_{n}" for n in ("Wr", "W1s", "b1s", "W2s", "b2s", "W1p", "b1p", "W2p", "b2p")]


def kernel(**inputs):
    import numpy as np
    import concourse.bacc as bacc
    from concourse import mybir as _mybir
    from concourse.bass_utils import run_bass_kernel_spmd

    nc = bacc.Bacc("TRN2", target_bir_lowering=False, num_devices=1)
    arrays, args = {}, []
    for name in INS:
        a = np.ascontiguousarray(inputs[name])
        arrays[f"in_{name}"] = a
        args.append(nc.dram_tensor(f"in_{name}", a.shape, _mybir.dt.from_np(a.dtype), kind="ExternalInput").ap())
    out = nc.dram_tensor("result", (TOK, D), _mybir.dt.float32, kind="ExternalOutput").ap()
    build(nc, *args, out)
    r = run_bass_kernel_spmd(nc, [arrays], core_ids=[0])
    return r.results[0]["result"].reshape(BATCH, NODES, D)
```

```python
import concourse.bass as bass
from concourse import mybir
from contextlib import ExitStack

P = 128
D = 128
NODES = 1024
BATCH = 8
TOK = BATCH * NODES
CH = NODES // P
BLK = TOK // P
H = 256
HG = H // P
F = 512
FC = F // P
E = 8
T = 512
NT = TOK // T
BT = T // P
HALVES = 2
HB = BLK // HALVES
HT = NT // HALVES
TR = 256
RB = TR // P
GB = 8
GH = HB // GB
TILES = (2 * TOK // HALVES + E * (TR - 1)) // TR
NR = HALVES * TILES
STEP = 2
XGROUPS = ((0, 2), (2, 4), (4, BATCH))
LATE = 34
LEAD = 3
SUM0 = 23
ROW = D + 2
SKIP = 1 << 20
WSCALE = 256.0
EPS = 1e-5
BIG = 3.0e38

VEC = dict(b1=(0, HG), g1=(2, HG), be1=(4, HG), b2=(6, 1), g2=(7, 1), be2=(8, 1), b1s=(9, FC), b1p=(13, E * FC))
NVEC = 13 + E * FC


def build(nc, x, adj, W1, b1, g1, be1, W2, b2, g2, be2, Wr, W1s, b1s, W2s, b2s, W1p, b1p, W2p, b2p, out):
    f32, f16, i32 = mybir.dt.float32, mybir.dt.float16, mybir.dt.int32
    ALU = mybir.AluOpType
    ACT = mybir.ActivationFunctionType
    AX = mybir.AxisListType
    ds = bass.ds

    def wait_alone(engine, semaphore, value, tick):
        engine.wait_ge(semaphore, value)
        engine.sem_inc(tick, 1)

    class Experts:
        def __init__(self, engine, table):
            self.engine, self.table = engine, table
            self.regs = [engine.alloc_register(f"expert{n}") for n in range(3)]
            self.later = [engine.alloc_register(f"later{n}") for n in range(2)]

        def fetch_first(self):
            for n in range(3):
                self.engine.reg_load(self.regs[n], self.table[0:1, n:n + 1])

        def fetch(self, g):
            self.engine.load(self.later, self.table[0:1, ds(g, 2)])

        def shift(self):
            self.engine.reg_mov(self.regs[0], self.regs[2])
            for n in range(2):
                self.engine.reg_mov(self.regs[n + 1], self.later[n])

        def of(self, n):
            return self.engine.snap(self.regs[n], min_val=0, max_val=E - 1)

    ctx = ExitStack()
    with ctx:
        def sb(name, cols, dt=f32, parts=P):
            return ctx.enter_context(nc.sbuf_tensor(name, [parts, cols], dt))

        def sem(name):
            return ctx.enter_context(nc.semaphore(name))

        xres = sb("xres", BLK * D)
        region1 = sb("region1", 16384)
        region2 = sb("region2", 16384)
        misc = sb("misc", HB * ROW)
        wprep = sb("wprep", 4096)

        r1h = region1[:, :].bitcast(f16)
        at_hi, at_lo = r1h[:, 0:8192], r1h[:, 8192:16384]
        xn_hi, xn_lo = r1h[:, 16384:24576], r1h[:, 24576:32768]
        wall = r1h[:, 0:(E + 1) * 2048]
        pay0 = region1[:, 9216:9216 + HB * ROW]
        ybuf = [region1[:, 13440 + 512 * u:13952 + 512 * u] for u in range(2)]

        b2p_raw = region1[0:2, 13440:13440 + E * D]
        b2p_hi = region1[0:2, 14464:14464 + E * D // 2].bitcast(f16)
        b2p_cut = region1[0:2, 15488:15488 + E * D // 2].bitcast(f16)

        adjn = region2[:, 0:8192]
        hpre = region2
        out2 = region2[:, 0:8192]
        r2h = region2[:, 8192:16384].bitcast(f16)
        xt_hi, xt_lo = r2h[:, 0:8192], r2h[:, 8192:16384]
        h32 = region2[:, 0:FC * T]
        fh = region2[:, 2048:6144].bitcast(f16)
        h_hi = [fh[:, 4096 * u:4096 * u + 2048] for u in range(2)]
        h_lo = [fh[:, 4096 * u + 2048:4096 * u + 4096] for u in range(2)]
        xr = [region2[:, 6144 + 320 * u:6144 + 320 * u + RB * ROW] for u in range(2)]
        yr = [region2[:, 6784 + 256 * u:7040 + 256 * u] for u in range(2)]
        xrh = region2[:, 7296:7808].bitcast(f16)
        xr_hi = [xrh[:, 512 * u:512 * u + 256] for u in range(2)]
        xr_lo = [xrh[:, 512 * u + 256:512 * u + 512] for u in range(2)]
        rdest = [region2[:, 7824 + 8 * u:7824 + 8 * u + RB].bitcast(i32) for u in range(2)]

        xnf = misc[:, 0:1024]
        aggf = [misc[:, 1024 + 512 * u:1536 + 512 * u] for u in range(2)]
        mh = misc[:, 2048:3072].bitcast(f16)
        agg_hi = [mh[:, 1024 * u:1024 * u + 512] for u in range(2)]
        agg_lo = [mh[:, 1024 * u + 512:1024 * u + 1024] for u in range(2)]
        dinvrow = misc[:, 3072:4096]
        diagd = misc[:, 1024:2048]
        junk = misc[:, 0:1024]
        junkd = misc[:, 2048:2176]
        hr = [misc[:, 1024 * u:1024 * u + 1024] for u in range(2)]
        mc = misc[:, 2048:4096].bitcast(f16)
        hr_hi = [mc[:, 2048 * u:2048 * u + 1024] for u in range(2)]
        hr_lo = [mc[:, 2048 * u + 1024:2048 * u + 2048] for u in range(2)]
        pay1 = misc[:, 0:HB * ROW]
        pay = [pay0, pay1]
        yload = [[misc[:, (2 * u + k) * 1024:(2 * u + k + 1) * 1024] for k in range(2)] for u in range(2)]

        wraw = [wprep[:, 1024 * u:1024 * u + 1024] for u in range(2)]
        wph = wprep[:, 2048:4096].bitcast(f16)
        wcut = [wph[:, 2048 * u:2048 * u + 2048] for u in range(2)]
        rt = [wprep[:, 256 * n:256 * n + 256] for n in range(16)]

        ident = sb("ident_sb", P)
        onesf = sb("onesf", P)
        ones16 = sb("ones16", P, f16)
        before16 = sb("before16", P, f16)
        gw1 = sb("gw1", HG * D)
        gw2 = sb("gw2", H)
        w1t_hi, w1t_lo = sb("w1t_hi", H, f16), sb("w1t_lo", H, f16)
        w2t_hi, w2t_lo = sb("w2t_hi", H, f16), sb("w2t_lo", H, f16)
        vrows = sb("vrows", P)
        vec = sb("vec", NVEC)
        wr_sb = sb("wr_sb", E)
        wr_hi, wr_lo = sb("wr_hi", E, f16), sb("wr_lo", E, f16)
        b2s_rep = sb("b2s_rep", D)
        st = sb("st", BLK * 6)
        st_bn = sb("st_bn", HG * NT * 6)
        msum, rstd = sb("msum", BLK), sb("rstd", BLK)
        mean = sb("mean", BLK)
        ids = sb("ids", BLK, i32)
        tails = sb("tails", NR * RB * 2)
        second = [sb(f"second{s}", HB * 2) for s in range(HALVES)]
        sdiff, sm2 = sb("sdiff", BLK), sb("sm2", BLK)
        mhalf = sb("mhalf", BLK)
        csum = sb("csum", CH)
        rsum, diag, dinv = sb("rsum", CH), sb("diag", CH), sb("dinv", CH)
        bnm = sb("bnm", 2 * HG)
        bna, bnc = sb("bna", 4), sb("bnc", 4)
        bnv = sb("bnv", 4)
        desc8 = sb("desc8", E)
        tile_at = sb("tile_at", TILES)
        ones_hb = sb("ones_hb", HB)
        trash = sb("trash", RB * ROW)
        idx = [sb(f"idx{k}", BLK, i32) for k in range(2)]
        tile_f = sb("tile_f", TILES)
        tile_e = sb("tile_e", NR + 1, i32)
        small = [sb(f"small{n}", E) for n in range(4)]
        small_i = sb("small_i", E, i32)

        bank = [ctx.enter_context(nc.psum_tensor(f"bank{n}", [P, 512], f32)) for n in range(8)]

        wsc = nc.dram_tensor("weights_cut", (E + 1, P, 2048), f16, kind="Internal").ap()
        xs = nc.dram_tensor("rows_by_expert", (NR * TR, ROW), f32, kind="Internal").ap()
        ys = nc.dram_tensor("rows_by_token", (2 * TOK, D), f32, kind="Internal").ap()

        small_loaded = sem("small_loaded")
        late_loaded, b2p_loaded = sem("late_loaded"), sem("b2p_loaded")
        adj_loaded = [sem(f"adj_loaded{c}") for c in range(CH)]
        x_loaded = [sem(f"x_loaded{b}") for b in range(BATCH)]
        pool_made = sem("pool_made")
        pool_pow = sem("pool_pow")
        act_tick, pool_tick = sem("act_tick"), sem("pool_tick")
        pow_in = sem("pow_in")
        dve = sem("dve")
        act_s = sem("act_s")
        w_raw = [sem(f"w_raw{u}") for u in range(2)]
        w_cut = sem("w_cut")
        w_chain = sem("w_chain")
        w_kept = [sem(f"w_kept{u}") for u in range(2)]
        wall_loaded = sem("wall_loaded")
        trash_stored = sem("trash_stored")
        prep_t = sem("prep_t")
        prep_hi = sem("prep_hi")
        prep_ready = sem("prep_ready")
        adj_eye = sem("adj_eye")
        at_t, at_hi_done, at_lo_done = sem("at_t"), sem("at_hi_done"), sem("at_lo_done")
        colsum_done = sem("colsum_done")
        rowsum_done = sem("rowsum_done")
        diagd_done = sem("diagd_done")
        dinv_in_psum = sem("dinv_in_psum")
        xn_f, xn_h, xn_l = sem("xn_f"), sem("xn_h"), sem("xn_l")
        agg_done, agg_f, agg_h, agg_l = sem("agg_done"), sem("agg_f"), sem("agg_h"), sem("agg_l")
        up1_done, up1_out = sem("up1_done"), sem("up1_out")
        bn_ready, scale_in, wr_cut = sem("bn_ready"), sem("scale_in"), sem("wr_cut")
        c_relu, c_hi, c_lo, c_mm, c_out, c_stat = (sem(n) for n in ("c_relu", "c_hi", "c_lo", "c_mm", "c_out", "c_stat"))
        y_done, y_t, x2_done = sem("y_done"), sem("y_t"), sem("x2_done")
        row_done, row_t, xt_h, xt_l, lg_done, lg_out = (
            sem(n) for n in ("row_done", "row_t", "xt_h", "xt_l", "lg_done", "lg_out"))
        exp_in, exp_done = sem("exp_in"), sem("exp_done")
        oh_ready, rank_done, route_ready = sem("oh_ready"), sem("rank_done"), sem("route_ready")
        dispatched = [sem(f"dispatched{s}") for s in range(HALVES)]
        stats_done, bias_in = sem("stats_done"), sem("bias_in")
        tails_read, hi_r, bias_cut = sem("tails_read"), sem("hi_r"), sem("bias_cut")
        second_in, y_out, dest_in = sem("second_in"), sem("y_out"), sem("dest_in")
        up_done, gelu_done, lo_done, down_done, ffn_out = (
            sem(n) for n in ("up_done", "gelu_done", "lo_done", "down_done", "ffn_out"))
        xr_loaded = [sem(f"xr_loaded{u}") for u in range(2)]
        xr_t, xr_h, xr_l = sem("xr_t"), sem("xr_h"), sem("xr_l")
        returned = [sem(f"returned{u}") for u in range(2)]
        y_loaded = [sem(f"y_loaded{u}") for u in range(2)]
        y_used = sem("y_used")
        combined = sem("combined")
        stored = sem("stored")

        RING = 2

        block = ctx.enter_context(nc.Block())
        W1S, W1L, W2S, W2L = 0, 512, 1024, 1536
        NSH = NT * FC

        @block.sync
        def _(sp):
            def rows(v, n, at):
                sp.dma_start(vrows[at:at + n, :], v).then_inc(small_loaded, 16)
            rows(b1.rearrange("(g p) -> g p", p=P), HG, VEC["b1"][0])
            rows(g1.rearrange("(g p) -> g p", p=P), HG, VEC["g1"][0])
            rows(be1.rearrange("(g p) -> g p", p=P), HG, VEC["be1"][0])
            rows(b2.rearrange("(g p) -> g p", p=P), 1, VEC["b2"][0])
            rows(g2.rearrange("(g p) -> g p", p=P), 1, VEC["g2"][0])
            rows(be2.rearrange("(g p) -> g p", p=P), 1, VEC["be2"][0])
            rows(b1s.rearrange("(g p) -> g p", p=P), FC, VEC["b1s"][0])
            rows(b1p.rearrange("e (g p) -> (e g) p", p=P), E * FC, VEC["b1p"][0])
            sp.dma_start(gw1[:, :].rearrange("p (g d) -> p g d", g=HG),
                         W1.rearrange("(g p) d -> p g d", p=P)).then_inc(small_loaded, 16)
            sp.dma_start(gw2[:, :], W2).then_inc(small_loaded, 16)
            def raw(u, w1, w2):
                sp.dma_start(wraw[u][:, 0:F], w1).then_inc(w_raw[u], 16)
                sp.dma_start(wraw[u][:, F:2 * F].rearrange("p (c d) -> p c d", c=FC), w2).then_inc(w_raw[u], 16)

            def keep(u, e):
                sp.dma_start(wsc[ds(e, 1), :, :].rearrange("o p n -> (o p) n"), wcut[u]).then_inc(w_kept[u], 16)

            for c in range(CH):
                sp.dma_start(adjn[:, c * NODES:(c + 1) * NODES], adj[c * P:(c + 1) * P, :]).then_inc(adj_loaded[c], 16)
                if c == 1:
                    raw(0, W1s, W2s.rearrange("(c p) d -> p c d", p=P))
            for b in range(BATCH):
                sp.dma_start(xres[:, b * NODES:(b + 1) * NODES].rearrange("p (c d) -> p c d", c=CH),
                             x[b].rearrange("(c p) d -> p c d", p=P)).then_inc(x_loaded[b], 16)
            sp.dma_start(wr_sb[:, :], Wr).then_inc(late_loaded, 16)
            sp.dma_start(b2s_rep[:, :], b2s.rearrange("(o d) -> o d", o=1).broadcast_to((P, D))).then_inc(late_loaded, 16)

            sp.wait_ge(w_cut, 1)
            keep(0, E)
            with sp.Fori(0, E // 2) as i:
                for u in range(2):
                    raw(u, W1p[ds(2 * i + u, 1), :, :].rearrange("o p f -> (o p) f"),
                        W2p[ds(2 * i + u, 1), :, :].rearrange("o (c p) d -> p (o c) d", p=P))
                for u in range(2):
                    sp.wait_ge(w_cut, 2 * i + u + 2)
                    keep(u, 2 * i + u)

            sp.wait_ge(pool_made, 8)
            with sp.Fori(0, NR) as k:
                sp.dma_start(xs[ds(k * TR, TR), :].rearrange("(j p) n -> p j n", p=P),
                             trash[:, :].rearrange("p (j n) -> p j n", j=RB)).then_inc(trash_stored, 16)

            sp.wait_ge(agg_done, NT)
            sp.wait_ge(w_kept[0], 16 * (1 + E // 2))
            sp.wait_ge(w_kept[1], 16 * (E // 2))
            sp.dma_start(wall.rearrange("p (e n) -> p e n", e=E + 1), wsc.rearrange("e p n -> p e n")).then_inc(wall_loaded, 16)

            def load_rows(u, g, use):
                sp.wait_ge(xr_t, use)
                sp.wait_ge(tails_read, use)
                sp.dma_start(xr[u].rearrange("p (j n) -> p j n", j=RB),
                             xs[ds(g * TR, TR), :].rearrange("(j p) n -> p j n", p=P)).then_inc(xr_loaded[u], 16)
            sp.wait_ge(x2_done, NT + RING)
            sp.dma_start(b2p_raw, b2p.rearrange("(o e) d -> o (e d)", o=1).broadcast_to((2, E * D))).then_inc(b2p_loaded, 16)
            sp.wait_ge(dispatched[0], 16 * 2 * HB)
            for g in range(2):
                sp.dma_start(xr[g].rearrange("p (j n) -> p j n", j=RB),
                             xs[g * TR:(g + 1) * TR, :].rearrange("(j p) n -> p j n", p=P)).then_inc(xr_loaded[g], 16)
            with sp.Fori(1, TILES // 2) as i:
                for u in range(2):
                    load_rows(u, 2 * i + u, 2 * i + u - 1)
            load_rows(0, TILES - 1, TILES - 2)
            sp.wait_ge(dispatched[1], 16 * 2 * HB)
            load_rows(1, TILES, TILES - 1)
            def load_y(u, n):
                for k in range(2):
                    sp.dma_start(yload[u][k].rearrange("p (b d) -> p b d", b=GB),
                                 ys[ds(k * TOK + n * GB * P, GB * P), :].rearrange("(b p) d -> p b d", p=P)).then_inc(y_loaded[u], 16)

            def store(n):
                sp.dma_start(out[ds(n * GB * P, GB * P), :].rearrange("(b p) d -> p b d", p=P),
                             xres[:, ds(n * GB * D, GB * D)].rearrange("p (b d) -> p b d", b=GB)).then_inc(stored, 16)

            def load_pairs(first, end):
                with sp.Fori(first, end) as i:
                    for u in range(2):
                        load_rows(u, 2 * i + u, 2 * i + u - 1)

            def sum_step(w, n):
                load_y(w, n)
                load_pairs(SUM0 + 1 + n * STEP, SUM0 + 1 + (n + 1) * STEP)

            def store_earlier(n):
                sp.wait_ge(combined, n)
                store(n - 1)
            load_pairs((TILES + 1) // 2, SUM0 + 1)
            sp.wait_ge(returned[0], 16 * RB * (TILES + 1) // 2)
            sp.wait_ge(returned[1], 16 * RB * (TILES // 2))
            sum_step(0, 0)
            sum_step(1, 1)
            store_earlier(1)
            with sp.Fori(1, GH // 2) as m:
                for w in range(2):
                    sum_step(w, 2 * m + w)
                    store_earlier(2 * m + w)
            load_pairs(SUM0 + 1 + GH * STEP, NR // 2)
            store_earlier(GH)
            sp.wait_ge(returned[0], 16 * RB * NR // 2)
            sp.wait_ge(returned[1], 16 * RB * NR // 2)
            load_y(0, GH)
            load_y(1, GH + 1)
            with sp.Fori(GH // 2, GH - 1) as i:
                for u in range(2):
                    sp.wait_ge(combined, 2 * i + u + 1)
                    load_y(u, 2 * i + u + 2)
                    store(2 * i + u)
            for n in range(2 * GH - 2, 2 * GH):
                sp.wait_ge(combined, n + 1)
                store(n)
            sp.wait_ge(stored, 16 * (BLK // GB))
            sp.wait_ge(trash_stored, 16 * NR)

        @block.gpsimd
        def _(pool):
            pool.memset(ident[:, :], 0.0).then_inc(pool_made, 1)
            pool.memset(before16[:, :], 1.0).then_inc(pool_made, 1)
            pool.wait_ge(pool_made, 2)
            pool.affine_select(out=ident[:, :], in_=ident[:, :], compare_op=ALU.not_equal, fill=1.0,
                               base=0, pattern=[[-1, P]], channel_multiplier=1).then_inc(pool_made, 1)
            pool.affine_select(out=before16[:, :], in_=before16[:, :], compare_op=ALU.is_gt, fill=0.0,
                               base=0, pattern=[[1, P]], channel_multiplier=-1).then_inc(pool_made, 1)
            pool.memset(onesf[:, :], 1.0)
            pool.memset(ones16[:, :], 1.0)
            pool.memset(ones_hb[:, :], 1.0)
            pool.memset(mhalf[:, :], -0.5).then_inc(pool_made, 1)
            pool.iota(desc8[:, :], [[-1, E]], base=E, channel_multiplier=0, allow_small_or_imprecise_dtypes=True)
            pool.iota(tile_at[:, :], [[TR, TILES]], base=0, channel_multiplier=0,
                      allow_small_or_imprecise_dtypes=True).then_inc(pool_made, 1)
            pool.memset(tile_e[:, NR:NR + 1], 0)
            pool.memset(trash[:, :], 0.0).then_inc(pool_made, 1)
            pool.wait_ge(pool_made, 7)
            tv = trash[:, :].rearrange("p (j n) -> p j n", j=RB)
            pool.iota(tv[:, :, D:D + 1].bitcast(i32), [[P, RB], [0, 1]], base=SKIP, channel_multiplier=1).then_inc(pool_made, 1)

            def inverse_root(o, v, n, turn):
                pool.wait_ge(pow_in, turn)
                pool.tensor_tensor(o, v, mhalf[:, 0:n], ALU.pow).then_inc(pool_pow, 1)

            pool.iota(ids[:, :], [[P, BLK]], base=0, channel_multiplier=1).then_inc(pool_made, 1)

            def cut(u, turn, kept):
                v = wraw[u].rearrange("p (w f) -> p w f", w=2)
                parts = wcut[u].rearrange("p (w s f) -> p w s f", w=2, s=2)
                wait_alone(pool, w_raw[u], 32 * turn, pool_tick)
                pool.tensor_scalar(v, v, WSCALE, None, ALU.mult).then_inc(w_chain, 1)
                if kept is not None:
                    pool.wait_ge(w_kept[u], kept)
                return v, parts

            def cut2(u, v, parts, c):
                wait_alone(pool, w_chain, c + 1, pool_tick)
                pool.tensor_copy(parts[:, :, 0, :], v).then_inc(w_chain, 1)
                pool.wait_ge(w_chain, c + 2)
                pool.tensor_tensor(parts[:, :, 1, :], v, parts[:, :, 0, :], ALU.subtract).then_inc(w_cut, 1)

            v, parts = cut(0, 1, None)
            cut2(0, v, parts, 0)
            def batch_root(b, turn):
                inverse_root(rstd[:, b * CH:(b + 1) * CH], sm2[:, b * CH:(b + 1) * CH], CH, turn)

            batch_root(0, 1)
            inverse_root(dinv[:, :], diag[:, :], CH, 2)
            batch_root(1, 1)
            for n, (b0, b1) in enumerate(XGROUPS[1:]):
                for b in range(b0, b1):
                    batch_root(b, 3 + n)

            v, parts = cut(0, 2, 16)
            cut2(0, v, parts, 2)
            v, parts = cut(1, 1, None)
            cut2(1, v, parts, 4)
            with pool.Fori(1, E // 2) as i:
                for u in range(2):
                    v, parts = cut(u, i + (2 if u == 0 else 1), 16 * i + (16 if u == 0 else 0))
                    cut2(u, v, parts, 4 * i + 2 * u + 2)

            inverse_root(bna[:, 0:HG], bnv[:, 0:HG], HG, 5)
            inverse_root(bna[:, HG:HG + 1], bnv[:, HG:HG + 1], 1, 6)
            Q = BLK // 4
            for q in range(4):
                inverse_root(rstd[:, q * Q:(q + 1) * Q], sm2[:, q * Q:(q + 1) * Q], Q, 7 + q)

            pool.wait_ge(trash_stored, 16 * NR)
            def dispatch(s, k, n):
                blk = s * HB + n
                pool.indirect_dma_start(xs, bass.IndirectOffsetOnAxis(idx[k][:, blk:blk + 1], 0),
                                        pay[s][:, n * ROW:(n + 1) * ROW], None).then_inc(dispatched[s], 16)

            def second_tails(s):
                pool.wait_ge(dispatched[s], 16 * HB)
                pv = pay[s].rearrange("p (b n) -> p b n", n=ROW)
                pool.tensor_copy(pv[:, :, D:ROW], second[s][:, :].rearrange("p (b n) -> p b n", n=2)).then_inc(second_in, 1)
                pool.wait_ge(second_in, s + 1)

            def give_back(u, g):
                wait_alone(pool, y_out, g + 1 + RING, pool_tick)
                wait_alone(pool, dest_in, g + 1, pool_tick)
                for j in range(RB):
                    pool.indirect_dma_start(ys, bass.IndirectOffsetOnAxis(rdest[u][:, j:j + 1], 0),
                                            yr[u][:, j * D:(j + 1) * D], None,
                                            bounds_check=2 * TOK - 1, oob_is_err=False).then_inc(returned[u], 16)

            pool.wait_ge(route_ready, 1)
            for n in range(HB):
                dispatch(0, 0, n)
            second_tails(0)
            for n in range(HB):
                dispatch(0, 1, n)
            pool.wait_ge(route_ready, 2)
            for n in range(2 * HB - LATE):
                dispatch(1, 0, n)
            for g in range(LATE):
                give_back(g % 2, g)
                n = 2 * HB - LATE + g
                if n == HB:
                    second_tails(1)
                dispatch(1, n // HB, n % HB)
            with pool.Fori(LATE // 2, NR // 2) as i:
                for u in range(2):
                    give_back(u, 2 * i + u)

        @block.scalar
        def _(act):
            act.sem_inc(c_out, RING)
            act.sem_inc(gelu_done, FC)
            act.sem_inc(y_out, RING)
            act.wait_ge(prep_t, 1)
            nc.scalar.activation(vec[:, :], bank[7][:, 0:NVEC], ACT.Copy).then_inc(prep_hi, 1)
            nc.scalar.activation(w1t_hi[:, :], bank[6][:, 0:H], ACT.Copy, scale=WSCALE).then_inc(prep_hi, 1)
            nc.scalar.activation(w2t_hi[:, :], bank[6][:, H:2 * H], ACT.Copy, scale=WSCALE).then_inc(prep_hi, 1)

            atv = at_hi.rearrange("p (m n) -> p m n", m=CH)
            for c in range(CH):
                act.wait_ge(adj_eye, c + 1)
                if c:
                    act.wait_ge(rowsum_done, c)
                nc.scalar.activation(junk, adjn[:, c * NODES:(c + 1) * NODES], ACT.Copy,
                                     accum_out=rsum[:, c:c + 1]).then_inc(rowsum_done, 1)
                for h in range(2):
                    act.wait_ge(at_t, 2 * c + h + 1)
                    nc.scalar.activation(atv[:, 4 * h:4 * h + 4, c * P:(c + 1) * P],
                                         bank[2 * (c % 2) + h][:, :].rearrange("p (m n) -> p m n", m=4),
                                         ACT.Copy).then_inc(at_hi_done, 1)
            def xn_high(b):
                wait_alone(act, xn_f, b + 1, act_tick)
                nc.scalar.activation(xn_hi[:, ds(b * NODES, NODES)], xnf, ACT.Copy).then_inc(xn_h, 1)

            def agg_high(u, t):
                act.wait_ge(agg_f, t + 1)
                nc.scalar.activation(agg_hi[u], aggf[u], ACT.Copy).then_inc(agg_h, 1)

            def hidden_out(u, t):
                for g in range(HG):
                    wait_alone(act, up1_done, 2 * t + g + 1, act_tick)
                    nc.scalar.activation(hpre[:, ds(g * TOK + t * T, T)], bank[2 + 2 * u + g][:, :], ACT.Identity,
                                         bias=vec[:, g:g + 1], scale=1.0 / WSCALE).then_inc(up1_out, 1)

            xn_high(0)
            xn_high(1)
            act.wait_ge(dinv_in_psum, 1)
            for h in range(2):
                nc.scalar.activation(dinvrow[:, h * T:(h + 1) * T], bank[6 + h][:, :], ACT.Copy).then_inc(act_s, 1)
            agg_high(0, 0)

            def aggregated(b):
                agg_high(1, 2 * b + 1)
                hidden_out(0, 2 * b)
                agg_high(0, 2 * b + 2)
                hidden_out(1, 2 * b + 1)
            aggregated(0)
            with act.Fori(1, BATCH - 1) as b:
                xn_high(b + 1)
                aggregated(b)
            agg_high(1, NT - 1)
            hidden_out(0, NT - 2)
            hidden_out(1, NT - 1)

            act.wait_ge(bn_ready, 1)

            def relu(u, t):
                wait_alone(act, c_lo, t + 1, act_tick)
                for g in range(HG):
                    nc.scalar.activation(hr[u][:, g * T:(g + 1) * T], hpre[:, ds(g * TOK + t * T, T)], ACT.Relu,
                                         bias=bnc[:, g:g + 1], scale=bna[:, g:g + 1]).then_inc(c_relu, 1)

            def second_out(u, t):
                wait_alone(act, c_mm, t + 1 + RING, act_tick)
                nc.scalar.activation(out2[:, ds(t * T, T)], bank[u][:, :], ACT.Identity,
                                     bias=vec[:, 6:7], scale=1.0 / WSCALE).then_inc(c_out, 1)
            relu(0, 0)
            relu(1, 1)
            with act.Fori(0, NT // 2 - 1) as i:
                for u in range(2):
                    relu(u, 2 * i + u + 2)
                    second_out(u, 2 * i + u)
            second_out(0, NT - 2)
            second_out(1, NT - 1)

            act.wait_ge(bn_ready, 2)
            with act.Fori(0, NT // 4) as q:
                for k in range(4):
                    wait_alone(act, y_t, 4 * q + k + 1, act_tick)
                    nc.scalar.activation(ybuf[k % 2], out2[:, ds((4 * q + k) * T, T)], ACT.Identity,
                                         bias=bnc[:, HG:HG + 1], scale=bna[:, HG:HG + 1]).then_inc(y_done, 1)

            def rows_high(b_, t):
                wait_alone(act, row_t, t + 1, act_tick)
                nc.scalar.activation(xt_hi[:, ds(t * T, T)], b_[:, :], ACT.Copy).then_inc(xt_h, 1)

            def exponentials(s):
                act.wait_ge(exp_in, s + 1)
                nc.scalar.activation(rt[3], rt[2], ACT.Exp).then_inc(exp_done, 1)

            with act.Fori(0, HT // 2) as i:
                for u in range(2):
                    rows_high(bank[2 + u], 2 * i + u)
            exponentials(0)

            def gelu_shared(u, t, c):
                act.wait_ge(up_done, FC * t + c + 1)
                act.wait_ge(lo_done, FC * t + c + 1)
                nc.scalar.activation(h32[:, c * T:(c + 1) * T], bank[c][:, :], ACT.Gelu,
                                     bias=vec[:, VEC["b1s"][0] + c:VEC["b1s"][0] + c + 1], scale=1.0 / WSCALE)
                nc.scalar.activation(h_hi[u][:, c * T:(c + 1) * T], bank[c][:, :], ACT.Gelu,
                                     bias=vec[:, VEC["b1s"][0] + c:VEC["b1s"][0] + c + 1],
                                     scale=1.0 / WSCALE).then_inc(gelu_done, 1)

            def gelus_shared(u, t):
                act.wait_ge(down_done, t + 1)
                for c in range(FC):
                    gelu_shared(u, t, c)

            gelus_shared(0, 0)
            with act.Fori(0, HT // 2) as i:
                for u in range(2):
                    rows_high(bank[6], HT + 2 * i + u)
                    gelus_shared(1 - u, 2 * i + u + 1)
            gelus_shared(1, HT + 1)
            exponentials(1)
            with act.Fori(HT // 2 + 1, NT // 2) as i:
                for u in range(2):
                    gelus_shared(u, 2 * i + u)

            def row_high(u, g):
                act.wait_ge(xr_t, g + 1)
                nc.scalar.activation(xr_hi[u], bank[6 + u][:, 0:TR], ACT.Copy).then_inc(xr_h, 1)

            experts = Experts(act, tile_e)

            def gelu_routed(g, number):
                e = experts.of(number)
                for c in range(FC):
                    act.wait_ge(up_done, NSH + FC * g + c + 1)
                    wait_alone(act, lo_done, NSH + FC * g + c + 1, act_tick)
                    nc.scalar.activation(h32[:, c * TR:(c + 1) * TR], bank[c][:, 0:TR], ACT.Gelu,
                                         bias=vec[:, ds(e * FC + VEC["b1p"][0] + c, 1)],
                                         scale=1.0 / WSCALE).then_inc(gelu_done, 1)
            def weighted_out(u, g, free):
                if free is not None:
                    wait_alone(act, returned[u], free, act_tick)
                wait_alone(act, down_done, NT + g + 1 + RING, act_tick)
                for j in range(RB):
                    ins = nc.scalar.activation(yr[u][:, j * D:(j + 1) * D], bank[4 + u][:, j * D:(j + 1) * D], ACT.Copy,
                                               scale=tails[:, ds(g * RB * 2 + 2 * j + 1, 1)])
                ins.then_inc(y_out, 1)

            act.wait_ge(lo_done, NSH + FC)
            row_high(0, 0)
            row_high(1, 1)
            act.wait_ge(route_ready, HALVES)
            experts.fetch_first()
            gelu_routed(0, 0)

            def act_pair(i, free):
                experts.fetch(2 * i + 3)
                for u in range(2):
                    g = 2 * i + u
                    row_high(u, g + 2)
                    gelu_routed(g + 1, u + 1)
                    weighted_out(u, g, free)
                experts.shift()
            act_pair(0, None)
            with act.Fori(1, NR // 2 - 1) as i:
                act_pair(i, 16 * RB * i)
            gelu_routed(NR - 1, 1)
            weighted_out(0, NR - 2, 16 * RB * (NR // 2 - 1))
            weighted_out(1, NR - 1, 16 * RB * (NR // 2 - 1))

        @block.vector
        def _(v):
            count = [0]

            def link(ins, base=None):
                count[0] += 1
                ins.then_inc(dve, 1)
                v.wait_ge(dve, count[0] if base is None else base + count[0])

            tt, ts, stt = nc.vector.tensor_tensor, nc.vector.tensor_scalar, nc.vector.scalar_tensor_tensor

            v.sem_inc(lo_done, FC)
            for ring in (c_lo, x2_done, xt_l, lg_out, ffn_out, xr_l):
                v.sem_inc(ring, RING)

            v.wait_ge(prep_hi, 3)
            stt(w1t_lo[:, :], bank[6][:, 0:H], WSCALE, w1t_hi[:, :], ALU.mult, ALU.subtract)
            stt(w2t_lo[:, :], bank[6][:, H:2 * H], WSCALE, w2t_hi[:, :], ALU.mult, ALU.subtract).then_inc(prep_ready, 1)

            def at_low(c):
                lov = at_lo.rearrange("p (m n) -> p m n", m=CH)
                hiv = at_hi.rearrange("p (m n) -> p m n", m=CH)
                for h in range(2):
                    v.wait_ge(at_hi_done, 2 * c + h + 1)
                    tt(lov[:, 4 * h:4 * h + 4, c * P:(c + 1) * P],
                       bank[2 * (c % 2) + h][:, :].rearrange("p (m n) -> p m n", m=4),
                       hiv[:, 4 * h:4 * h + 4, c * P:(c + 1) * P], ALU.subtract).then_inc(at_lo_done, 1)

            def variance(b0, n, base=None):
                sv = st[:, :].rearrange("p (b s) -> p b s", s=6)[:, b0:b0 + n, :]
                w = slice(b0, b0 + n)
                tt(msum[:, w], sv[:, :, 1], sv[:, :, 4], ALU.add)
                tt(sm2[:, w], sv[:, :, 2], sv[:, :, 5], ALU.add)
                link(tt(sdiff[:, w], sv[:, :, 1], sv[:, :, 4], ALU.subtract), base)
                ts(mean[:, w], msum[:, w], 0.5, None, ALU.mult)
                link(stt(sdiff[:, w], sdiff[:, w], D / 4.0, sdiff[:, w], ALU.mult, ALU.mult), base)
                link(tt(sm2[:, w], sm2[:, w], sdiff[:, w], ALU.add), base)
                ts(sm2[:, w], sm2[:, w], 1.0 / D, EPS, ALU.mult, ALU.add).then_inc(pow_in, 1)

            def norm_stats(b):
                v.wait_ge(x_loaded[b], 16)
                for n in range(b * CH, (b + 1) * CH):
                    ins = nc.vector.bn_stats(st[:, 6 * n:6 * n + 6], xres[:, n * D:(n + 1) * D])
                return ins

            v.wait_ge(pool_made, 3)
            for c in range(CH):
                dblk = adjn[:, c * NODES + c * P:c * NODES + (c + 1) * P]
                v.wait_ge(adj_loaded[c], 16)
                tt(dblk, dblk, ident[:, :], ALU.add).then_inc(adj_eye, 1)
                v.wait_ge(adj_eye, c + 1)
                link(stt(junkd, dblk, 1.0, ident[:, :], ALU.mult, ALU.mult, accum_out=diag[:, c:c + 1]))
                if c:
                    at_low(c - 1)
                if c >= CH - 2:
                    ins = norm_stats(c - CH + 2)
            link(ins)
            variance(0, XGROUPS[0][1] * CH)
            at_low(CH - 1)
            v.wait_ge(rowsum_done, CH)
            v.wait_ge(colsum_done, 1)
            for c in range(CH):
                ins = stt(diagd[:, c * P:(c + 1) * P], bank[4 + c // 4][:, c % 4 * P:(c % 4 + 1) * P], 1.0, ident[:, :],
                          ALU.mult, ALU.mult, accum_out=csum[:, c:c + 1])
            link(ins)
            link(tt(rsum[:, :], rsum[:, :], csum[:, :], ALU.add))
            tt(diag[:, :], rsum[:, :], diag[:, :], ALU.subtract).then_inc(pow_in, 1)

            def group_stats(n):
                b0, b1 = XGROUPS[n]
                for b in range(b0, b1):
                    ins = norm_stats(b)
                link(ins)
                variance(b0 * CH, (b1 - b0) * CH)

            def normalise(b):
                v.wait_ge(pool_pow, b + 2)
                r = rstd[:, ds(b * CH, CH)]
                tt(r, r, dinv[:, :], ALU.mult).then_inc(scale_in, 1)
                v.wait_ge(scale_in, b + 1)
                for j in range(CH):
                    n = b * CH + j
                    ins = ts(xnf[:, j * D:(j + 1) * D], xres[:, ds(n * D, D)], mean[:, ds(n, 1)], rstd[:, ds(n, 1)],
                             ALU.subtract, ALU.mult)
                ins.then_inc(xn_f, 1)

            def normalised_low(b):
                v.wait_ge(xn_h, b + 1)
                tt(xn_lo[:, ds(b * NODES, NODES)], xnf, xn_hi[:, ds(b * NODES, NODES)], ALU.subtract).then_inc(xn_l, 1)

            def agg_low(u, t, wait_free):
                v.wait_ge(agg_done, t + 1)
                if wait_free:
                    v.wait_ge(up1_done, 2 * t - 2)
                tt(aggf[u], bank[u][:, :], dinvrow[:, u * T:(u + 1) * T], ALU.mult).then_inc(agg_f, 1)
                v.wait_ge(agg_h, t + 1)
                tt(agg_lo[u], aggf[u], agg_hi[u], ALU.subtract).then_inc(agg_l, 1)

            def hidden_stats(t):
                v.wait_ge(up1_out, 2 * t + 2)
                for g in range(HG):
                    ins = nc.vector.bn_stats(st_bn[:, ds((g * NT + t) * 6, 6)], hpre[:, ds(g * TOK + t * T, T)])
                return ins

            normalise(0)
            normalised_low(0)
            for c in range(CH):
                ins = ts(diagd[:, c * P:(c + 1) * P], ident[:, :], dinv[:, c:c + 1], None, ALU.mult)
            ins.then_inc(diagd_done, 1)
            normalise(1)
            normalised_low(1)
            group_stats(1)
            v.wait_ge(act_s, 2)
            agg_low(0, 0, False)
            agg_low(1, 1, False)
            group_stats(2)
            hidden_stats(0)
            agg_low(0, 2, True)
            with v.Fori(1, BATCH - 1) as b:
                normalise(b + 1)
                hidden_stats(2 * b - 1)
                normalised_low(b + 1)
                agg_low(1, 2 * b + 1, True)
                hidden_stats(2 * b)
                agg_low(0, 2 * b + 2, True)
            hidden_stats(NT - 3)
            agg_low(1, NT - 1, True)
            hidden_stats(NT - 2)
            link(hidden_stats(NT - 1))

            for g in range(HG):
                link(nc.vector.bn_aggr(bnm[:, 2 * g:2 * g + 2], st_bn[:, g * NT * 6:(g + 1) * NT * 6]))
            ts(bnv[:, 0:HG], bnm[:, 1:2 * HG:2], EPS, None, ALU.add).then_inc(pow_in, 1)
            v.wait_ge(pool_pow, BATCH + 2)
            link(tt(bna[:, 0:HG], bna[:, 0:HG], vec[:, 2:2 + HG], ALU.mult))
            link(tt(bnc[:, 0:HG], bnm[:, 0:2 * HG:2], bna[:, 0:HG], ALU.mult))
            tt(bnc[:, 0:HG], vec[:, 4:4 + HG], bnc[:, 0:HG], ALU.subtract).then_inc(bn_ready, 1)

            def c_low(u, t):
                v.wait_ge(c_relu, 2 * t + 2)
                v.wait_ge(c_mm, t + 1)
                nc.vector.tensor_copy(hr_hi[u], hr[u]).then_inc(c_hi, 1)
                v.wait_ge(c_hi, t + 1)
                tt(hr_lo[u], hr[u], hr_hi[u], ALU.subtract).then_inc(c_lo, 1)

            def c_stats(t):
                v.wait_ge(c_out, t + 1 + RING)
                return nc.vector.bn_stats(st_bn[:, ds(t * 6, 6)], out2[:, ds(t * T, T)])
            c_low(0, 0)
            c_low(1, 1)
            with v.Fori(0, NT // 2 - 1) as i:
                for u in range(2):
                    c_low(u, 2 * i + u + 2)
                    c_stats(2 * i + u)
            c_stats(NT - 2)
            link(c_stats(NT - 1))
            link(nc.vector.bn_aggr(bnm[:, 0:2], st_bn[:, 0:NT * 6]))
            ts(bnv[:, HG:HG + 1], bnm[:, 1:2], EPS, None, ALU.add).then_inc(pow_in, 1)
            v.wait_ge(pool_pow, BATCH + 3)
            link(tt(bna[:, HG:HG + 1], bna[:, HG:HG + 1], vec[:, 7:8], ALU.mult))
            link(tt(bnc[:, HG:HG + 1], bnm[:, 0:1], bna[:, HG:HG + 1], ALU.mult))
            tt(bnc[:, HG:HG + 1], vec[:, 8:9], bnc[:, HG:HG + 1], ALU.subtract).then_inc(bn_ready, 1)

            def add_x(u, t):
                v.wait_ge(y_t, t + 1 + RING)
                tile = xres[:, ds(t * T, T)]
                tt(tile, tile, bank[u][:, :], ALU.add).then_inc(x2_done, 1)

            def x2_stats(t):
                v.wait_ge(x2_done, t + 1 + RING)
                for j in range(BT):
                    ins = nc.vector.bn_stats(st[:, ds((t * BT + j) * 6, 6)], xres[:, ds(t * T + j * D, D)])
                ins.then_inc(stats_done, 1)

            v.wait_ge(late_loaded, 32)
            link(ts(wr_hi[:, :], wr_sb[:, :], WSCALE, None, ALU.mult))
            stt(wr_lo[:, :], wr_sb[:, :], WSCALE, wr_hi[:, :], ALU.mult, ALU.subtract).then_inc(wr_cut, 1)
            add_x(0, 0)
            for q in range(4):
                with v.Fori(2 * q, 2 * q + 1) as i:
                    for u in range(2):
                        add_x(1 - u, 2 * i + u + 1)
                        x2_stats(2 * i + u)
                t = 4 * q + 2
                add_x(1, t + 1)
                x2_stats(t)
                if q < 3:
                    add_x(0, t + 2)
                x2_stats(t + 1)
                v.wait_ge(stats_done, 4 * (q + 1))
                variance(q * BLK // 4, BLK // 4)

            def rows_out(s, t, tl):
                for j in range(BT):
                    n = t * BT + j
                    ins = ts(pay[s][:, ds((tl * BT + j) * ROW, D)], xres[:, ds(n * D, D)], mean[:, ds(n, 1)], rstd[:, ds(n, 1)],
                             ALU.subtract, ALU.mult)
                ins.then_inc(row_done, 1)

            def rows_low(b_, t):
                v.wait_ge(xt_h, t + 1)
                tt(xt_lo[:, ds(t * T, T)], b_[:, :], xt_hi[:, ds(t * T, T)], ALU.subtract).then_inc(xt_l, 1)

            def logits_out(b_, t, tl):
                v.wait_ge(lg_done, t + 1 + RING)
                ts(rt[0][:, ds(tl * BT * E, BT * E)], b_[:, 0:BT * E], 1.0 / WSCALE, None, ALU.mult).then_inc(lg_out, 1)

            def eb(ap):
                return ap.rearrange("p (b o) -> p b o", o=1).broadcast_to((P, HB, E))

            def be(ap):
                return ap.rearrange("p (o e) -> p o e", o=1).broadcast_to((P, HB, E))

            def three(ap):
                return ap.rearrange("p (b e) -> p b e", e=E)

            reduce = nc.vector.tensor_reduce

            L, Z, X, EX = rt[0], rt[1], rt[2], rt[3]
            oh1, oh2 = rt[4], rt[5]
            m1, f1, m2, f2, S, t1, t2, t3 = [rt[15][:, 32 * n:32 * n + HB] for n in range(8)]
            L3 = three(L)

            def choose(s):
                v.wait_ge(lg_out, s * HT + HT + RING)
                link(reduce(m1, L3, AX.X, ALU.max))
                tt(three(X), L3, eb(m1), ALU.subtract).then_inc(exp_in, 1)
                link(tt(three(Z), L3, eb(m1), ALU.is_equal))
                link(tt(three(Z), three(Z), be(desc8[:, :]), ALU.mult))
                link(reduce(f1, three(Z), AX.X, ALU.max))
                link(tt(three(oh1), three(Z), eb(f1), ALU.is_equal))
                link(stt(L, oh1, -BIG, L, ALU.mult, ALU.add))
                link(reduce(m2, L3, AX.X, ALU.max))
                link(tt(three(Z), L3, eb(m2), ALU.is_equal))
                link(tt(three(Z), three(Z), be(desc8[:, :]), ALU.mult))
                link(reduce(f2, three(Z), AX.X, ALU.max))
                link(tt(three(oh2), three(Z), eb(f2), ALU.is_equal))
                oh16 = rt[6].bitcast(f16)[:, 0:HB * E]
                tt(oh16, oh1, oh2, ALU.add).then_inc(oh_ready, 1)

            def weigh(s):
                v.wait_ge(exp_done, s + 1)
                link(reduce(S, three(EX), AX.X, ALU.add))
                link(nc.vector.reciprocal(S, S))
                link(tt(three(EX), three(EX), eb(S), ALU.mult))
                tt(rt[8], EX, oh1, ALU.mult)
                link(tt(rt[9], EX, oh2, ALU.mult))
                reduce(t1, three(rt[8]), AX.X, ALU.add)
                link(reduce(t2, three(rt[9]), AX.X, ALU.add))
                link(tt(t3, t1, t2, ALU.add))
                link(nc.vector.reciprocal(t3, t3))
                pv = pay[s].rearrange("p (b n) -> p b n", n=ROW)
                sv = second[s][:, :].rearrange("p (b n) -> p b n", n=2)
                stt(pv[:, :, D + 1], t1, 1.0 / WSCALE, t3, ALU.mult, ALU.mult)
                stt(sv[:, :, 1], t2, 1.0 / WSCALE, t3, ALU.mult, ALU.mult)
                nc.vector.tensor_copy(pv[:, :, D].bitcast(i32), ids[:, s * HB:(s + 1) * HB])
                ts(sv[:, :, 0].bitcast(i32), ids[:, s * HB:(s + 1) * HB], float(TOK), None, ALU.add)

            rank, total = bank[6][:, 0:HB * E], bank[7][:, 0:HB * E]
            incl = rt[10]
            inc3 = incl.rearrange("p (e b) -> p b e", e=E)
            padded, ends, base = small[0], small[1], small[2]

            def bases(s):
                v.wait_ge(rank_done, s + 1)
                nc.vector.tensor_copy(rt[11].rearrange("p (e b) -> p b e", e=E), three(total))
                link(nc.vector.tensor_copy(rt[12], total))
                for e in range(E):
                    ins = nc.vector.tensor_tensor_scan(incl[:, e * HB:(e + 1) * HB], ones_hb[:, :], rt[11][:, e * HB:(e + 1) * HB],
                                                       0.0, ALU.mult, ALU.add)
                link(ins)
                sh = TR.bit_length() - 1
                link(ts(small_i[:, :], incl.rearrange("p (e b) -> p e b", e=E)[:, :, HB - 1], float(TR - 1), None, ALU.add))
                link(ts(small_i[:, :], small_i[:, :], sh, sh, ALU.logical_shift_right, ALU.logical_shift_left))
                link(nc.vector.tensor_copy(padded[:, :], small_i[:, :]))
                link(nc.vector.tensor_tensor_scan(ends[:, :], ones_hb[:, 0:E], padded[:, :], 0.0, ALU.mult, ALU.add))
                link(stt(base[:, :], ends[:, :], float(s * TILES * TR), padded[:, :], ALU.add, ALU.subtract))

            def place(s):
                link(tt(three(rt[12]), inc3, three(rt[12]), ALU.subtract))
                link(tt(rt[12], rt[12], rank, ALU.add))
                link(tt(three(rt[12]), three(rt[12]), be(base[:, :]), ALU.add))
                tt(rt[8], rt[12], oh1, ALU.mult)
                link(tt(rt[9], rt[12], oh2, ALU.mult))
                reduce(t1, three(rt[8]), AX.X, ALU.add)
                link(reduce(t2, three(rt[9]), AX.X, ALU.add))
                nc.vector.tensor_copy(idx[0][:, s * HB:(s + 1) * HB], t1)
                nc.vector.tensor_copy(idx[1][:, s * HB:(s + 1) * HB], t2)
                cmp = wprep[:, 256 * 13:256 * 13 + TILES * E].rearrange("p (k e) -> p k e", e=E)
                link(tt(cmp, tile_at[:, :].rearrange("p (k o) -> p k o", o=1).broadcast_to((P, TILES, E)),
                        ends[:, :].rearrange("p (o e) -> p o e", o=1).broadcast_to((P, TILES, E)), ALU.is_ge))
                tf = tile_f[:, :]
                link(reduce(tf, cmp, AX.X, ALU.add))
                link(ts(tf, tf, float(E - 1), None, ALU.min))
                nc.vector.tensor_copy(tile_e[:, s * TILES:(s + 1) * TILES], tf).then_inc(route_ready, 1)

            v.wait_ge(pool_pow, BATCH + 5)
            v.wait_ge(pool_made, 9)
            v.wait_ge(w_kept[0], 16 * (1 + E // 2))
            v.wait_ge(w_kept[1], 16 * (E // 2))
            rows_out(0, 0, 0)
            rows_out(0, 1, 1)
            rows_low(bank[2], 0)
            with v.Fori(0, HT // 2 - 1) as i:
                for u in range(2):
                    t = 2 * i + u
                    rows_out(0, t + 2, t + 2)
                    rows_low(bank[3 - u], t + 1)
                    logits_out(bank[4 + u], t, t)
            rows_low(bank[3], HT - 1)
            logits_out(bank[4], HT - 2, HT - 2)
            logits_out(bank[5], HT - 1, HT - 1)
            choose(0)
            weigh(0)
            bases(0)
            place(0)

            def shared_low(u, t, c):
                v.wait_ge(gelu_done, FC * (t + 1) + c + 1)
                tt(h_lo[u][:, c * T:(c + 1) * T], h32[:, c * T:(c + 1) * T], h_hi[u][:, c * T:(c + 1) * T],
                   ALU.subtract).then_inc(lo_done, 1)

            def shared_out(u, t):
                tile = xres[:, ds(t * T, T)]
                tv = tile.rearrange("p (j d) -> p j d", j=BT)
                tt(tv, tv, b2s_rep[:, :].rearrange("p (o d) -> p o d", o=1).broadcast_to((P, BT, D)), ALU.add).then_inc(bias_in, 1)
                v.wait_ge(bias_in, t + 1)
                v.wait_ge(down_done, t + 1 + RING)
                stt(tile, bank[4 + u][:, :], 1.0 / WSCALE, tile, ALU.mult, ALU.add).then_inc(ffn_out, 1)

            def shared_step(u, t):
                for c in range(FC):
                    shared_low(1 - u, t + 1, c)
                shared_out(u, t)

            def both_step(u, t, more):
                rows_low(bank[6], HT + t)
                if more:
                    rows_out(1, HT + t + 1, t + 1)
                for c in range(FC):
                    shared_low(1 - u, t + 1, c)
                logits_out(bank[7], HT + t, t)
                shared_out(u, t)

            v.wait_ge(pool_pow, BATCH + 7)
            rows_out(1, HT, 0)
            for c in range(FC):
                shared_low(0, 0, c)
            with v.Fori(0, HT // 2 - 1) as i:
                for u in range(2):
                    both_step(u, 2 * i + u, True)
            both_step(0, HT - 2, True)
            both_step(1, HT - 1, False)
            choose(1)
            shared_step(0, HT)
            weigh(1)
            shared_step(1, HT + 1)
            bases(1)
            shared_step(0, HT + 2)
            place(1)
            shared_step(1, HT + 3)
            v.wait_ge(b2p_loaded, 16)
            link(ts(b2p_raw, b2p_raw, -WSCALE, None, ALU.mult))
            link(nc.vector.tensor_copy(b2p_hi, b2p_raw))
            stt(b2p_cut, b2p_hi, ident[0:2, 1:2], b2p_raw, ALU.mult, ALU.subtract).then_inc(bias_cut, 1)
            with v.Fori(HT // 2 + 2, NT // 2 - 1) as i:
                for u in range(2):
                    shared_step(u, 2 * i + u)
            shared_step(0, NT - 2)

            def row_low(u, g, turn):
                v.wait_ge(xr_loaded[u], 16 * turn)
                xv = xr[u].rearrange("p (j n) -> p j n", j=RB)
                nc.vector.tensor_copy(tails[:, ds(g * RB * 2, RB * 2)].rearrange("p (j n) -> p j n", j=RB),
                                      xv[:, :, D:ROW]).then_inc(tails_read, 1)
                v.wait_ge(xr_h, g + 1)
                tt(xr_lo[u], bank[6 + u][:, 0:TR], xr_hi[u], ALU.subtract).then_inc(xr_l, 1)

            def routed_cut(u, g):
                halves = [slice(c * TR, (c + 2) * TR) for c in range(0, FC, 2)]
                v.wait_ge(down_done, NT + g + 1)
                for n, w in enumerate(halves):
                    v.wait_ge(gelu_done, NSH + FC * (g + 1) + 2 * n + 2)
                    nc.vector.tensor_copy(h_hi[u][:, w], h32[:, w]).then_inc(hi_r, 1)
                    v.wait_ge(hi_r, 2 * g + n + 1)
                    tt(h_lo[u][:, w], h32[:, w], h_hi[u][:, w], ALU.subtract).then_inc(lo_done, 2)

            def routed_dest(u, g, free):
                if free is not None:
                    v.wait_ge(returned[u], free)
                v.wait_ge(tails_read, g + 1)
                tg = tails[:, ds(g * RB * 2, RB * 2)].rearrange("p (j n) -> p j n", j=RB)
                nc.vector.tensor_copy(rdest[u], tg[:, :, 0].bitcast(i32)).then_inc(dest_in, 1)

            def combine(u, n, turn):
                v.wait_ge(y_loaded[u], 32 * turn)
                acc = xres[:, ds(n * GB * D, GB * D)]
                tt(acc, acc, yload[u][0], ALU.add).then_inc(y_used, 1)
                v.wait_ge(y_used, n + 1)
                tt(acc, acc, yload[u][1], ALU.add).then_inc(combined, 1)

            row_low(0, 0, 1)
            row_low(1, 1, 1)
            shared_out(1, NT - 1)
            routed_cut(0, 0)
            for g in range(2):
                row_low(g, g + 2, 2)
                routed_cut(1 - g, g + 1)
                routed_dest(g, g, None)

            def tiles_pair(i):
                for u in range(2):
                    g = 2 * i + u
                    row_low(u, g + 2, i + 2)
                    routed_cut(1 - u, g + 1)
                    routed_dest(u, g, 16 * RB * i)
            with v.Fori(1, SUM0) as i:
                tiles_pair(i)
            with v.Fori(0, GH // 2) as m:
                for w in range(2):
                    with v.Fori(0, STEP) as k:
                        tiles_pair(SUM0 + (2 * m + w) * STEP + k)
                    combine(w, 2 * m + w, m + 1)
            with v.Fori(SUM0 + GH * STEP, NR // 2 - 1) as i:
                tiles_pair(i)
            routed_cut(1, NR - 1)
            routed_dest(0, NR - 2, 16 * RB * (NR // 2 - 1))
            routed_dest(1, NR - 1, 16 * RB * (NR // 2 - 1))

            with v.Fori(GH // 2, GH) as i:
                for u in range(2):
                    combine(u, 2 * i + u, i + 1)

        @block.tensor
        def _(pe):
            mm, transpose = nc.tensor.matmul, nc.tensor.transpose
            for ring in (c_mm, y_t, lg_done, down_done):
                pe.sem_inc(ring, RING)

            def three_pass(o, l, r, start, stop, last_inc=None):
                (lh, ll), (rh, rl) = l, r
                mm(o, lh, rh, start=start, stop=False)
                mm(o, lh, rl, start=False, stop=False)
                return mm(o, ll, rh, start=False, stop=stop)

            pe.wait_ge(small_loaded, 16 * 10)
            pe.wait_ge(pool_made, 5)
            transpose(bank[7][:, 0:NVEC], vrows[0:NVEC, :], ident[0:NVEC, 0:NVEC])
            for g in range(HG):
                transpose(bank[6][:, g * P:(g + 1) * P], gw1[:, g * D:(g + 1) * D], ident[:, :])
                ins = transpose(bank[6][:, H + g * P:H + (g + 1) * P], gw2[:, g * P:(g + 1) * P], ident[:, :])
            ins.then_inc(prep_t, 1)

            for c in range(CH):
                pe.wait_ge(adj_eye, c + 1)
                if c >= 2:
                    pe.wait_ge(at_lo_done, 2 * c - 2)
                for h in range(2):
                    for m in range(4):
                        k = 4 * h + m
                        ins = transpose(bank[2 * (c % 2) + h][:, m * P:(m + 1) * P],
                                        adjn[:, c * NODES + k * P:c * NODES + (k + 1) * P], ident[:, :])
                    ins.then_inc(at_t, 1)
                for h in range(2):
                    ins = mm(bank[4 + h][:, :], onesf[:, :], adjn[:, c * NODES + h * T:c * NODES + (h + 1) * T],
                             start=(c == 0), stop=(c == CH - 1))
            ins.then_inc(colsum_done, 1)

            def aggregate(u, b, t, free):
                pe.wait_ge(xn_l, b + 1)
                if free is not None:
                    pe.wait_ge(agg_f, free)
                for m in range(CH):
                    l = (xn_hi[:, ds((b * CH + m) * D, D)], xn_lo[:, ds((b * CH + m) * D, D)])
                    w = slice(m * NODES + u * T, m * NODES + (u + 1) * T)
                    ins = three_pass(bank[u][:, :], l, (at_hi[:, w], at_lo[:, w]), m == 0, m == CH - 1)
                ins.then_inc(agg_done, 1)

            def first_product(u, t, free):
                pe.wait_ge(agg_l, t + 1)
                if free is not None:
                    pe.wait_ge(up1_out, free)
                for g in range(HG):
                    w = slice(g * P, (g + 1) * P)
                    three_pass(bank[2 + 2 * u + g][:, :], (w1t_hi[:, w], w1t_lo[:, w]), (agg_hi[u], agg_lo[u]),
                               True, True).then_inc(up1_done, 1)
            pe.wait_ge(at_lo_done, 2 * CH)
            aggregate(0, 0, 0, None)
            pe.wait_ge(diagd_done, 1)
            pe.wait_ge(prep_ready, 1)
            for h in range(2):
                ins = mm(bank[6 + h][:, :], onesf[:, :], diagd[:, h * T:(h + 1) * T], start=True, stop=True)
            ins.then_inc(dinv_in_psum, 1)
            aggregate(1, 0, 1, None)
            first_product(0, 0, None)
            aggregate(0, 1, 2, 1)
            first_product(1, 1, None)
            with pe.Fori(1, BATCH - 1) as b:
                aggregate(1, b, 2 * b + 1, 2 * b)
                first_product(0, 2 * b, 4 * b - 2)
                aggregate(0, b + 1, 2 * b + 2, 2 * b + 1)
                first_product(1, 2 * b + 1, 4 * b)
            aggregate(1, BATCH - 1, NT - 1, NT - 2)
            first_product(0, NT - 2, 2 * NT - 6)
            first_product(1, NT - 1, 2 * NT - 4)

            with pe.Fori(0, NT // 2) as i:
                for u in range(2):
                    t = 2 * i + u
                    pe.wait_ge(c_lo, t + 1 + RING)
                    pe.wait_ge(c_out, t + 1)
                    for g in range(HG):
                        w = slice(g * P, (g + 1) * P)
                        r = (hr_hi[u][:, g * T:(g + 1) * T], hr_lo[u][:, g * T:(g + 1) * T])
                        ins = three_pass(bank[u][:, :], (w2t_hi[:, w], w2t_lo[:, w]), r, g == 0, g == HG - 1)
                    ins.then_inc(c_mm, 1)

            with pe.Fori(0, NT // 2) as i:
                for u in range(2):
                    t = 2 * i + u
                    pe.wait_ge(y_done, t + 1)
                    pe.wait_ge(x2_done, t + 1)
                    for j in range(BT):
                        ins = transpose(bank[u][:, j * P:(j + 1) * P], ybuf[u][:, j * P:(j + 1) * P], ident[:, :])
                    ins.then_inc(y_t, 1)

            pe.wait_ge(wr_cut, 1)

            def rows_t(s, b_, tl, free):
                t = s * HT + tl
                pe.wait_ge(row_done, t + 1)
                pe.wait_ge(xt_l, free)
                for j in range(BT):
                    ins = transpose(b_[:, j * P:(j + 1) * P], pay[s][:, (tl * BT + j) * ROW:(tl * BT + j) * ROW + D], ident[:, :])
                ins.then_inc(row_t, 1)

            def logits(b_, t, free):
                pe.wait_ge(xt_l, t + 1 + RING)
                pe.wait_ge(lg_out, free)
                for j in range(BT):
                    w = slice(t * T + j * P, t * T + (j + 1) * P)
                    ins = three_pass(b_[:, j * E:(j + 1) * E], (xt_hi[:, w], xt_lo[:, w]),
                                     (wr_hi[:, :], wr_lo[:, :]), True, True)
                ins.then_inc(lg_done, 1)

            def ranks(s):
                pe.wait_ge(oh_ready, s + 1)
                oh16 = rt[6].bitcast(f16)[:, 0:HB * E]
                mm(bank[6][:, 0:HB * E], before16[:, :], oh16, start=True, stop=True)
                mm(bank[7][:, 0:HB * E], ones16[:, :], oh16, start=True, stop=True).then_inc(rank_done, 1)

            rows_t(0, bank[2], 0, 1)
            rows_t(0, bank[3], 1, 2)
            for t in range(HT):
                if 0 < t < HT - 1:
                    rows_t(0, bank[2 + (t + 1) % 2], t + 1, t + 2)
                logits(bank[4 + t % 2], t, t + 1)
            ranks(0)

            pe.wait_ge(wall_loaded, 16)
            SW = E * 2048

            def shared_up(t):
                for c in range(FC):
                    pe.wait_ge(gelu_done, FC * t + c + 1)
                    a, b_ = SW + W1S + c * P, SW + W1L + c * P
                    three_pass(bank[c][:, :], (wall[:, a:a + P], wall[:, b_:b_ + P]),
                               (xt_hi[:, ds(t * T, T)], xt_lo[:, ds(t * T, T)]), True, True).then_inc(up_done, 1)

            def shared_down(u, t):
                pe.wait_ge(lo_done, FC * (t + 2))
                pe.wait_ge(ffn_out, t + 1)
                for j in range(BT):
                    for c in range(FC):
                        l = tuple(h[:, c * T + j * P:c * T + (j + 1) * P] for h in (h_hi[u], h_lo[u]))
                        a, b_ = SW + W2S + c * D, SW + W2L + c * D
                        ins = three_pass(bank[4 + u][:, j * D:(j + 1) * D], l, (wall[:, a:a + D], wall[:, b_:b_ + D]),
                                         c == 0, c == FC - 1)
                ins.then_inc(down_done, 1)

            pe.wait_ge(x2_done, NT + RING)
            pe.wait_ge(xt_l, HT + RING)
            pe.wait_ge(lg_out, HT + RING)
            shared_up(0)
            pe.wait_ge(route_ready, 1)
            rows_t(1, bank[6], 0, 1)
            for t in range(HT):
                shared_up(t + 1)
                logits(bank[7], HT + t, HT + t + RING)
                shared_down(t % 2, t)
                if t + 1 < HT:
                    rows_t(1, bank[6], t + 1, HT + t + 1 + RING)
            shared_up(HT + 1)
            shared_down(0, HT)
            pe.wait_ge(lg_out, NT + RING)
            ranks(1)
            shared_up(HT + 2)
            shared_down(1, HT + 1)
            with pe.Fori(HT // 2 + 1, NT // 2 - 1) as i:
                for u in range(2):
                    shared_up(2 * i + u + 1)
                    shared_down(u, 2 * i + u)
            shared_up(NT - 1)

            def routed_t(u, g, turn):
                pe.wait_ge(xr_loaded[u], 16 * turn)
                pe.wait_ge(xr_l, g + 1)
                for j in range(RB):
                    ins = transpose(bank[6 + u][:, j * P:(j + 1) * P], xr[u][:, j * ROW:j * ROW + D], ident[:, :])
                ins.then_inc(xr_t, 1)


            def up_part(u, g, e, c):
                pe.wait_ge(gelu_done, NSH + FC * g + c + 1)
                l = (wall[:, ds(e * 2048 + W1S + c * P, P)], wall[:, ds(e * 2048 + W1L + c * P, P)])
                three_pass(bank[c][:, 0:TR], l, (xr_hi[u], xr_lo[u]), True, True).then_inc(up_done, 1)

            def down_part(u, e, j, c):
                if c == 0:
                    mm(bank[4 + u][:, j * D:(j + 1) * D], ones16[0:2, :], b2p_cut[:, ds(e * D, D)], start=True, stop=False)
                l = tuple(h[:, c * TR + j * P:c * TR + (j + 1) * P] for h in (h_hi[u], h_lo[u]))
                r = (wall[:, ds(e * 2048 + W2S + c * D, D)], wall[:, ds(e * 2048 + W2L + c * D, D)])
                return three_pass(bank[4 + u][:, j * D:(j + 1) * D], l, r, False, c == FC - 1)

            def routed_up(u, g, number):
                e = experts.of(number)
                pe.wait_ge(xr_l, g + 1 + RING)
                for c in range(FC):
                    up_part(u, g, e, c)

            def routed_down(u, g, number):
                e = experts.of(number)
                pe.wait_ge(lo_done, NSH + FC * (g + 2))
                pe.wait_ge(y_out, g + 1)
                for j in range(RB):
                    for c in range(FC):
                        ins = down_part(u, e, j, c)
                ins.then_inc(down_done, 1)

            def routed_both(u, g, number):
                e_up, e_down = experts.of(number + 1), experts.of(number)
                pe.wait_ge(xr_l, g + 2 + RING)
                for c in range(LEAD):
                    up_part(1 - u, g + 1, e_up, c)
                pe.wait_ge(lo_done, NSH + FC * (g + 2))
                pe.wait_ge(y_out, g + 1)
                for c in range(FC):
                    if c + LEAD < FC:
                        up_part(1 - u, g + 1, e_up, c + LEAD)
                    down_part(u, e_down, 0, c)
                for j in range(1, RB):
                    for c in range(FC):
                        ins = down_part(u, e_down, j, c)
                ins.then_inc(down_done, 1)

            pe.wait_ge(bias_cut, 1)
            experts = Experts(pe, tile_e)
            routed_t(0, 0, 1)
            routed_t(1, 1, 1)
            shared_down(0, NT - 2)
            experts.fetch_first()
            routed_up(0, 0, 0)
            shared_down(1, NT - 1)
            pe.wait_ge(ffn_out, NT + RING)
            with pe.Fori(0, NR // 2 - 1) as i:
                for u in range(2):
                    routed_t(u, 2 * i + u + 2, i + 2)
                    if u == 1:
                        experts.fetch(2 * i + 3)
                    routed_both(u, 2 * i + u, u)
                experts.shift()
            routed_up(1, NR - 1, 1)
            routed_down(0, NR - 2, 0)
            routed_down(1, NR - 1, 1)


INS = ["x", "adj"] + [f"L0_gnn_{n}" for n in ("W1", "b1", "g1", "be1", "W2", "b2", "g2", "be2")] + \
      [f"L0_ffn_{n}" for n in ("Wr", "W1s", "b1s", "W2s", "b2s", "W1p", "b1p", "W2p", "b2p")]


def kernel(**inputs):
    import numpy as np
    import concourse.bacc as bacc
    from concourse import mybir as _mybir
    from concourse.bass_utils import run_bass_kernel_spmd

    nc = bacc.Bacc("TRN2", target_bir_lowering=False, num_devices=1)
    arrays, args = {}, []
    for name in INS:
        a = np.ascontiguousarray(inputs[name])
        arrays[f"in_{name}"] = a
        args.append(nc.dram_tensor(f"in_{name}", a.shape, _mybir.dt.from_np(a.dtype), kind="ExternalInput").ap())
    out = nc.dram_tensor("result", (TOK, D), _mybir.dt.float32, kind="ExternalOutput").ap()
    build(nc, *args, out)
    r = run_bass_kernel_spmd(nc, [arrays], core_ids=[0])
    return r.results[0]["result"].reshape(BATCH, NODES, D)
```

```python
import concourse.bass as bass
from concourse import mybir
from contextlib import ExitStack

P = 128
D = 128
NODES = 1024
BATCH = 8
TOK = BATCH * NODES
CH = NODES // P
BLK = TOK // P
H = 256
HG = H // P
F = 512
FC = F // P
E = 8
T = 512
NT = TOK // T
BT = T // P
HALVES = 2
HB = BLK // HALVES
HT = NT // HALVES
TR = 256
RB = TR // P
GB = 4
YR = 4
GH = HB // GB
TILES = (2 * TOK // HALVES + E * (TR - 1)) // TR
NR = HALVES * TILES
STEP = 1
XGROUPS = ((0, 2), (2, 4), (4, 6), (6, BATCH))
LATE = 34
SUM0 = 24
ROW = D + 2
SKIP = 1 << 20
WSCALE = 256.0
EPS = 1e-5
BIG = 3.0e38

VEC = dict(b1=(0, HG), g1=(2, HG), be1=(4, HG), b2=(6, 1), g2=(7, 1), be2=(8, 1), b1s=(9, FC), b1p=(13, E * FC))
NVEC = 13 + E * FC


def build(nc, x, adj, W1, b1, g1, be1, W2, b2, g2, be2, Wr, W1s, b1s, W2s, b2s, W1p, b1p, W2p, b2p, out):
    f32, f16, i32 = mybir.dt.float32, mybir.dt.float16, mybir.dt.int32
    ALU = mybir.AluOpType
    ACT = mybir.ActivationFunctionType
    AX = mybir.AxisListType
    ds = bass.ds

    def wait_alone(engine, semaphore, value, tick):
        engine.wait_ge(semaphore, value)
        engine.sem_inc(tick, 1)

    class Experts:
        def __init__(self, engine, table):
            self.engine, self.table = engine, table
            self.regs = [engine.alloc_register(f"expert{n}") for n in range(3)]
            self.later = [engine.alloc_register(f"later{n}") for n in range(2)]

        def fetch_first(self):
            for n in range(3):
                self.engine.reg_load(self.regs[n], self.table[0:1, n:n + 1])

        def fetch(self, g):
            self.engine.load(self.later, self.table[0:1, ds(g, 2)])

        def shift(self):
            self.engine.reg_mov(self.regs[0], self.regs[2])
            for n in range(2):
                self.engine.reg_mov(self.regs[n + 1], self.later[n])

        def of(self, n):
            return self.engine.snap(self.regs[n], min_val=0, max_val=E - 1)

    ctx = ExitStack()
    with ctx:
        def sb(name, cols, dt=f32, parts=P):
            return ctx.enter_context(nc.sbuf_tensor(name, [parts, cols], dt))

        def sem(name):
            return ctx.enter_context(nc.semaphore(name))

        xres = sb("xres", BLK * D)
        region1 = sb("region1", 16384)
        region2 = sb("region2", 16384)
        misc = sb("misc", HB * ROW)
        wprep = sb("wprep", 4096)

        r1h = region1[:, :].bitcast(f16)
        at_hi, at_lo = r1h[:, 0:8192], r1h[:, 8192:16384]
        xn_hi, xn_lo = r1h[:, 16384:24576], r1h[:, 24576:32768]
        wall = r1h[:, 0:(E + 1) * 2048]
        pay0 = region1[:, 9216:9216 + HB * ROW]
        ybuf = [region1[:, 13440 + 512 * u:13952 + 512 * u] for u in range(2)]

        b2p_raw = region1[0:2, 13440:13440 + E * D]
        b2p_hi = region1[0:2, 14464:14464 + E * D // 2].bitcast(f16)
        b2p_cut = region1[0:2, 15488:15488 + E * D // 2].bitcast(f16)

        adjn = region2[:, 0:8192]
        hpre = region2
        out2 = region2[:, 0:8192]
        r2h = region2[:, 8192:16384].bitcast(f16)
        xt_hi, xt_lo = r2h[:, 0:8192], r2h[:, 8192:16384]
        h32 = region2[:, 0:FC * T]
        fh = region2[:, 2048:6144].bitcast(f16)
        h_hi = [fh[:, 4096 * u:4096 * u + 2048] for u in range(2)]
        h_lo = [fh[:, 4096 * u + 2048:4096 * u + 4096] for u in range(2)]
        xr = [region2[:, 6144 + 320 * u:6144 + 320 * u + RB * ROW] for u in range(2)]
        yr = [region2[:, 6784 + 256 * u:7040 + 256 * u] for u in range(2)]
        xrh = region2[:, 7296:7808].bitcast(f16)
        xr_hi = [xrh[:, 512 * u:512 * u + 256] for u in range(2)]
        xr_lo = [xrh[:, 512 * u + 256:512 * u + 512] for u in range(2)]
        rdest = [region2[:, 7824 + 8 * u:7824 + 8 * u + RB].bitcast(i32) for u in range(2)]

        xnf = misc[:, 0:1024]
        aggf = [misc[:, 1024 + 512 * u:1536 + 512 * u] for u in range(2)]
        mh = misc[:, 2048:3072].bitcast(f16)
        agg_hi = [mh[:, 1024 * u:1024 * u + 512] for u in range(2)]
        agg_lo = [mh[:, 1024 * u + 512:1024 * u + 1024] for u in range(2)]
        dinvrow = misc[:, 3072:4096]
        diagd = misc[:, 1024:2048]
        junk = misc[:, 0:1024]
        junkd = misc[:, 2048:2176]
        hr = [misc[:, 1024 * u:1024 * u + 1024] for u in range(2)]
        mc = misc[:, 2048:4096].bitcast(f16)
        hr_hi = [mc[:, 2048 * u:2048 * u + 1024] for u in range(2)]
        hr_lo = [mc[:, 2048 * u + 1024:2048 * u + 2048] for u in range(2)]
        pay1 = misc[:, 0:HB * ROW]
        pay = [pay0, pay1]
        yload = [[misc[:, (2 * w + k) * GB * D:(2 * w + k + 1) * GB * D] for k in range(2)] for w in range(YR)]

        wraw = [wprep[:, 1024 * u:1024 * u + 1024] for u in range(2)]
        wph = wprep[:, 2048:4096].bitcast(f16)
        wcut = [wph[:, 2048 * u:2048 * u + 2048] for u in range(2)]
        rt = [wprep[:, 256 * n:256 * n + 256] for n in range(16)]

        ident = sb("ident_sb", P)
        onesf = sb("onesf", P)
        ones16 = sb("ones16", P, f16)
        before16 = sb("before16", P, f16)
        gw1 = sb("gw1", HG * D)
        gw2 = sb("gw2", H)
        w1t_hi, w1t_lo = sb("w1t_hi", H, f16), sb("w1t_lo", H, f16)
        w2t_hi, w2t_lo = sb("w2t_hi", H, f16), sb("w2t_lo", H, f16)
        vrows = sb("vrows", P)
        vec = sb("vec", NVEC)
        wr_sb = sb("wr_sb", E)
        wr_hi, wr_lo = sb("wr_hi", E, f16), sb("wr_lo", E, f16)
        b2s_raw = sb("b2s_raw", D, parts=2)
        b2s_cut, b2s_hi = (gw1[0:2, n * D // 2:(n + 1) * D // 2].bitcast(f16) for n in range(2))
        st = sb("st", BLK * 6)
        st_bn = sb("st_bn", HG * NT * 6)
        msum, rstd = sb("msum", BLK), sb("rstd", BLK)
        mean = sb("mean", BLK)
        ids = sb("ids", BLK, i32)
        tails = sb("tails", NR * RB * 2)
        second = [sb(f"second{s}", HB * 2) for s in range(HALVES)]
        sdiff, sm2 = sb("sdiff", BLK), sb("sm2", BLK)
        mhalf = sb("mhalf", BLK)
        csum = sb("csum", CH)
        rsum, diag, dinv = sb("rsum", CH), sb("diag", CH), sb("dinv", CH)
        bnm = sb("bnm", 2 * HG)
        bna, bnc = sb("bna", 4), sb("bnc", 4)
        bnv = sb("bnv", 4)
        desc8 = sb("desc8", E)
        tile_at = sb("tile_at", TILES)
        ones_hb = sb("ones_hb", HB)
        trash = sb("trash", RB * ROW)
        idx = [sb(f"idx{k}", BLK, i32) for k in range(2)]
        tile_f = sb("tile_f", TILES)
        tile_e = sb("tile_e", NR + 1, i32)
        small = [sb(f"small{n}", E) for n in range(4)]
        small_i = sb("small_i", E, i32)

        bank = [ctx.enter_context(nc.psum_tensor(f"bank{n}", [P, 512], f32)) for n in range(8)]

        wsc = nc.dram_tensor("weights_cut", (E + 1, P, 2048), f16, kind="Internal").ap()
        xs = nc.dram_tensor("rows_by_expert", (NR * TR, ROW), f32, kind="Internal").ap()
        ys = nc.dram_tensor("rows_by_token", (2 * TOK, D), f32, kind="Internal").ap()

        small_loaded = sem("small_loaded")
        late_loaded, b2p_loaded = sem("late_loaded"), sem("b2p_loaded")
        adj_loaded = [sem(f"adj_loaded{c}") for c in range(CH)]
        x_loaded = [sem(f"x_loaded{b}") for b in range(BATCH)]
        pool_made = sem("pool_made")
        pool_pow = sem("pool_pow")
        act_tick, pool_tick = sem("act_tick"), sem("pool_tick")
        pow_in = sem("pow_in")
        dve = sem("dve")
        act_s = sem("act_s")
        w_raw = [sem(f"w_raw{u}") for u in range(2)]
        w_cut = sem("w_cut")
        w_chain = sem("w_chain")
        w_kept = [sem(f"w_kept{u}") for u in range(2)]
        wall_loaded = sem("wall_loaded")
        trash_stored = sem("trash_stored")
        prep_t = sem("prep_t")
        prep_hi = sem("prep_hi")
        prep_ready = sem("prep_ready")
        adj_eye = sem("adj_eye")
        at_t, at_hi_done, at_lo_done = sem("at_t"), sem("at_hi_done"), sem("at_lo_done")
        colsum_done = sem("colsum_done")
        rowsum_done = sem("rowsum_done")
        diagd_done = sem("diagd_done")
        dinv_in_psum = sem("dinv_in_psum")
        xn_f, xn_h, xn_l = sem("xn_f"), sem("xn_h"), sem("xn_l")
        agg_done, agg_f, agg_h, agg_l = sem("agg_done"), sem("agg_f"), sem("agg_h"), sem("agg_l")
        up1_done, up1_out = sem("up1_done"), sem("up1_out")
        bn_ready, scale_in, wr_cut = sem("bn_ready"), sem("scale_in"), sem("wr_cut")
        c_relu, c_hi, c_lo, c_lo2, c_mm, c_out = (sem(n) for n in ("c_relu", "c_hi", "c_lo", "c_lo2", "c_mm", "c_out"))
        y_done, y_t, x2_done = sem("y_done"), sem("y_t"), sem("x2_done")
        row_done, row_t, xt_h, xt_l, lg_done, lg_out = (
            sem(n) for n in ("row_done", "row_t", "xt_h", "xt_l", "lg_done", "lg_out"))
        exp_in, exp_done = sem("exp_in"), sem("exp_done")
        oh_ready, rank_done, route_ready = sem("oh_ready"), sem("rank_done"), sem("route_ready")
        dispatched = [sem(f"dispatched{s}") for s in range(HALVES)]
        stats_done, ranks_out = sem("stats_done"), sem("ranks_out")
        tails_read, hi_r, bias_cut = sem("tails_read"), sem("hi_r"), sem("bias_cut")
        second_in, y_out, dest_in = sem("second_in"), sem("y_out"), sem("dest_in")
        up_done, gelu_done, lo_done, down_done, ffn_out = (
            sem(n) for n in ("up_done", "gelu_done", "lo_done", "down_done", "ffn_out"))
        xr_loaded = [sem(f"xr_loaded{u}") for u in range(2)]
        xr_t, xr_h, xr_l = sem("xr_t"), sem("xr_h"), sem("xr_l")
        returned = [sem(f"returned{u}") for u in range(2)]
        y_loaded = [sem(f"y_loaded{w}") for w in range(YR)]
        y_used = sem("y_used")
        combined = sem("combined")
        stored = sem("stored")

        RING = 2

        block = ctx.enter_context(nc.Block())
        W1S, W1L, W2S, W2L = 0, 512, 1024, 1536
        NSH = NT * FC

        @block.sync
        def _(sp):
            def rows(v, n, at):
                sp.dma_start(vrows[at:at + n, :], v).then_inc(small_loaded, 16)
            rows(b1.rearrange("(g p) -> g p", p=P), HG, VEC["b1"][0])
            rows(g1.rearrange("(g p) -> g p", p=P), HG, VEC["g1"][0])
            rows(be1.rearrange("(g p) -> g p", p=P), HG, VEC["be1"][0])
            rows(b2.rearrange("(g p) -> g p", p=P), 1, VEC["b2"][0])
            rows(g2.rearrange("(g p) -> g p", p=P), 1, VEC["g2"][0])
            rows(be2.rearrange("(g p) -> g p", p=P), 1, VEC["be2"][0])
            rows(b1s.rearrange("(g p) -> g p", p=P), FC, VEC["b1s"][0])
            rows(b1p.rearrange("e (g p) -> (e g) p", p=P), E * FC, VEC["b1p"][0])
            sp.dma_start(gw1[:, :].rearrange("p (g d) -> p g d", g=HG),
                         W1.rearrange("(g p) d -> p g d", p=P)).then_inc(small_loaded, 16)
            sp.dma_start(gw2[:, :], W2).then_inc(small_loaded, 16)
            def raw(u, w1, w2):
                sp.dma_start(wraw[u][:, 0:F], w1).then_inc(w_raw[u], 16)
                sp.dma_start(wraw[u][:, F:2 * F].rearrange("p (c d) -> p c d", c=FC), w2).then_inc(w_raw[u], 16)

            def raw_expert(u, e):
                raw(u, W1p[ds(e, 1), :, :].rearrange("o p f -> (o p) f"),
                    W2p[ds(e, 1), :, :].rearrange("o (c p) d -> p (o c) d", p=P))

            def keep(u, e):
                sp.dma_start(wsc[ds(e, 1), :, :].rearrange("o p n -> (o p) n"), wcut[u]).then_inc(w_kept[u], 16)

            for c in range(CH):
                sp.dma_start(adjn[:, c * NODES:(c + 1) * NODES], adj[c * P:(c + 1) * P, :]).then_inc(adj_loaded[c], 16)
                if c == 1:
                    raw(0, W1s, W2s.rearrange("(c p) d -> p c d", p=P))
                if c == 3:
                    raw_expert(1, 0)
            for b in range(BATCH):
                sp.dma_start(xres[:, b * NODES:(b + 1) * NODES].rearrange("p (c d) -> p c d", c=CH),
                             x[b].rearrange("(c p) d -> p c d", p=P)).then_inc(x_loaded[b], 16)
            sp.dma_start(wr_sb[:, :], Wr).then_inc(late_loaded, 16)
            sp.dma_start(b2s_raw[:, :], b2s.rearrange("(o d) -> o d", o=1).broadcast_to((2, D))).then_inc(late_loaded, 16)

            sp.wait_ge(w_cut, 1)
            keep(0, E)
            raw_expert(0, 1)
            sp.wait_ge(w_cut, 2)
            keep(1, 0)
            raw_expert(1, 2)
            with sp.Fori(1, E // 2 - 1) as i:
                for u in range(2):
                    n = 2 * i + u
                    sp.wait_ge(w_cut, n + 1)
                    keep(u, n - 1)
                    raw_expert(u, n + 1)
            for n in (E - 2, E - 1):
                sp.wait_ge(w_cut, n + 1)
                keep(n % 2, n - 1)
                if n == E - 2:
                    raw_expert(0, E - 1)
            sp.wait_ge(w_cut, E + 1)
            keep(0, E - 1)

            sp.wait_ge(pool_made, 8)
            with sp.Fori(0, NR) as k:
                sp.dma_start(xs[ds(k * TR, TR), :].rearrange("(j p) n -> p j n", p=P),
                             trash[:, :].rearrange("p (j n) -> p j n", j=RB)).then_inc(trash_stored, 16)

            sp.wait_ge(agg_done, NT)
            sp.wait_ge(w_kept[0], 16 * (1 + E // 2))
            sp.wait_ge(w_kept[1], 16 * (E // 2))
            sp.dma_start(wall.rearrange("p (e n) -> p e n", e=E + 1), wsc.rearrange("e p n -> p e n")).then_inc(wall_loaded, 16)

            def load_rows(u, g, use):
                sp.wait_ge(xr_t, use)
                sp.wait_ge(tails_read, use)
                sp.dma_start(xr[u].rearrange("p (j n) -> p j n", j=RB),
                             xs[ds(g * TR, TR), :].rearrange("(j p) n -> p j n", p=P)).then_inc(xr_loaded[u], 16)
            sp.wait_ge(x2_done, NT + RING)
            sp.dma_start(b2p_raw, b2p.rearrange("(o e) d -> o (e d)", o=1).broadcast_to((2, E * D))).then_inc(b2p_loaded, 16)
            sp.wait_ge(dispatched[0], 16 * 2 * HB)
            for g in range(2):
                sp.dma_start(xr[g].rearrange("p (j n) -> p j n", j=RB),
                             xs[g * TR:(g + 1) * TR, :].rearrange("(j p) n -> p j n", p=P)).then_inc(xr_loaded[g], 16)
            with sp.Fori(1, TILES // 2) as i:
                for u in range(2):
                    load_rows(u, 2 * i + u, 2 * i + u - 1)
            load_rows(0, TILES - 1, TILES - 2)
            sp.wait_ge(dispatched[1], 16 * 2 * HB)
            load_rows(1, TILES, TILES - 1)
            def load_y(u, n):
                for k in range(2):
                    sp.dma_start(yload[u][k].rearrange("p (b d) -> p b d", b=GB),
                                 ys[ds(k * TOK + n * GB * P, GB * P), :].rearrange("(b p) d -> p b d", p=P)).then_inc(y_loaded[u], 16)

            def store(n):
                sp.dma_start(out[ds(n * GB * P, GB * P), :].rearrange("(b p) d -> p b d", p=P),
                             xres[:, ds(n * GB * D, GB * D)].rearrange("p (b d) -> p b d", b=GB)).then_inc(stored, 16)

            def load_pairs(first, end):
                with sp.Fori(first, end) as i:
                    for u in range(2):
                        load_rows(u, 2 * i + u, 2 * i + u - 1)

            def sum_step(w, n):
                load_y(w, n)
                load_pairs(SUM0 + 1 + n * STEP, SUM0 + 1 + (n + 1) * STEP)

            def store_earlier(n):
                sp.wait_ge(combined, n)
                store(n - 1)
            load_pairs((TILES + 1) // 2, SUM0 + 1)
            sp.wait_ge(returned[0], 16 * RB * (TILES + 1) // 2)
            sp.wait_ge(returned[1], 16 * RB * (TILES // 2))
            for w in range(YR):
                sum_step(w, w)
                if w:
                    store_earlier(w)
            with sp.Fori(1, GH // YR) as m:
                for w in range(YR):
                    sum_step(w, YR * m + w)
                    store_earlier(YR * m + w)
            load_pairs(SUM0 + 1 + GH * STEP, NR // 2)
            store_earlier(GH)
            sp.wait_ge(returned[0], 16 * RB * NR // 2)
            sp.wait_ge(returned[1], 16 * RB * NR // 2)
            for w in range(YR):
                load_y(w, GH + w)
            with sp.Fori(GH // YR, 2 * GH // YR - 1) as m:
                for w in range(YR):
                    n = YR * m + w
                    sp.wait_ge(combined, n + 1)
                    load_y(w, n + YR)
                    store(n)
            for n in range(2 * GH - YR, 2 * GH):
                sp.wait_ge(combined, n + 1)
                store(n)
            sp.wait_ge(stored, 16 * (BLK // GB))
            sp.wait_ge(trash_stored, 16 * NR)

        @block.gpsimd
        def _(pool):
            pool.sem_inc(c_lo2, RING)
            pool.memset(ident[:, :], 0.0).then_inc(pool_made, 1)
            pool.memset(before16[:, :], 1.0).then_inc(pool_made, 1)
            pool.wait_ge(pool_made, 2)
            pool.affine_select(out=ident[:, :], in_=ident[:, :], compare_op=ALU.not_equal, fill=1.0,
                               base=0, pattern=[[-1, P]], channel_multiplier=1).then_inc(pool_made, 1)
            pool.affine_select(out=before16[:, :], in_=before16[:, :], compare_op=ALU.is_gt, fill=0.0,
                               base=0, pattern=[[1, P]], channel_multiplier=-1).then_inc(pool_made, 1)
            pool.memset(onesf[:, :], 1.0)
            pool.memset(ones16[:, :], 1.0)
            pool.memset(ones_hb[:, :], 1.0)
            pool.memset(mhalf[:, :], -0.5).then_inc(pool_made, 1)
            pool.iota(desc8[:, :], [[-1, E]], base=E, channel_multiplier=0, allow_small_or_imprecise_dtypes=True)
            pool.iota(tile_at[:, :], [[TR, TILES]], base=0, channel_multiplier=0,
                      allow_small_or_imprecise_dtypes=True).then_inc(pool_made, 1)
            pool.memset(tile_e[:, NR:NR + 1], 0)
            pool.memset(trash[:, :], 0.0).then_inc(pool_made, 1)
            pool.wait_ge(pool_made, 7)
            tv = trash[:, :].rearrange("p (j n) -> p j n", j=RB)
            pool.iota(tv[:, :, D:D + 1].bitcast(i32), [[P, RB], [0, 1]], base=SKIP, channel_multiplier=1).then_inc(pool_made, 1)

            def inverse_root(o, v, n, turn):
                pool.wait_ge(pow_in, turn)
                pool.tensor_tensor(o, v, mhalf[:, 0:n], ALU.pow).then_inc(pool_pow, 1)

            pool.iota(ids[:, :], [[P, BLK]], base=0, channel_multiplier=1).then_inc(pool_made, 1)

            def cut(u, n, turn):
                v = wraw[u].rearrange("p (w f) -> p w f", w=2)
                parts = wcut[u].rearrange("p (w s f) -> p w s f", w=2, s=2)
                wait_alone(pool, w_raw[u], 32 * (turn + 1), pool_tick)
                pool.tensor_scalar(v, v, WSCALE, None, ALU.mult).then_inc(w_chain, 1)
                if not (isinstance(turn, int) and turn == 0):
                    pool.wait_ge(w_kept[u], 16 * turn)
                wait_alone(pool, w_chain, 2 * n + 1, pool_tick)
                pool.tensor_copy(parts[:, :, 0, :], v).then_inc(w_chain, 1)
                pool.wait_ge(w_chain, 2 * n + 2)
                pool.tensor_tensor(parts[:, :, 1, :], v, parts[:, :, 0, :], ALU.subtract).then_inc(w_cut, 1)

            def group_roots(g):
                for b in range(*XGROUPS[g]):
                    inverse_root(rstd[:, b * CH:(b + 1) * CH], sm2[:, b * CH:(b + 1) * CH], CH, 2 + g)

            cut(0, 0, 0)
            cut(1, 1, 0)
            inverse_root(rstd[:, 0:CH], sm2[:, 0:CH], CH, 1)
            inverse_root(dinv[:, :], diag[:, :], CH, 2)
            inverse_root(rstd[:, CH:2 * CH], sm2[:, CH:2 * CH], CH, 1)
            group_roots(1)
            cut(0, 2, 1)
            group_roots(2)
            cut(1, 3, 1)
            group_roots(3)
            with pool.Fori(2, E // 2) as i:
                for u in range(2):
                    cut(u, 2 * i + u, i)
            cut(0, E, E // 2)

            inverse_root(bna[:, 0:HG], bnv[:, 0:HG], HG, 6)
            with pool.Fori(0, NT // 2) as i:
                for u in range(2):
                    pool.wait_ge(c_hi, 2 * i + u + 1)
                    pool.tensor_tensor(hr_lo[u][:, T:], hr[u][:, T:], hr_hi[u][:, T:], ALU.subtract).then_inc(c_lo2, 1)
            inverse_root(bna[:, HG:HG + 1], bnv[:, HG:HG + 1], 1, 7)
            for s in range(HALVES):
                inverse_root(rstd[:, s * HB:(s + 1) * HB], sm2[:, s * HB:(s + 1) * HB], HB, 8 + s)

            pool.wait_ge(trash_stored, 16 * NR)
            def dispatch(s, k, n):
                blk = s * HB + n
                pool.indirect_dma_start(xs, bass.IndirectOffsetOnAxis(idx[k][:, blk:blk + 1], 0),
                                        pay[s][:, n * ROW:(n + 1) * ROW], None).then_inc(dispatched[s], 16)

            def second_tails(s):
                pool.wait_ge(dispatched[s], 16 * HB)
                pv = pay[s].rearrange("p (b n) -> p b n", n=ROW)
                pool.tensor_copy(pv[:, :, D:ROW], second[s][:, :].rearrange("p (b n) -> p b n", n=2)).then_inc(second_in, 1)
                pool.wait_ge(second_in, s + 1)

            def give_back(u, g):
                wait_alone(pool, y_out, g + 1 + RING, pool_tick)
                wait_alone(pool, dest_in, g + 1, pool_tick)
                for j in range(RB):
                    pool.indirect_dma_start(ys, bass.IndirectOffsetOnAxis(rdest[u][:, j:j + 1], 0),
                                            yr[u][:, j * D:(j + 1) * D], None,
                                            bounds_check=2 * TOK - 1, oob_is_err=False).then_inc(returned[u], 16)

            pool.wait_ge(route_ready, 1)
            for n in range(HB):
                dispatch(0, 0, n)
            second_tails(0)
            for n in range(HB):
                dispatch(0, 1, n)
            pool.wait_ge(route_ready, 2)
            for n in range(2 * HB - LATE):
                dispatch(1, 0, n)
            for g in range(LATE):
                give_back(g % 2, g)
                n = 2 * HB - LATE + g
                if n == HB:
                    second_tails(1)
                dispatch(1, n // HB, n % HB)
            def backs_pair(i):
                for u in range(2):
                    give_back(u, 2 * i + u)

            with pool.Fori(LATE // 2, SUM0) as i:
                backs_pair(i)
            pool.wait_ge(ffn_out, NT + RING)
            with pool.Fori(0, GH // YR) as m:
                for w in range(YR):
                    n = YR * m + w
                    wait_alone(pool, y_loaded[w], 32 * (m + 1), pool_tick)
                    acc = xres[:, ds(n * GB * D, GB * D)]
                    pool.tensor_tensor(acc, acc, yload[w][0], ALU.add).then_inc(y_used, 1)
                    with pool.Fori(0, STEP) as k:
                        backs_pair(SUM0 + (YR * m + w) * STEP + k)
            with pool.Fori(SUM0 + GH * STEP, NR // 2) as i:
                backs_pair(i)

        @block.scalar
        def _(act):
            act.sem_inc(c_out, RING)
            act.sem_inc(gelu_done, FC)
            act.sem_inc(y_out, RING)
            act.wait_ge(prep_t, 1)
            nc.scalar.activation(vec[:, :], bank[7][:, 0:NVEC], ACT.Copy).then_inc(prep_hi, 1)
            nc.scalar.activation(w1t_hi[:, :], bank[6][:, 0:H], ACT.Copy, scale=WSCALE).then_inc(prep_hi, 1)
            nc.scalar.activation(w2t_hi[:, :], bank[6][:, H:2 * H], ACT.Copy, scale=WSCALE).then_inc(prep_hi, 1)

            atv = at_hi.rearrange("p (m n) -> p m n", m=CH)
            for c in range(CH):
                act.wait_ge(adj_eye, c + 1)
                if c:
                    act.wait_ge(rowsum_done, c)
                nc.scalar.activation(junk, adjn[:, c * NODES:(c + 1) * NODES], ACT.Copy,
                                     accum_out=rsum[:, c:c + 1]).then_inc(rowsum_done, 1)
                for h in range(2):
                    act.wait_ge(at_t, 2 * c + h + 1)
                    nc.scalar.activation(atv[:, 4 * h:4 * h + 4, c * P:(c + 1) * P],
                                         bank[2 * (c % 2) + h][:, :].rearrange("p (m n) -> p m n", m=4),
                                         ACT.Copy).then_inc(at_hi_done, 1)
            def xn_high(b):
                wait_alone(act, xn_f, b + 1, act_tick)
                nc.scalar.activation(xn_hi[:, ds(b * NODES, NODES)], xnf, ACT.Copy).then_inc(xn_h, 1)

            def agg_high(u, t):
                act.wait_ge(agg_f, t + 1)
                nc.scalar.activation(agg_hi[u], aggf[u], ACT.Copy).then_inc(agg_h, 1)

            def hidden_out(u, t):
                for g in range(HG):
                    wait_alone(act, up1_done, 2 * t + g + 1, act_tick)
                    nc.scalar.activation(hpre[:, ds(g * TOK + t * T, T)], bank[2 + 2 * u + g][:, :], ACT.Identity,
                                         bias=vec[:, g:g + 1], scale=1.0 / WSCALE).then_inc(up1_out, 1)

            xn_high(0)
            xn_high(1)
            act.wait_ge(dinv_in_psum, 1)
            for h in range(2):
                nc.scalar.activation(dinvrow[:, h * T:(h + 1) * T], bank[6 + h][:, :], ACT.Copy).then_inc(act_s, 1)
            agg_high(0, 0)

            def aggregated(b, more=True):
                agg_high(1, 2 * b + 1)
                hidden_out(0, 2 * b)
                if more:
                    xn_high(b + 2)
                agg_high(0, 2 * b + 2)
                hidden_out(1, 2 * b + 1)
            with act.Fori(0, BATCH - 2) as b:
                aggregated(b)
            aggregated(BATCH - 2, False)
            agg_high(1, NT - 1)
            hidden_out(0, NT - 2)
            hidden_out(1, NT - 1)

            act.wait_ge(bn_ready, 1)

            def relu(u, t):
                wait_alone(act, c_lo, t + 1, act_tick)
                wait_alone(act, c_lo2, t + 1, act_tick)
                for g in range(HG):
                    nc.scalar.activation(hr[u][:, g * T:(g + 1) * T], hpre[:, ds(g * TOK + t * T, T)], ACT.Relu,
                                         bias=bnc[:, g:g + 1], scale=bna[:, g:g + 1]).then_inc(c_relu, 1)

            def second_out(u, t):
                wait_alone(act, c_mm, t + 1 + RING, act_tick)
                nc.scalar.activation(out2[:, ds(t * T, T)], bank[u][:, :], ACT.Identity,
                                     bias=vec[:, 6:7], scale=1.0 / WSCALE).then_inc(c_out, 1)
            relu(0, 0)
            relu(1, 1)
            with act.Fori(0, NT // 2 - 1) as i:
                for u in range(2):
                    relu(u, 2 * i + u + 2)
                    second_out(u, 2 * i + u)
            second_out(0, NT - 2)
            second_out(1, NT - 1)

            act.wait_ge(bn_ready, 2)
            with act.Fori(0, NT // 4) as q:
                for k in range(4):
                    wait_alone(act, y_t, 4 * q + k + 1, act_tick)
                    nc.scalar.activation(ybuf[k % 2], out2[:, ds((4 * q + k) * T, T)], ACT.Identity,
                                         bias=bnc[:, HG:HG + 1], scale=bna[:, HG:HG + 1]).then_inc(y_done, 1)

            def rows_high(b_, t):
                wait_alone(act, row_t, t + 1, act_tick)
                nc.scalar.activation(xt_hi[:, ds(t * T, T)], b_[:, :], ACT.Copy).then_inc(xt_h, 1)

            def exponentials(s):
                act.wait_ge(exp_in, s + 1)
                nc.scalar.activation(rt[3], rt[2], ACT.Exp).then_inc(exp_done, 1)

            with act.Fori(0, HT // 2) as i:
                for u in range(2):
                    rows_high(bank[2 + u], 2 * i + u)
            exponentials(0)

            def gelu_shared(u, t, c):
                act.wait_ge(up_done, FC * t + c + 1)
                act.wait_ge(lo_done, FC * t + c + 1)
                nc.scalar.activation(h32[:, c * T:(c + 1) * T], bank[c][:, :], ACT.Gelu,
                                     bias=vec[:, VEC["b1s"][0] + c:VEC["b1s"][0] + c + 1], scale=1.0 / WSCALE)
                nc.scalar.activation(h_hi[u][:, c * T:(c + 1) * T], bank[c][:, :], ACT.Gelu,
                                     bias=vec[:, VEC["b1s"][0] + c:VEC["b1s"][0] + c + 1],
                                     scale=1.0 / WSCALE).then_inc(gelu_done, 1)

            def gelus_shared(u, t):
                act.wait_ge(down_done, t + 1)
                for c in range(FC):
                    gelu_shared(u, t, c)

            gelus_shared(0, 0)
            with act.Fori(0, HT // 2) as i:
                for u in range(2):
                    rows_high(bank[6], HT + 2 * i + u)
                    gelus_shared(1 - u, 2 * i + u + 1)
            gelus_shared(1, HT + 1)
            exponentials(1)
            with act.Fori(HT // 2 + 1, NT // 2) as i:
                for u in range(2):
                    gelus_shared(u, 2 * i + u)

            def row_high(u, g):
                act.wait_ge(xr_t, g + 1)
                nc.scalar.activation(xr_hi[u], bank[6 + u][:, 0:TR], ACT.Copy).then_inc(xr_h, 1)

            experts = Experts(act, tile_e)

            def gelu_routed(g, number, chunks=range(FC)):
                e = experts.of(number)
                for c in chunks:
                    act.wait_ge(up_done, NSH + FC * g + c + 1)
                    wait_alone(act, lo_done, NSH + FC * g + c + 1, act_tick)
                    nc.scalar.activation(h32[:, c * TR:(c + 1) * TR], bank[c][:, 0:TR], ACT.Gelu,
                                         bias=vec[:, ds(e * FC + VEC["b1p"][0] + c, 1)],
                                         scale=1.0 / WSCALE).then_inc(gelu_done, 1)
            def weighted_out(u, g, free):
                if free is not None:
                    wait_alone(act, returned[u], free, act_tick)
                wait_alone(act, down_done, NT + g + 1 + RING, act_tick)
                for j in range(RB):
                    ins = nc.scalar.activation(yr[u][:, j * D:(j + 1) * D], bank[4 + u][:, j * D:(j + 1) * D], ACT.Copy,
                                               scale=tails[:, ds(g * RB * 2 + 2 * j + 1, 1)])
                ins.then_inc(y_out, 1)

            act.wait_ge(lo_done, NSH + FC)
            row_high(0, 0)
            row_high(1, 1)
            act.wait_ge(route_ready, HALVES)
            experts.fetch_first()
            gelu_routed(0, 0)

            def act_pair(i, first=False):
                experts.fetch(2 * i + 3)
                for u in range(2):
                    g = 2 * i + u
                    row_high(u, g + 2)
                    gelu_routed(g + 1, u + 1, (0, 1))
                    if first:
                        if u == 1:
                            weighted_out(0, 0, None)
                    else:
                        turn = i - 1 + u
                        weighted_out(1 - u, g - 1, None if isinstance(turn, int) and turn == 0 else 16 * RB * turn)
                    gelu_routed(g + 1, u + 1, (2, 3))
                experts.shift()
            act_pair(0, first=True)
            act_pair(1)
            with act.Fori(2, NR // 2 - 1) as i:
                act_pair(i)
            last = NR // 2 - 1
            weighted_out(1, NR - 3, 16 * RB * (last - 1))
            gelu_routed(NR - 1, 1)
            weighted_out(0, NR - 2, 16 * RB * last)
            weighted_out(1, NR - 1, 16 * RB * last)

        @block.vector
        def _(v):
            count = [0]

            def link(ins, base=None):
                count[0] += 1
                ins.then_inc(dve, 1)
                v.wait_ge(dve, count[0] if base is None else base + count[0])

            tt, ts, stt = nc.vector.tensor_tensor, nc.vector.tensor_scalar, nc.vector.scalar_tensor_tensor

            v.sem_inc(lo_done, FC)
            for ring in (c_lo, x2_done, xt_l, lg_out, ffn_out, xr_l):
                v.sem_inc(ring, RING)

            v.wait_ge(prep_hi, 3)
            stt(w1t_lo[:, :], bank[6][:, 0:H], WSCALE, w1t_hi[:, :], ALU.mult, ALU.subtract)
            stt(w2t_lo[:, :], bank[6][:, H:2 * H], WSCALE, w2t_hi[:, :], ALU.mult, ALU.subtract).then_inc(prep_ready, 1)

            def at_low(c):
                lov = at_lo.rearrange("p (m n) -> p m n", m=CH)
                hiv = at_hi.rearrange("p (m n) -> p m n", m=CH)
                for h in range(2):
                    v.wait_ge(at_hi_done, 2 * c + h + 1)
                    tt(lov[:, 4 * h:4 * h + 4, c * P:(c + 1) * P],
                       bank[2 * (c % 2) + h][:, :].rearrange("p (m n) -> p m n", m=4),
                       hiv[:, 4 * h:4 * h + 4, c * P:(c + 1) * P], ALU.subtract).then_inc(at_lo_done, 1)

            def variance(b0, n, base=None):
                sv = st[:, :].rearrange("p (b s) -> p b s", s=6)[:, b0:b0 + n, :]
                w = slice(b0, b0 + n)
                tt(msum[:, w], sv[:, :, 1], sv[:, :, 4], ALU.add)
                tt(sm2[:, w], sv[:, :, 2], sv[:, :, 5], ALU.add)
                link(tt(sdiff[:, w], sv[:, :, 1], sv[:, :, 4], ALU.subtract), base)
                ts(mean[:, w], msum[:, w], 0.5, None, ALU.mult)
                link(stt(sdiff[:, w], sdiff[:, w], D / 4.0, sdiff[:, w], ALU.mult, ALU.mult), base)
                link(tt(sm2[:, w], sm2[:, w], sdiff[:, w], ALU.add), base)
                ts(sm2[:, w], sm2[:, w], 1.0 / D, EPS, ALU.mult, ALU.add).then_inc(pow_in, 1)

            def norm_stats(b):
                v.wait_ge(x_loaded[b], 16)
                for n in range(b * CH, (b + 1) * CH):
                    ins = nc.vector.bn_stats(st[:, 6 * n:6 * n + 6], xres[:, n * D:(n + 1) * D])
                return ins

            v.wait_ge(pool_made, 3)
            for c in range(CH):
                dblk = adjn[:, c * NODES + c * P:c * NODES + (c + 1) * P]
                v.wait_ge(adj_loaded[c], 16)
                tt(dblk, dblk, ident[:, :], ALU.add).then_inc(adj_eye, 1)
                v.wait_ge(adj_eye, c + 1)
                link(stt(junkd, dblk, 1.0, ident[:, :], ALU.mult, ALU.mult, accum_out=diag[:, c:c + 1]))
                if c:
                    at_low(c - 1)
                if c >= CH - 2:
                    ins = norm_stats(c - CH + 2)
            link(ins)
            variance(0, XGROUPS[0][1] * CH)
            at_low(CH - 1)
            v.wait_ge(rowsum_done, CH)
            v.wait_ge(colsum_done, 1)
            for c in range(CH):
                ins = stt(diagd[:, c * P:(c + 1) * P], bank[4 + c // 4][:, c % 4 * P:(c % 4 + 1) * P], 1.0, ident[:, :],
                          ALU.mult, ALU.mult, accum_out=csum[:, c:c + 1])
            link(ins)
            link(tt(rsum[:, :], rsum[:, :], csum[:, :], ALU.add))
            tt(diag[:, :], rsum[:, :], diag[:, :], ALU.subtract).then_inc(pow_in, 1)

            def group_stats(n):
                b0, b1 = XGROUPS[n]
                for b in range(b0, b1):
                    ins = norm_stats(b)
                link(ins)
                variance(b0 * CH, (b1 - b0) * CH)

            def normalise(b):
                v.wait_ge(pool_pow, b + 2)
                r = rstd[:, ds(b * CH, CH)]
                tt(r, r, dinv[:, :], ALU.mult).then_inc(scale_in, 1)
                v.wait_ge(scale_in, b + 1)
                for j in range(CH):
                    n = b * CH + j
                    ins = ts(xnf[:, j * D:(j + 1) * D], xres[:, ds(n * D, D)], mean[:, ds(n, 1)], rstd[:, ds(n, 1)],
                             ALU.subtract, ALU.mult)
                ins.then_inc(xn_f, 1)

            def normalised_low(b):
                v.wait_ge(xn_h, b + 1)
                tt(xn_lo[:, ds(b * NODES, NODES)], xnf, xn_hi[:, ds(b * NODES, NODES)], ALU.subtract).then_inc(xn_l, 1)

            def agg_low(u, t, wait_free):
                v.wait_ge(agg_done, t + 1)
                if wait_free:
                    v.wait_ge(up1_done, 2 * t - 2)
                tt(aggf[u], bank[u][:, :], dinvrow[:, u * T:(u + 1) * T], ALU.mult).then_inc(agg_f, 1)
                v.wait_ge(agg_h, t + 1)
                tt(agg_lo[u], aggf[u], agg_hi[u], ALU.subtract).then_inc(agg_l, 1)

            def hidden_stats(t):
                v.wait_ge(up1_out, 2 * t + 2)
                for g in range(HG):
                    ins = nc.vector.bn_stats(st_bn[:, ds((g * NT + t) * 6, 6)], hpre[:, ds(g * TOK + t * T, T)])
                return ins

            normalise(0)
            normalised_low(0)
            for c in range(CH):
                ins = ts(diagd[:, c * P:(c + 1) * P], ident[:, :], dinv[:, c:c + 1], None, ALU.mult)
            ins.then_inc(diagd_done, 1)
            normalise(1)
            normalised_low(1)
            group_stats(1)
            v.wait_ge(act_s, 2)
            agg_low(0, 0, False)
            agg_low(1, 1, False)
            normalise(2)
            normalised_low(2)
            group_stats(2)
            hidden_stats(0)
            agg_low(0, 2, True)
            group_stats(3)

            def aggregated(b, more=True):
                hidden_stats(2 * b - 1)
                agg_low(1, 2 * b + 1, True)
                if more:
                    normalise(b + 2)
                hidden_stats(2 * b)
                if more:
                    normalised_low(b + 2)
                agg_low(0, 2 * b + 2, True)
            with v.Fori(1, BATCH - 2) as b:
                aggregated(b)
            aggregated(BATCH - 2, False)
            hidden_stats(NT - 3)
            agg_low(1, NT - 1, True)
            hidden_stats(NT - 2)
            link(hidden_stats(NT - 1))

            for g in range(HG):
                link(nc.vector.bn_aggr(bnm[:, 2 * g:2 * g + 2], st_bn[:, g * NT * 6:(g + 1) * NT * 6]))
            ts(bnv[:, 0:HG], bnm[:, 1:2 * HG:2], EPS, None, ALU.add).then_inc(pow_in, 1)
            v.wait_ge(pool_pow, BATCH + 2)
            link(tt(bna[:, 0:HG], bna[:, 0:HG], vec[:, 2:2 + HG], ALU.mult))
            link(tt(bnc[:, 0:HG], bnm[:, 0:2 * HG:2], bna[:, 0:HG], ALU.mult))
            tt(bnc[:, 0:HG], vec[:, 4:4 + HG], bnc[:, 0:HG], ALU.subtract).then_inc(bn_ready, 1)

            def c_low(u, t):
                v.wait_ge(c_relu, 2 * t + 2)
                v.wait_ge(c_mm, t + 1)
                nc.vector.tensor_copy(hr_hi[u], hr[u]).then_inc(c_hi, 1)
                v.wait_ge(c_hi, t + 1)
                tt(hr_lo[u][:, 0:T], hr[u][:, 0:T], hr_hi[u][:, 0:T], ALU.subtract).then_inc(c_lo, 1)

            def c_stats(t):
                v.wait_ge(c_out, t + 1 + RING)
                return nc.vector.bn_stats(st_bn[:, ds(t * 6, 6)], out2[:, ds(t * T, T)])
            c_low(0, 0)
            c_low(1, 1)
            with v.Fori(0, NT // 2 - 1) as i:
                for u in range(2):
                    c_low(u, 2 * i + u + 2)
                    c_stats(2 * i + u)
            c_stats(NT - 2)
            link(c_stats(NT - 1))
            link(nc.vector.bn_aggr(bnm[:, 0:2], st_bn[:, 0:NT * 6]))
            ts(bnv[:, HG:HG + 1], bnm[:, 1:2], EPS, None, ALU.add).then_inc(pow_in, 1)
            v.wait_ge(pool_pow, BATCH + 3)
            link(tt(bna[:, HG:HG + 1], bna[:, HG:HG + 1], vec[:, 7:8], ALU.mult))
            link(tt(bnc[:, HG:HG + 1], bnm[:, 0:1], bna[:, HG:HG + 1], ALU.mult))
            tt(bnc[:, HG:HG + 1], vec[:, 8:9], bnc[:, HG:HG + 1], ALU.subtract).then_inc(bn_ready, 1)

            def add_x(u, t):
                v.wait_ge(y_t, t + 1 + RING)
                tile = xres[:, ds(t * T, T)]
                tt(tile, tile, bank[u][:, :], ALU.add).then_inc(x2_done, 1)

            def x2_stats(t):
                v.wait_ge(x2_done, t + 1 + RING)
                for j in range(BT):
                    ins = nc.vector.bn_stats(st[:, ds((t * BT + j) * 6, 6)], xres[:, ds(t * T + j * D, D)])
                ins.then_inc(stats_done, 1)

            v.wait_ge(late_loaded, 32)
            link(ts(wr_hi[:, :], wr_sb[:, :], WSCALE, None, ALU.mult))
            stt(wr_lo[:, :], wr_sb[:, :], WSCALE, wr_hi[:, :], ALU.mult, ALU.subtract)

            def cut_bias(raw, hi, parts):
                link(ts(raw, raw, -WSCALE, None, ALU.mult))
                link(nc.vector.tensor_copy(hi, raw))
                return stt(parts, hi, ident[0:2, 1:2], raw, ALU.mult, ALU.subtract)

            cut_bias(b2s_raw[:, :], b2s_hi, b2s_cut).then_inc(wr_cut, 1)
            add_x(0, 0)
            for t in range(NT):
                if t + 1 < NT:
                    add_x((t + 1) % 2, t + 1)
                x2_stats(t)
                if t % HT == HT - 1:
                    v.wait_ge(stats_done, t + 1)
                    variance((t - HT + 1) * BT, HB)

            def rows_out(s, t, tl):
                for j in range(BT):
                    n = t * BT + j
                    ins = ts(pay[s][:, ds((tl * BT + j) * ROW, D)], xres[:, ds(n * D, D)], mean[:, ds(n, 1)], rstd[:, ds(n, 1)],
                             ALU.subtract, ALU.mult)
                ins.then_inc(row_done, 1)

            def rows_low(b_, t):
                v.wait_ge(xt_h, t + 1)
                tt(xt_lo[:, ds(t * T, T)], b_[:, :], xt_hi[:, ds(t * T, T)], ALU.subtract).then_inc(xt_l, 1)

            def logits_out(b_, t, tl):
                v.wait_ge(lg_done, t + 1 + RING)
                ts(rt[0][:, ds(tl * BT * E, BT * E)], b_[:, 0:BT * E], 1.0 / WSCALE, None, ALU.mult).then_inc(lg_out, 1)

            def eb(ap):
                return ap.rearrange("p (b o) -> p b o", o=1).broadcast_to((P, HB, E))

            def be(ap):
                return ap.rearrange("p (o e) -> p o e", o=1).broadcast_to((P, HB, E))

            def three(ap):
                return ap.rearrange("p (b e) -> p b e", e=E)

            reduce = nc.vector.tensor_reduce

            L, Z, X, EX = rt[0], rt[1], rt[2], rt[3]
            oh1, oh2 = rt[4], rt[5]
            m1, f1, m2, f2, S, t1, t2, t3 = [rt[15][:, 32 * n:32 * n + HB] for n in range(8)]
            L3 = three(L)

            def choose(s):
                v.wait_ge(lg_out, s * HT + HT + RING)
                link(reduce(m1, L3, AX.X, ALU.max))
                tt(three(X), L3, eb(m1), ALU.subtract).then_inc(exp_in, 1)
                link(tt(three(Z), L3, eb(m1), ALU.is_equal))
                link(tt(three(Z), three(Z), be(desc8[:, :]), ALU.mult))
                link(reduce(f1, three(Z), AX.X, ALU.max))
                link(tt(three(oh1), three(Z), eb(f1), ALU.is_equal))
                link(stt(L, oh1, -BIG, L, ALU.mult, ALU.add))
                link(reduce(m2, L3, AX.X, ALU.max))
                link(tt(three(Z), L3, eb(m2), ALU.is_equal))
                link(tt(three(Z), three(Z), be(desc8[:, :]), ALU.mult))
                link(reduce(f2, three(Z), AX.X, ALU.max))
                link(tt(three(oh2), three(Z), eb(f2), ALU.is_equal))
                oh16 = rt[6].bitcast(f16)[:, 0:HB * E]
                tt(oh16, oh1, oh2, ALU.add).then_inc(oh_ready, 1)

            def weigh(s):
                v.wait_ge(exp_done, s + 1)
                link(reduce(S, three(EX), AX.X, ALU.add))
                link(nc.vector.reciprocal(S, S))
                link(tt(three(EX), three(EX), eb(S), ALU.mult))
                tt(rt[8], EX, oh1, ALU.mult)
                link(tt(rt[9], EX, oh2, ALU.mult))
                reduce(t1, three(rt[8]), AX.X, ALU.add)
                link(reduce(t2, three(rt[9]), AX.X, ALU.add))
                link(tt(t3, t1, t2, ALU.add))
                link(nc.vector.reciprocal(t3, t3))
                pv = pay[s].rearrange("p (b n) -> p b n", n=ROW)
                sv = second[s][:, :].rearrange("p (b n) -> p b n", n=2)
                stt(pv[:, :, D + 1], t1, 1.0 / WSCALE, t3, ALU.mult, ALU.mult)
                stt(sv[:, :, 1], t2, 1.0 / WSCALE, t3, ALU.mult, ALU.mult)
                nc.vector.tensor_copy(pv[:, :, D].bitcast(i32), ids[:, s * HB:(s + 1) * HB])
                ts(sv[:, :, 0].bitcast(i32), ids[:, s * HB:(s + 1) * HB], float(TOK), None, ALU.add)

            rank, total = bank[6][:, 0:HB * E], bank[7][:, 0:HB * E]
            incl = rt[10]
            inc3 = incl.rearrange("p (e b) -> p b e", e=E)
            padded, ends, base = small[0], small[1], small[2]

            def take_ranks(s):
                v.wait_ge(rank_done, s + 1)
                nc.vector.tensor_copy(rt[11].rearrange("p (e b) -> p b e", e=E), three(total))
                nc.vector.tensor_copy(rt[12], total)
                nc.vector.tensor_copy(rt[7], rank).then_inc(ranks_out, 1)

            def bases(s):
                v.wait_ge(ranks_out, s + 1)
                for e in range(E):
                    ins = nc.vector.tensor_tensor_scan(incl[:, e * HB:(e + 1) * HB], ones_hb[:, :], rt[11][:, e * HB:(e + 1) * HB],
                                                       0.0, ALU.mult, ALU.add)
                link(ins)
                sh = TR.bit_length() - 1
                link(ts(small_i[:, :], incl.rearrange("p (e b) -> p e b", e=E)[:, :, HB - 1], float(TR - 1), None, ALU.add))
                link(ts(small_i[:, :], small_i[:, :], sh, sh, ALU.logical_shift_right, ALU.logical_shift_left))
                link(nc.vector.tensor_copy(padded[:, :], small_i[:, :]))
                link(nc.vector.tensor_tensor_scan(ends[:, :], ones_hb[:, 0:E], padded[:, :], 0.0, ALU.mult, ALU.add))
                link(stt(base[:, :], ends[:, :], float(s * TILES * TR), padded[:, :], ALU.add, ALU.subtract))

            def place(s):
                link(tt(three(rt[12]), inc3, three(rt[12]), ALU.subtract))
                link(tt(rt[12], rt[12], rt[7], ALU.add))
                link(tt(three(rt[12]), three(rt[12]), be(base[:, :]), ALU.add))
                tt(rt[8], rt[12], oh1, ALU.mult)
                link(tt(rt[9], rt[12], oh2, ALU.mult))
                reduce(t1, three(rt[8]), AX.X, ALU.add)
                link(reduce(t2, three(rt[9]), AX.X, ALU.add))
                nc.vector.tensor_copy(idx[0][:, s * HB:(s + 1) * HB], t1)
                nc.vector.tensor_copy(idx[1][:, s * HB:(s + 1) * HB], t2)
                cmp = wprep[:, 256 * 13:256 * 13 + TILES * E].rearrange("p (k e) -> p k e", e=E)
                link(tt(cmp, tile_at[:, :].rearrange("p (k o) -> p k o", o=1).broadcast_to((P, TILES, E)),
                        ends[:, :].rearrange("p (o e) -> p o e", o=1).broadcast_to((P, TILES, E)), ALU.is_ge))
                tf = tile_f[:, :]
                link(reduce(tf, cmp, AX.X, ALU.add))
                link(ts(tf, tf, float(E - 1), None, ALU.min))
                nc.vector.tensor_copy(tile_e[:, s * TILES:(s + 1) * TILES], tf).then_inc(route_ready, 1)

            v.wait_ge(pool_pow, BATCH + 4)
            v.wait_ge(pool_made, 9)
            v.wait_ge(w_kept[0], 16 * (1 + E // 2))
            v.wait_ge(w_kept[1], 16 * (E // 2))
            rows_out(0, 0, 0)
            rows_out(0, 1, 1)
            rows_low(bank[2], 0)
            for t in range(HT - 2):
                rows_out(0, t + 2, t + 2)
                rows_low(bank[2 + (t + 1) % 2], t + 1)
                logits_out(bank[4 + t % 2], t, t)
            rows_low(bank[3], HT - 1)
            logits_out(bank[4], HT - 2, HT - 2)
            logits_out(bank[5], HT - 1, HT - 1)
            choose(0)
            take_ranks(0)

            def shared_low(u, t, c):
                v.wait_ge(gelu_done, FC * (t + 1) + c + 1)
                tt(h_lo[u][:, c * T:(c + 1) * T], h32[:, c * T:(c + 1) * T], h_hi[u][:, c * T:(c + 1) * T],
                   ALU.subtract).then_inc(lo_done, 1)

            def shared_out(u, t):
                tile = xres[:, ds(t * T, T)]
                v.wait_ge(down_done, t + 1 + RING)
                stt(tile, bank[4 + u][:, :], 1.0 / WSCALE, tile, ALU.mult, ALU.add).then_inc(ffn_out, 1)

            def shared_step(u, t):
                for c in range(FC):
                    shared_low(1 - u, t + 1, c)
                shared_out(u, t)

            def both_step(u, t, more):
                rows_low(bank[6], HT + t)
                if more:
                    rows_out(1, HT + t + 1, t + 1)
                for c in range(FC):
                    shared_low(1 - u, t + 1, c)
                logits_out(bank[7], HT + t, t)
                shared_out(u, t)

            v.wait_ge(pool_pow, BATCH + 5)
            rows_out(1, HT, 0)
            weigh(0)
            bases(0)
            for c in range(FC):
                shared_low(0, 0, c)
            both_step(0, 0, True)
            place(0)
            both_step(1, 1, True)
            with v.Fori(1, HT // 2 - 1) as i:
                for u in range(2):
                    both_step(u, 2 * i + u, True)
            both_step(0, HT - 2, True)
            both_step(1, HT - 1, False)
            choose(1)
            shared_step(0, HT)
            weigh(1)
            shared_step(1, HT + 1)
            take_ranks(1)
            bases(1)
            shared_step(0, HT + 2)
            place(1)
            shared_step(1, HT + 3)
            v.wait_ge(b2p_loaded, 16)
            cut_bias(b2p_raw, b2p_hi, b2p_cut).then_inc(bias_cut, 1)
            with v.Fori(HT // 2 + 2, NT // 2 - 1) as i:
                for u in range(2):
                    shared_step(u, 2 * i + u)
            shared_step(0, NT - 2)

            def keep_tails(u, g, turn):
                v.wait_ge(xr_loaded[u], 16 * turn)
                xv = xr[u].rearrange("p (j n) -> p j n", j=RB)
                nc.vector.tensor_copy(tails[:, ds(g * RB * 2, RB * 2)].rearrange("p (j n) -> p j n", j=RB),
                                      xv[:, :, D:ROW]).then_inc(tails_read, 1)

            def row_low(u, g):
                v.wait_ge(xr_h, g + 1)
                tt(xr_lo[u], bank[6 + u][:, 0:TR], xr_hi[u], ALU.subtract).then_inc(xr_l, 1)

            def routed_dest(u, g, free):
                if free is not None:
                    v.wait_ge(returned[u], free)
                v.wait_ge(tails_read, g + 1)
                tg = tails[:, ds(g * RB * 2, RB * 2)].rearrange("p (j n) -> p j n", j=RB)
                nc.vector.tensor_copy(rdest[u], tg[:, :, 0].bitcast(i32)).then_inc(dest_in, 1)

            def cut_high(u, g, n):
                w = slice(2 * n * TR, (2 * n + 2) * TR)
                if n == 0:
                    v.wait_ge(down_done, NT + g + 1)
                v.wait_ge(gelu_done, NSH + FC * (g + 1) + 2 * n + 2)
                nc.vector.tensor_copy(h_hi[u][:, w], h32[:, w]).then_inc(hi_r, 1)

            def cut_low(u, g, n):
                w = slice(2 * n * TR, (2 * n + 2) * TR)
                v.wait_ge(hi_r, 2 * g + n + 1)
                tt(h_lo[u][:, w], h32[:, w], h_hi[u][:, w], ALU.subtract).then_inc(lo_done, 2)

            def routed_cut(u, g):
                for n in range(2):
                    cut_high(u, g, n)
                    cut_low(u, g, n)

            def routed_step(u, g, free, turn):
                row_low(u, g + 2)
                cut_high(1 - u, g + 1, 0)
                keep_tails(u, g + 2, turn)
                cut_low(1 - u, g + 1, 0)
                cut_high(1 - u, g + 1, 1)
                routed_dest(u, g, free)
                cut_low(1 - u, g + 1, 1)

            def combine(u, n, turn, whole):
                v.wait_ge(y_loaded[u], 32 * turn)
                acc = xres[:, ds(n * GB * D, GB * D)]
                if whole:
                    tt(acc, acc, yload[u][0], ALU.add).then_inc(y_used, 1)
                v.wait_ge(y_used, n + 1)
                tt(acc, acc, yload[u][1], ALU.add).then_inc(combined, 1)

            for g in range(2):
                keep_tails(g, g, 1)
                row_low(g, g)
            shared_out(1, NT - 1)
            routed_cut(0, 0)
            for g in range(2):
                routed_step(g, g, None, 2)

            def tiles_pair(i):
                for u in range(2):
                    routed_step(u, 2 * i + u, 16 * RB * i, i + 2)
            with v.Fori(1, SUM0) as i:
                tiles_pair(i)
            with v.Fori(0, GH // YR) as m:
                for w in range(YR):
                    with v.Fori(0, STEP) as k:
                        tiles_pair(SUM0 + (YR * m + w) * STEP + k)
                    combine(w, YR * m + w, m + 1, False)
            with v.Fori(SUM0 + GH * STEP, NR // 2 - 1) as i:
                tiles_pair(i)
            routed_cut(1, NR - 1)
            routed_dest(0, NR - 2, 16 * RB * (NR // 2 - 1))
            routed_dest(1, NR - 1, 16 * RB * (NR // 2 - 1))

            with v.Fori(GH // YR, 2 * GH // YR) as m:
                for w in range(YR):
                    combine(w, YR * m + w, m + 1, True)

        @block.tensor
        def _(pe):
            mm, transpose = nc.tensor.matmul, nc.tensor.transpose
            for ring in (c_mm, y_t, lg_done, down_done):
                pe.sem_inc(ring, RING)

            def three_pass(o, l, r, start, stop, last_inc=None):
                (lh, ll), (rh, rl) = l, r
                mm(o, lh, rh, start=start, stop=False)
                mm(o, lh, rl, start=False, stop=False)
                return mm(o, ll, rh, start=False, stop=stop)

            pe.wait_ge(small_loaded, 16 * 10)
            pe.wait_ge(pool_made, 5)
            transpose(bank[7][:, 0:NVEC], vrows[0:NVEC, :], ident[0:NVEC, 0:NVEC])
            for g in range(HG):
                transpose(bank[6][:, g * P:(g + 1) * P], gw1[:, g * D:(g + 1) * D], ident[:, :])
                ins = transpose(bank[6][:, H + g * P:H + (g + 1) * P], gw2[:, g * P:(g + 1) * P], ident[:, :])
            ins.then_inc(prep_t, 1)

            for c in range(CH):
                pe.wait_ge(adj_eye, c + 1)
                if c >= 2:
                    pe.wait_ge(at_lo_done, 2 * c - 2)
                for h in range(2):
                    for m in range(4):
                        k = 4 * h + m
                        ins = transpose(bank[2 * (c % 2) + h][:, m * P:(m + 1) * P],
                                        adjn[:, c * NODES + k * P:c * NODES + (k + 1) * P], ident[:, :])
                    ins.then_inc(at_t, 1)
                for h in range(2):
                    ins = mm(bank[4 + h][:, :], onesf[:, :], adjn[:, c * NODES + h * T:c * NODES + (h + 1) * T],
                             start=(c == 0), stop=(c == CH - 1))
            ins.then_inc(colsum_done, 1)

            def aggregate(u, b, t, free):
                pe.wait_ge(xn_l, b + 1)
                if free is not None:
                    pe.wait_ge(agg_f, free)
                for m in range(CH):
                    l = (xn_hi[:, ds((b * CH + m) * D, D)], xn_lo[:, ds((b * CH + m) * D, D)])
                    w = slice(m * NODES + u * T, m * NODES + (u + 1) * T)
                    ins = three_pass(bank[u][:, :], l, (at_hi[:, w], at_lo[:, w]), m == 0, m == CH - 1)
                ins.then_inc(agg_done, 1)

            def first_product(u, t, free):
                pe.wait_ge(agg_l, t + 1)
                if free is not None:
                    pe.wait_ge(up1_out, free)
                for g in range(HG):
                    w = slice(g * P, (g + 1) * P)
                    three_pass(bank[2 + 2 * u + g][:, :], (w1t_hi[:, w], w1t_lo[:, w]), (agg_hi[u], agg_lo[u]),
                               True, True).then_inc(up1_done, 1)
            pe.wait_ge(at_lo_done, 2 * CH)
            aggregate(0, 0, 0, None)
            pe.wait_ge(diagd_done, 1)
            pe.wait_ge(prep_ready, 1)
            for h in range(2):
                ins = mm(bank[6 + h][:, :], onesf[:, :], diagd[:, h * T:(h + 1) * T], start=True, stop=True)
            ins.then_inc(dinv_in_psum, 1)
            aggregate(1, 0, 1, None)
            first_product(0, 0, None)
            aggregate(0, 1, 2, 1)
            first_product(1, 1, None)
            with pe.Fori(1, BATCH - 1) as b:
                aggregate(1, b, 2 * b + 1, 2 * b)
                first_product(0, 2 * b, 4 * b - 2)
                aggregate(0, b + 1, 2 * b + 2, 2 * b + 1)
                first_product(1, 2 * b + 1, 4 * b)
            aggregate(1, BATCH - 1, NT - 1, NT - 2)
            first_product(0, NT - 2, 2 * NT - 6)
            first_product(1, NT - 1, 2 * NT - 4)

            with pe.Fori(0, NT // 2) as i:
                for u in range(2):
                    t = 2 * i + u
                    pe.wait_ge(c_lo, t + 1 + RING)
                    pe.wait_ge(c_lo2, t + 1 + RING)
                    pe.wait_ge(c_out, t + 1)
                    for g in range(HG):
                        w = slice(g * P, (g + 1) * P)
                        r = (hr_hi[u][:, g * T:(g + 1) * T], hr_lo[u][:, g * T:(g + 1) * T])
                        ins = three_pass(bank[u][:, :], (w2t_hi[:, w], w2t_lo[:, w]), r, g == 0, g == HG - 1)
                    ins.then_inc(c_mm, 1)

            with pe.Fori(0, NT // 2) as i:
                for u in range(2):
                    t = 2 * i + u
                    pe.wait_ge(y_done, t + 1)
                    pe.wait_ge(x2_done, t + 1)
                    for j in range(BT):
                        ins = transpose(bank[u][:, j * P:(j + 1) * P], ybuf[u][:, j * P:(j + 1) * P], ident[:, :])
                    ins.then_inc(y_t, 1)

            pe.wait_ge(wr_cut, 1)

            def rows_t(s, b_, tl, free):
                t = s * HT + tl
                pe.wait_ge(row_done, t + 1)
                pe.wait_ge(xt_l, free)
                for j in range(BT):
                    ins = transpose(b_[:, j * P:(j + 1) * P], pay[s][:, (tl * BT + j) * ROW:(tl * BT + j) * ROW + D], ident[:, :])
                ins.then_inc(row_t, 1)

            def logits(b_, t, free):
                pe.wait_ge(xt_l, t + 1 + RING)
                pe.wait_ge(lg_out, free)
                for j in range(BT):
                    w = slice(t * T + j * P, t * T + (j + 1) * P)
                    ins = three_pass(b_[:, j * E:(j + 1) * E], (xt_hi[:, w], xt_lo[:, w]),
                                     (wr_hi[:, :], wr_lo[:, :]), True, True)
                ins.then_inc(lg_done, 1)

            def ranks(s):
                pe.wait_ge(oh_ready, s + 1)
                oh16 = rt[6].bitcast(f16)[:, 0:HB * E]
                mm(bank[6][:, 0:HB * E], before16[:, :], oh16, start=True, stop=True)
                mm(bank[7][:, 0:HB * E], ones16[:, :], oh16, start=True, stop=True).then_inc(rank_done, 1)

            rows_t(0, bank[2], 0, 1)
            rows_t(0, bank[3], 1, 2)
            for t in range(HT):
                if 0 < t < HT - 1:
                    rows_t(0, bank[2 + (t + 1) % 2], t + 1, t + 2)
                logits(bank[4 + t % 2], t, t + 1)
            ranks(0)

            pe.wait_ge(wall_loaded, 16)
            SW = E * 2048

            def shared_up(t):
                for c in range(FC):
                    pe.wait_ge(gelu_done, FC * t + c + 1)
                    a, b_ = SW + W1S + c * P, SW + W1L + c * P
                    three_pass(bank[c][:, :], (wall[:, a:a + P], wall[:, b_:b_ + P]),
                               (xt_hi[:, ds(t * T, T)], xt_lo[:, ds(t * T, T)]), True, True).then_inc(up_done, 1)

            def shared_down(u, t):
                pe.wait_ge(lo_done, FC * (t + 2))
                pe.wait_ge(ffn_out, t + 1)
                for j in range(BT):
                    mm(bank[4 + u][:, j * D:(j + 1) * D], ones16[0:2, :], b2s_cut, start=True, stop=False)
                    for c in range(FC):
                        l = tuple(h[:, c * T + j * P:c * T + (j + 1) * P] for h in (h_hi[u], h_lo[u]))
                        a, b_ = SW + W2S + c * D, SW + W2L + c * D
                        ins = three_pass(bank[4 + u][:, j * D:(j + 1) * D], l, (wall[:, a:a + D], wall[:, b_:b_ + D]),
                                         False, c == FC - 1)
                ins.then_inc(down_done, 1)

            pe.wait_ge(x2_done, NT + RING)
            pe.wait_ge(xt_l, HT + RING)
            pe.wait_ge(lg_out, HT + RING)
            shared_up(0)
            pe.wait_ge(ranks_out, 1)
            rows_t(1, bank[6], 0, 1)
            for t in range(HT):
                shared_up(t + 1)
                logits(bank[7], HT + t, HT + t + RING)
                shared_down(t % 2, t)
                if t + 1 < HT:
                    rows_t(1, bank[6], t + 1, HT + t + 1 + RING)
            shared_up(HT + 1)
            shared_down(0, HT)
            pe.wait_ge(lg_out, NT + RING)
            ranks(1)
            shared_up(HT + 2)
            shared_down(1, HT + 1)
            with pe.Fori(HT // 2 + 1, NT // 2 - 1) as i:
                for u in range(2):
                    shared_up(2 * i + u + 1)
                    shared_down(u, 2 * i + u)
            shared_up(NT - 1)

            def routed_t(u, g, turn):
                pe.wait_ge(xr_loaded[u], 16 * turn)
                pe.wait_ge(xr_l, g + 1)
                for j in range(RB):
                    ins = transpose(bank[6 + u][:, j * P:(j + 1) * P], xr[u][:, j * ROW:j * ROW + D], ident[:, :])
                ins.then_inc(xr_t, 1)


            def up_part(u, g, e, c):
                l = (wall[:, ds(e * 2048 + W1S + c * P, P)], wall[:, ds(e * 2048 + W1L + c * P, P)])
                three_pass(bank[c][:, 0:TR], l, (xr_hi[u], xr_lo[u]), True, True).then_inc(up_done, 1)

            def down_part(u, e, j, c):
                if c == 0:
                    mm(bank[4 + u][:, j * D:(j + 1) * D], ones16[0:2, :], b2p_cut[:, ds(e * D, D)], start=True, stop=False)
                l = tuple(h[:, c * TR + j * P:c * TR + (j + 1) * P] for h in (h_hi[u], h_lo[u]))
                r = (wall[:, ds(e * 2048 + W2S + c * D, D)], wall[:, ds(e * 2048 + W2L + c * D, D)])
                return three_pass(bank[4 + u][:, j * D:(j + 1) * D], l, r, False, c == FC - 1)

            def routed_up(u, g, number):
                e = experts.of(number)
                pe.wait_ge(gelu_done, NSH + FC * (g + 1))
                pe.wait_ge(xr_l, g + 1 + RING)
                for c in range(FC):
                    up_part(u, g, e, c)

            def routed_down(u, g, number):
                e = experts.of(number)
                pe.wait_ge(lo_done, NSH + FC * (g + 2))
                pe.wait_ge(y_out, g + 1)
                for j in range(RB):
                    for c in range(FC):
                        ins = down_part(u, e, j, c)
                ins.then_inc(down_done, 1)

            def routed_both(u, g, number):
                e_up, e_down = experts.of(number + 1), experts.of(number)
                pe.wait_ge(gelu_done, NSH + FC * (g + 2))
                pe.wait_ge(xr_l, g + 2 + RING)
                for c in range(FC):
                    up_part(1 - u, g + 1, e_up, c)
                pe.wait_ge(lo_done, NSH + FC * (g + 2))
                for j in range(RB):
                    for c in range(FC):
                        ins = down_part(u, e_down, j, c)
                ins.then_inc(down_done, 1)

            pe.wait_ge(bias_cut, 1)
            experts = Experts(pe, tile_e)
            routed_t(0, 0, 1)
            routed_t(1, 1, 1)
            shared_down(0, NT - 2)
            experts.fetch_first()
            routed_up(0, 0, 0)
            shared_down(1, NT - 1)
            pe.wait_ge(ffn_out, NT + RING)
            with pe.Fori(0, NR // 2 - 1) as i:
                for u in range(2):
                    routed_t(u, 2 * i + u + 2, i + 2)
                    if u == 1:
                        experts.fetch(2 * i + 3)
                    routed_both(u, 2 * i + u, u)
                experts.shift()
            routed_up(1, NR - 1, 1)
            routed_down(0, NR - 2, 0)
            routed_down(1, NR - 1, 1)


INS = ["x", "adj"] + [f"L0_gnn_{n}" for n in ("W1", "b1", "g1", "be1", "W2", "b2", "g2", "be2")] + \
      [f"L0_ffn_{n}" for n in ("Wr", "W1s", "b1s", "W2s", "b2s", "W1p", "b1p", "W2p", "b2p")]


def kernel(**inputs):
    import numpy as np
    import concourse.bacc as bacc
    from concourse import mybir as _mybir
    from concourse.bass_utils import run_bass_kernel_spmd

    nc = bacc.Bacc("TRN2", target_bir_lowering=False, num_devices=1)
    arrays, args = {}, []
    for name in INS:
        a = np.ascontiguousarray(inputs[name])
        arrays[f"in_{name}"] = a
        args.append(nc.dram_tensor(f"in_{name}", a.shape, _mybir.dt.from_np(a.dtype), kind="ExternalInput").ap())
    out = nc.dram_tensor("result", (TOK, D), _mybir.dt.float32, kind="ExternalOutput").ap()
    build(nc, *args, out)
    r = run_bass_kernel_spmd(nc, [arrays], core_ids=[0])
    return r.results[0]["result"].reshape(BATCH, NODES, D)
```
